# Optimizing a Trainium2 kernel written in Bass

```python
import numpy as np
import jax
import jax.numpy as jnp

def _softmax(x, axis=-1):
    return jax.nn.softmax(x, axis=axis)

def _gelu(x):
    return jax.nn.gelu(x, approximate=True)

def _silu(x):
    return jax.nn.silu(x)

def _sigmoid(x):
    return jax.nn.sigmoid(x)

def _layernorm(x, axis=-1, eps=1e-05):
    m = jnp.mean(x, axis=axis, keepdims=True)
    v = jnp.var(x, axis=axis, keepdims=True)
    return (x - m) / jnp.sqrt(v + eps)

def _scatter_add(tgt, idx, src, axis=0):
    return tgt.at[idx].add(src)

def _segment_sum(src, seg, n):
    return jax.ops.segment_sum(src, seg, n)
kernel_name = 'mk_flamingo_gated_d1_seqx_r4_59f8c8'

def setup_inputs(seed: int=0):
    np.random.seed(seed)
    _w = jnp.asarray

    def _rec_inputs():
        import jax
        import jax.numpy as jnp
        _rk = jax.random.key(seed)
        x = 7.22e-05 + 1 * jax.random.normal(jax.random.fold_in(_rk, 1), (16, 112, 512), jnp.float32)
        _lenS = 112 - jax.random.randint(jax.random.fold_in(_rk, 7), (16,), 0, max(1, 112 // 4) + 1, jnp.int32)
        _lenS2 = 375 - jax.random.randint(jax.random.fold_in(_rk, 8), (16,), 0, max(1, 375 // 4) + 1, jnp.int32)
        _ctx_1024P = jax.random.normal(jax.random.fold_in(_rk, 11), (16, 16, 256), jnp.float32)
        _ctx_1024c = jax.random.dirichlet(jax.random.fold_in(_rk, 511), 0.3 * jnp.ones((16,), jnp.float32), (16, 375))
        _ctx_1024t = jnp.einsum('bsk,bkd->bsd', _ctx_1024c, _ctx_1024P)
        _ctx_1024t = _ctx_1024t * jax.lax.rsqrt(jnp.mean(jnp.square(_ctx_1024t)) + 1e-12) * 0.953939
        ctx_1024 = -0.000673644 + 1.00013 * (_ctx_1024t + 0.3 * jax.random.normal(jax.random.fold_in(_rk, 611), (16, 375, 256), jnp.float32))
        _g = jax.random.normal(jax.random.fold_in(_rk, 9001), (2, 1), jnp.float32)
        _g = jnp.sign(_g) * jnp.maximum(jnp.abs(_g), 1.0) + (_g == 0) * 1.0
        g_xattn = _g[0]
        g_ffn = _g[1]
        return (x, ctx_1024, g_xattn, g_ffn)
    x, ctx_1024, g_xattn, g_ffn = _rec_inputs()

    def _L0_xattn_setup():
        import jax, jax.numpy as jnp
        import numpy as np
        B, S1, S2, DCA = (2, 512, 256, 16)
        QDIM, KDIM, H = (512, 256, 16)
        HD = QDIM // H
        SCALE = HD ** (-0.5)
        EPS = 1e-06
        DCA_WEIGHT = 1.0

        def _ln(t, w, b):
            m = jnp.mean(t, axis=-1, keepdims=True)
            v = jnp.var(t, axis=-1, keepdims=True)
            return (t - m) * jax.lax.rsqrt(v + EPS) * w + b

        def _attn(q, k, v):
            s = jnp.einsum('bhqd,bhkd->bhqk', q, k) * SCALE
            p = jax.nn.softmax(s, axis=-1)
            return jnp.einsum('bhqk,bhkd->bhqd', p, v)
        key = jax.random.key(seed)
        ks = jax.random.split(key, 8)
        w = lambda k, shape: jax.random.normal(k, shape, jnp.float32) * 0.02
        return {'x': jax.random.normal(ks[0], (B, S1, QDIM), jnp.float32), 'y': jax.random.normal(ks[1], (B, S2 + DCA, KDIM), jnp.float32), 'Wq': w(ks[2], (QDIM, QDIM)), 'bq': jnp.zeros((QDIM,), jnp.float32), 'Wk': w(ks[3], (KDIM, QDIM)), 'bk': jnp.zeros((QDIM,), jnp.float32), 'Wv': w(ks[4], (KDIM, QDIM)), 'bv': jnp.zeros((QDIM,), jnp.float32), 'Wkv_dca': w(ks[5], (KDIM, 2 * QDIM)), 'bkv_dca': jnp.zeros((2 * QDIM,), jnp.float32), 'qn_w': jnp.ones((HD,), jnp.float32), 'qn_b': jnp.zeros((HD,), jnp.float32), 'kn_w': jnp.ones((HD,), jnp.float32), 'kn_b': jnp.zeros((HD,), jnp.float32), 'kn_dca_w': jnp.ones((HD,), jnp.float32), 'kn_dca_b': jnp.zeros((HD,), jnp.float32), 'Wo': w(ks[6], (QDIM, QDIM)), 'bo': jnp.zeros((QDIM,), jnp.float32)}
    _L0_xattn_all = _L0_xattn_setup()
    _L0_xattn_in = {k: v for k, v in _L0_xattn_all.items() if k in ('Wq', 'bq', 'Wk', 'bk', 'Wv', 'bv', 'Wkv_dca', 'bkv_dca', 'qn_w', 'qn_b', 'kn_w', 'kn_b', 'kn_dca_w', 'kn_dca_b', 'Wo', 'bo')}
    del _L0_xattn_all

    def _L0_ffn_setup():
        import jax, jax.numpy as jnp
        import numpy as np
        H = 512
        key = jax.random.key(seed)
        ks = jax.random.split(key, 10)
        s = 1.0 / np.sqrt(H)
        x = jax.random.normal(ks[0], (4, 512, H), dtype=jnp.float32)
        Wg = jax.random.uniform(ks[1], (2, H), jnp.float32, -s, s)
        W0a = jax.random.uniform(ks[2], (2 * H, H), jnp.float32, -s, s)
        b0a = jax.random.uniform(ks[3], (2 * H,), jnp.float32, -s, s)
        W0b = jax.random.uniform(ks[4], (H, 2 * H), jnp.float32, -s, s)
        b0b = jax.random.uniform(ks[5], (H,), jnp.float32, -s, s)
        W1a = jax.random.uniform(ks[6], (2 * H, H), jnp.float32, -s, s)
        b1a = jax.random.uniform(ks[7], (2 * H,), jnp.float32, -s, s)
        W1b = jax.random.uniform(ks[8], (H, 2 * H), jnp.float32, -s, s)
        b1b = jax.random.uniform(ks[9], (H,), jnp.float32, -s, s)
        return {'x': x, 'Wg': Wg, 'W0a': W0a, 'b0a': b0a, 'W0b': W0b, 'b0b': b0b, 'W1a': W1a, 'b1a': b1a, 'W1b': W1b, 'b1b': b1b}
    _L0_ffn_all = _L0_ffn_setup()
    _L0_ffn_in = {k: v for k, v in _L0_ffn_all.items() if k in ('Wg', 'W0a', 'b0a', 'W0b', 'b0b', 'W1a', 'b1a', 'W1b', 'b1b')}
    del _L0_ffn_all
    return {'x': x, 'ctx_1024': ctx_1024, 'g_xattn': g_xattn, 'g_ffn': g_ffn, 'L0_xattn_Wq': _L0_xattn_in['Wq'], 'L0_xattn_bq': _L0_xattn_in['bq'], 'L0_xattn_Wk': _L0_xattn_in['Wk'], 'L0_xattn_bk': _L0_xattn_in['bk'], 'L0_xattn_Wv': _L0_xattn_in['Wv'], 'L0_xattn_bv': _L0_xattn_in['bv'], 'L0_xattn_Wkv_dca': _L0_xattn_in['Wkv_dca'], 'L0_xattn_bkv_dca': _L0_xattn_in['bkv_dca'], 'L0_xattn_qn_w': _L0_xattn_in['qn_w'], 'L0_xattn_qn_b': _L0_xattn_in['qn_b'], 'L0_xattn_kn_w': _L0_xattn_in['kn_w'], 'L0_xattn_kn_b': _L0_xattn_in['kn_b'], 'L0_xattn_kn_dca_w': _L0_xattn_in['kn_dca_w'], 'L0_xattn_kn_dca_b': _L0_xattn_in['kn_dca_b'], 'L0_xattn_Wo': _L0_xattn_in['Wo'], 'L0_xattn_bo': _L0_xattn_in['bo'], 'L0_ffn_Wg': _L0_ffn_in['Wg'], 'L0_ffn_W0a': _L0_ffn_in['W0a'], 'L0_ffn_b0a': _L0_ffn_in['b0a'], 'L0_ffn_W0b': _L0_ffn_in['W0b'], 'L0_ffn_b0b': _L0_ffn_in['b0b'], 'L0_ffn_W1a': _L0_ffn_in['W1a'], 'L0_ffn_b1a': _L0_ffn_in['b1a'], 'L0_ffn_W1b': _L0_ffn_in['W1b'], 'L0_ffn_b1b': _L0_ffn_in['b1b']}

def reference(x, ctx_1024, g_xattn, g_ffn, L0_xattn_Wq, L0_xattn_bq, L0_xattn_Wk, L0_xattn_bk, L0_xattn_Wv, L0_xattn_bv, L0_xattn_Wkv_dca, L0_xattn_bkv_dca, L0_xattn_qn_w, L0_xattn_qn_b, L0_xattn_kn_w, L0_xattn_kn_b, L0_xattn_kn_dca_w, L0_xattn_kn_dca_b, L0_xattn_Wo, L0_xattn_bo, L0_ffn_Wg, L0_ffn_W0a, L0_ffn_b0a, L0_ffn_W0b, L0_ffn_b0b, L0_ffn_W1a, L0_ffn_b1a, L0_ffn_W1b, L0_ffn_b1b):
    import jax
    import jax.numpy as jnp

    def _L0_xattn_ref(x, y, Wq, bq, Wk, bk, Wv, bv, Wkv_dca, bkv_dca, qn_w, qn_b, kn_w, kn_b, kn_dca_w, kn_dca_b, Wo, bo):
        import jax, jax.numpy as jnp
        import numpy as np
        B, S1, S2, DCA = (2, 512, 256, 16)
        QDIM, KDIM, H = (512, 256, 16)
        HD = QDIM // H
        SCALE = HD ** (-0.5)
        EPS = 1e-06
        DCA_WEIGHT = 1.0

        def _ln(t, w, b):
            m = jnp.mean(t, axis=-1, keepdims=True)
            v = jnp.var(t, axis=-1, keepdims=True)
            return (t - m) * jax.lax.rsqrt(v + EPS) * w + b

        def _attn(q, k, v):
            s = jnp.einsum('bhqd,bhkd->bhqk', q, k) * SCALE
            p = jax.nn.softmax(s, axis=-1)
            return jnp.einsum('bhqk,bhkd->bhqd', p, v)
        b, s1, _ = x.shape
        y_dca = y[:, -DCA:, :]
        y_main = y[:, :-DCA, :]
        kv_dca = (y_dca @ Wkv_dca + bkv_dca).reshape(b, DCA, 2, H, HD)
        k_dca = _ln(kv_dca[:, :, 0], kn_dca_w, kn_dca_b)
        v_dca = kv_dca[:, :, 1]
        s2 = y_main.shape[1]
        q = _ln((x @ Wq + bq).reshape(b, s1, H, HD), qn_w, qn_b)
        kv = jnp.concatenate([y_main @ Wk + bk, y_main @ Wv + bv], axis=-1)
        kv = kv.reshape(b, s2, H, 2 * HD)
        k = _ln(kv[..., :HD], kn_w, kn_b)
        v = kv[..., HD:]
        qT = q.transpose(0, 2, 1, 3)
        ctx = _attn(qT, k.transpose(0, 2, 1, 3), v.transpose(0, 2, 1, 3))
        ctx = ctx.transpose(0, 2, 1, 3).reshape(b, s1, QDIM)
        ctx_dca = _attn(qT, k_dca.transpose(0, 2, 1, 3), v_dca.transpose(0, 2, 1, 3))
        ctx_dca = ctx_dca.transpose(0, 2, 1, 3).reshape(b, s1, QDIM)
        ctx = ctx + DCA_WEIGHT * ctx_dca
        return ctx @ Wo + bo

    def _L0_ffn_ref(x, Wg, W0a, b0a, W0b, b0b, W1a, b1a, W1b, b1b):
        import jax, jax.numpy as jnp
        import numpy as np
        H = 512
        scores = jax.nn.softmax(jnp.einsum('bsh,eh->bse', x, Wg), axis=-1)
        top_expert = jnp.argmax(scores, axis=-1)
        h0 = jax.nn.gelu(jnp.einsum('bsh,fh->bsf', x, W0a) + b0a, approximate=False)
        out0 = jnp.einsum('bsf,hf->bsh', h0, W0b) + b0b
        h1 = jax.nn.relu(jnp.einsum('bsh,fh->bsf', x, W1a) + b1a)
        out1 = jnp.einsum('bsf,hf->bsh', h1, W1b) + b1b
        mask0 = (top_expert == 0).astype(x.dtype)[..., None]
        return out0 * mask0 + out1 * (1.0 - mask0)
    x = x + jnp.tanh(g_xattn[0]) * _L0_xattn_ref(_layernorm(x, axis=-1), ctx_1024, L0_xattn_Wq, L0_xattn_bq, L0_xattn_Wk, L0_xattn_bk, L0_xattn_Wv, L0_xattn_bv, L0_xattn_Wkv_dca, L0_xattn_bkv_dca, L0_xattn_qn_w, L0_xattn_qn_b, L0_xattn_kn_w, L0_xattn_kn_b, L0_xattn_kn_dca_w, L0_xattn_kn_dca_b, L0_xattn_Wo, L0_xattn_bo)
    x = x + jnp.tanh(g_ffn[0]) * _L0_ffn_ref(_layernorm(x, axis=-1), L0_ffn_Wg, L0_ffn_W0a, L0_ffn_b0a, L0_ffn_W0b, L0_ffn_b0b, L0_ffn_W1a, L0_ffn_b1a, L0_ffn_W1b, L0_ffn_b1b)
    return x

_drawn_inputs = setup_inputs


def setup_inputs(seed=0):
    import zlib

    import numpy as np

    out = dict(_drawn_inputs(seed))
    spreads = {'L0_xattn_bq': (0.0, 0.361),
     'L0_xattn_bk': (0.0, 0.1),
     'L0_xattn_bv': (0.0, 0.327),
     'L0_xattn_bkv_dca': (0.0, 0.1),
     'L0_xattn_qn_w': (1.0, 0.6),
     'L0_xattn_qn_b': (0.0, 1.147),
     'L0_xattn_kn_w': (1.0, 0.6),
     'L0_xattn_kn_b': (0.0, 2.0),
     'L0_xattn_kn_dca_w': (1.0, 0.6),
     'L0_xattn_kn_dca_b': (0.0, 2.0),
     'L0_xattn_bo': (0.0, 0.1)}
    factors = {'L0_ffn_b0a': 7.7, 'L0_ffn_b0b': 3.578, 'L0_ffn_b1a': 5.963, 'L0_ffn_b1b': 3.379}
    for name, (base, spread) in spreads.items():
        noise = np.random.default_rng([zlib.crc32(name.encode()), seed]).standard_normal(out[name].shape)
        drawn = base * np.exp(spread * noise) if base else spread * noise
        out[name] = jnp.asarray(drawn.astype(out[name].dtype))
    for name, factor in factors.items():
        out[name] = (out[name] * factor).astype(out[name].dtype)
    return out
```

```python
from contextlib import ExitStack

import concourse.bass as bass
from concourse import mybir

F32 = mybir.dt.float32
F32R = mybir.dt.float32r
F16 = mybir.dt.float16
ALU = mybir.AluOpType
ACT = mybir.ActivationFunctionType
AX = mybir.AxisListType

P = 128
B, T, C = 16, 112, 512
S, CK, DCA = 375, 256, 16
H, HD = 16, 32
M = S - DCA
SCALE = HD ** -0.5
EPS_HEAD, EPS_ROW = 1e-6, 1e-5
F = 1024
KC, KK, KF = C // P, CK // P, F // P
ROWS = [P, P, M - 2 * P]
KEYS = [P, P, S - 2 * P]
G = 4
NG = H // G
UNIT = 64.0
VW = 66

USES = ["mt0", "ct3", "xT", "K0", "V0", "cT", "Wo",
        "mt1", "ct0", "Q", "K1", "V1",
        "mt2", "ct1", "kt00", "kt01", "qt0", "qt1", "K2", "V2",
        "mt3", "ct2", "kt10", "kt11", "kt20", "kt21"]
OF_C = {"mt0", "mt1", "mt2", "mt3", "ct0", "ct1", "ct2"}
OF_D = {"ct3", "cT", "Wo"}
BANKS = 3
VECTOR_OWN, SCALAR_OWN, POOL_OWN = 86, 10, 8
CHAIN = ["K0", "Q", "K1", "K2"]


class Step:

    def __init__(self, b, parity, a, c, d, base, pre=True):
        self.b, self.parity, self.a, self.c, self.d, self.base = b, parity, a, c, d, base
        self.pre = a and pre
        self.uses = [u for u in USES if (c if u in OF_C else d if u in OF_D else a)]

    @staticmethod
    def bank(use):
        return USES.index(use) % BANKS

    def before(self, use):
        bank = self.bank(use)
        return self.base[bank] + sum(self.bank(u) == bank for u in self.uses[:self.uses.index(use)])

    def after(self):
        return [self.base[k] + sum(self.bank(u) == k for u in self.uses) for k in range(BANKS)]


def at_least(eng, sem, value):
    if not (isinstance(value, int) and value <= 0):
        eng.wait_ge(sem, value)


PAIRS = (B - 4) // 2


def run_steps(eng, body, chain=None):
    st = Step(-1, 1, True, False, False, [0] * BANKS)
    body(st)
    st = Step(0, 0, True, True, False, st.after())
    body(st)
    per = [sum(Step.bank(u) == k for u in USES) for k in range(BANKS)]
    start = st.after()
    with eng.Fori(0, PAIRS) as i:
        if chain:
            chain.enter(i)
        for second in (0, 1):
            base = [i * (2 * per[k]) + (start[k] + second * per[k]) for k in range(BANKS)]
            body(Step(i * 2 + (1 + second), 1 - second, True, True, True, base))
        if chain:
            chain.leave(PAIRS)
    st = Step(B - 3, 1, True, True, True, [start[k] + 2 * PAIRS * per[k] for k in range(BANKS)])
    body(st)
    st = Step(B - 2, 0, True, True, True, st.after(), pre=False)
    body(st)
    st = Step(B - 1, 1, False, True, True, st.after())
    body(st)
    body(Step(B, 0, False, False, True, st.after()))


class Chain:

    def __init__(self, eng, sem, per_turn=0):
        self.eng, self.sem, self.n, self.base, self.per_turn = eng, sem, 0, 0, per_turn

    def enter(self, i):
        self.before, self.n, self.base = self.n, 0, i * self.per_turn + self.n

    def leave(self, turns):
        assert self.n == self.per_turn, f"{self.n} own results a turn"
        self.n, self.base = self.before + turns * self.per_turn, 0

    def link(self, ins):
        ins.then_inc(self.sem, 1)
        self.n += 1
        self.eng.wait_ge(self.sem, self.base + self.n)


def one(n, size):
    return slice(n * size, (n + 1) * size) if isinstance(n, int) else bass.ds(n * size, size)


def transfers(n, par, more):
    return n * 8 + (16 * more - 8 * par)


def heads(ap):
    return ap.rearrange("p (h d) -> p h d", d=HD)


def build(nc, a, out):
    x1_dram = nc.dram_tensor("x1_scratch", (B * T, C + 2), F32, kind="Internal").ap()
    vd_dram = nc.dram_tensor("vd_scratch", (B * DCA, H * VW), F32, kind="Internal").ap()

    with ExitStack() as whole:
        def sem(name):
            return whole.enter_context(nc.semaphore(name))

        def sbuf(name, shape, dt=F32):
            return whole.enter_context(nc.sbuf_tensor(name, shape, dt))

        gates = sbuf("gates", [P, 2])
        identf = sbuf("identf", [P, P])
        identh = sbuf("identh", [P, P], F16)

        with ExitStack() as attention:
            def asb(name, shape, dt=F32):
                return attention.enter_context(nc.sbuf_tensor(name, shape, dt))

            w = {n: [asb(f"{n}_{part}", [P, k, C], F32R) for part in ("hi", "lo")]
                 for n, k in (("wq", KC), ("wk", KK), ("wv", KK), ("wo", KC))}
            rows = {n: asb(f"row_{n}", [P, C]) for n in ("bq", "bk", "bv", "bo")}
            norms = {n: asb(f"row_{n}", [P, HD]) for n in ("qn_w", "qn_b", "kn_w", "kn_b")}
            kdT = asb("kdT", [P, H, B * DCA], F16)
            prepare(nc, a, w, rows, norms, kdT, vd_dram, gates, identf, identh)
            attend(nc, a, w, rows, norms, kdT, vd_dram, gates, identf, identh, x1_dram)

        experts(nc, a, gates, identf, x1_dram, out)


def prepare(nc, a, w, rows, norms, kdT, vd_dram, gates, identf, identh):
    with ExitStack() as ctx:
        def sb(name, shape, dt=F32):
            return ctx.enter_context(nc.sbuf_tensor(name, shape, dt))

        def sem(name):
            return ctx.enter_context(nc.semaphore(name))

        def bank(name):
            return ctx.enter_context(nc.psum_tensor(name, [P, 512], F32))

        ND = B * DCA // P
        raw = {n: sb(f"raw_{n}", [P, k, C]) for n, k in
               (("wq", KC), ("wk", KK), ("wkd", KK), ("wv", KK), ("wvd", KK), ("wo", KC))}
        bkd, bvd = sb("bkd", [P, C]), sb("bvd", [P, C])
        vd = sb("vd", [P, ND, H, VW])
        kd_w, kd_b = sb("kd_w", [P, HD]), sb("kd_b", [P, HD])
        wd = {n: [sb(f"{n}_{part}", [P, KK, C], F32R) for part in ("hi", "lo")] for n in ("wkd", "wvd")}
        yd = sb("yd", [P, KK, B, DCA])
        yd_hi, yd_lo = sb("yd_hi", [P, KK, B * DCA], F32R), sb("yd_lo", [P, KK, B * DCA], F32R)
        mean = sb("mean", [P, KC * H])
        kb, sq, kn = sb("kb", [P, C]), sb("sq", [P, C]), sb("kn", [P, C])
        ve, lnv, y, r = (sb(n, [P, H]) for n in ("ve", "lnv", "y", "r"))
        stack = sb("stack", [P, H, P], F16)
        gate_raw = sb("gate_raw", [P, 2])
        pk, pv = bank("pk"), bank("pv")
        pt = [ctx.enter_context(nc.psum_tensor(f"pt{j}", [P, 8, P], F16)) for j in range(2)]

        loaded = {n: sem(f"loaded_{n}") for n in
                  ("wkd", "yd", "bkd", "wvd", "wk", "wq", "wv", "wo", "kd", "rows", "gates")}
        idents, tanhs = sem("idents_ready"), sem("tanhs_ready")
        own, own_act = sem("vector_own"), sem("scalar_own")
        hi_ready, lo_ready = sem("prep_hi_ready"), sem("prep_lo_ready")
        centered = sem("prep_centered")
        kd_ready, vd_ready, kd_used, vd_used = (sem(n) for n in ("kd_ready", "vd_ready", "kd_used", "vd_used"))
        added, squared, var_ready, y_ready = (sem(n) for n in ("pre_added", "pre_squared", "pre_var", "pre_y"))
        vd_stored = sem("vd_stored")
        stacked, turned, kept = sem("pre_stacked"), sem("pre_turned"), sem("pre_kept")

        order = ["wkd", "yd", "wvd", "wk", "wq", "wv", "wo"]
        source = {n: raw[n][:, :, :] for n in raw}
        source["yd"] = yd[:, :, :, :].rearrange("p k b d -> p k (b d)")
        target = {**{n: w[n] for n in w}, **{n: wd[n] for n in wd}, "yd": (yd_hi, yd_lo)}

        with nc.Block() as block:
            @block.sync
            def _(sp):
                def load(name, dst, src):
                    sp.dma_start(dst, src).then_inc(loaded[name], 16)

                def wide(name):
                    return a[name].rearrange("(k p) n -> p k n", p=P)

                def spread(ap):
                    return ap.unsqueeze(0).to_broadcast([P, ap.shape[0]])

                load("wkd", raw["wkd"][:, :, :], wide("Wkv_dca")[:, :, 0:C])
                for k in range(KK):
                    load("yd", yd[:, k, :, :], a["ctxT"][:, k * P:(k + 1) * P, M:S].rearrange("b p d -> p b d"))
                load("bkd", bkd[:, :], spread(a["bkv_dca"][0:C]))
                load("wvd", raw["wvd"][:, :, :], wide("Wkv_dca")[:, :, C:2 * C])
                load("kd", kd_w[:, :], spread(a["kn_dca_w"]))
                load("kd", kd_b[:, :], spread(a["kn_dca_b"]))
                load("wk", raw["wk"][:, :, :], wide("Wk_heads"))
                load("wq", raw["wq"][:, :, :], wide("Wq"))
                load("wv", raw["wv"][:, :, :], wide("Wv_heads"))
                load("wo", raw["wo"][:, :, :], wide("Wo"))
                load("gates", gate_raw[:, 0:1], spread(a["g_xattn"]))
                load("gates", gate_raw[:, 1:2], spread(a["g_ffn"]))
                load("rows", rows["bq"][:, :], spread(a["bq"]))
                load("rows", rows["bk"][:, :], spread(a["bk_heads"]))
                load("rows", rows["bv"][:, :], spread(a["bv_heads"]))
                load("rows", bvd[:, :], spread(a["bkv_dca"][C:2 * C]))
                load("rows", rows["bo"][:, :], spread(a["bo"]))
                for n in norms:
                    load("rows", norms[n][:, :], spread(a[n]))
                sp.wait_ge(vd_used, ND)
                sp.dma_start(vd_dram.rearrange("(t p) v -> p t v", p=P),
                             vd[:, :, :, :].rearrange("p t h v -> p t (h v)")).then_inc(vd_stored, 16)
                sp.wait_ge(vd_stored, 16)

            @block.gpsimd
            def _(pool):
                nc.gpsimd.memset(identf[:, :], 0.0).then_inc(idents, 1)
                pool.wait_ge(idents, 1)
                nc.gpsimd.affine_select(out=identf[:, :], in_=identf[:, :], compare_op=ALU.not_equal, fill=1.0,
                                        base=0, pattern=[[-1, P]], channel_multiplier=1).then_inc(idents, 1)
                pool.wait_ge(idents, 2)
                nc.gpsimd.tensor_copy(identh[:, :], identf[:, :]).then_inc(idents, 1)

            @block.vector
            def _(dve):
                chain = Chain(dve, own)
                link = chain.link

                def center(ap, k):
                    m = mean[:, 0:k * H]
                    link(nc.vector.tensor_reduce(m, ap, AX.X, ALU.add))
                    link(nc.vector.tensor_scalar(m, m, -1.0 / HD, None, ALU.mult))
                    return nc.vector.tensor_tensor(ap, ap, m.unsqueeze(2).to_broadcast([P, k * H, HD]), ALU.add)

                link(nc.vector.memset(stack[:, :, 3 * HD:], 0.0))
                link(nc.vector.memset(stack[:, :, 3 * HD + 1:3 * HD + 4:2], UNIT))
                link(nc.vector.memset(vd[:, :, :, 0:HD + 1], 0.0))
                link(nc.vector.memset(vd[:, :, :, VW - 1:VW], 1.0))
                for n, name in enumerate(order):
                    dve.wait_ge(loaded[name], 32 if name == "yd" else 16)
                    if name in ("wkd", "wk", "wq"):
                        k = KC if name == "wq" else KK
                        center(raw[name][:, :, :].rearrange("p k (h d) -> p (k h) d", d=HD), k).then_inc(centered, 1)
                    dve.wait_ge(hi_ready, n + 1)
                    nc.vector.tensor_tensor(target[name][1][:, :, :], source[name], target[name][0][:, :, :],
                                            ALU.subtract).then_inc(lo_ready, 1)
                dve.wait_ge(loaded["bkd"], 16)
                dve.wait_ge(loaded["kd"], 32)
                dve.wait_ge(loaded["rows"], 16 * (5 + len(norms)))
                link(center(heads(bkd[:, :]), 1))
                link(center(heads(rows["bq"][:, :]), 1))
                link(center(heads(rows["bk"][:, :]), 1))
                link(nc.vector.tensor_tensor(rows["bv"][:, :], rows["bv"][:, :], bvd[:, :], ALU.add))
                dve.wait_ge(tanhs, 1)
                link(nc.vector.tensor_scalar(rows["bo"][:, :], rows["bo"][:, :], gates[:, 0:1], None, ALU.mult))
                for t in range(ND):
                    dve.wait_ge(kd_ready, t + 1)
                    nc.vector.tensor_tensor(kb[:, :], pk[:, :], bkd[:, :], ALU.add).then_inc(added, 1)
                    dve.wait_ge(vd_ready, t + 1)
                    nc.vector.tensor_copy(vd[:, t, :, HD + 1:2 * HD + 1], heads(pv[:, :])).then_inc(vd_used, 1)
                    dve.wait_ge(squared, t + 1)
                    link(nc.vector.tensor_reduce(r[:, :], heads(sq[:, :]), AX.X, ALU.add))
                    nc.vector.tensor_scalar(ve[:, :], r[:, :], 1.0 / HD, EPS_HEAD, ALU.mult, ALU.add)\
                        .then_inc(var_ready, 1)
                    dve.wait_ge(y_ready, t + 1)
                    link(nc.vector.tensor_tensor(r[:, :], y[:, :], y[:, :], ALU.mult))
                    link(nc.vector.tensor_tensor(r[:, :], r[:, :], ve[:, :], ALU.mult))
                    link(nc.vector.tensor_scalar(r[:, :], r[:, :], -0.5, 1.5, ALU.mult, ALU.add))
                    link(nc.vector.tensor_tensor(r[:, :], r[:, :], y[:, :], ALU.mult))
                    dve.wait_ge(added, t + 1)
                    link(nc.vector.tensor_tensor(heads(kn[:, :]), heads(kb[:, :]),
                                                 r[:, :].unsqueeze(2).to_broadcast([P, H, HD]), ALU.mult))
                    link(nc.vector.tensor_tensor(heads(kn[:, :]), heads(kn[:, :]),
                                                 kd_w[:, :].unsqueeze(1).to_broadcast([P, H, HD]), ALU.mult))
                    link(nc.vector.tensor_tensor(heads(kn[:, :]), heads(kn[:, :]),
                                                 kd_b[:, :].unsqueeze(1).to_broadcast([P, H, HD]), ALU.add))
                    if t:
                        dve.wait_ge(turned, 2 * t)
                    link(nc.vector.tensor_copy(stack[:, :, 0:HD], heads(kn[:, :])))
                    link(nc.vector.tensor_copy(stack[:, :, HD:2 * HD], stack[:, :, 0:HD]))
                    nc.vector.tensor_tensor(stack[:, :, 2 * HD:3 * HD], heads(kn[:, :]), stack[:, :, 0:HD],
                                            ALU.subtract).then_inc(stacked, 1)
                    for j in range(2):
                        dve.wait_ge(turned, 2 * t + j + 1)
                        nc.vector.tensor_copy(kdT[:, 8 * j:8 * j + 8, t * P:(t + 1) * P], pt[j][:, :, :])\
                            .then_inc(kept, 1)

            @block.scalar
            def _(act):
                def hi(n):
                    name = order[n]
                    if name in ("wkd", "wk", "wq"):
                        act.wait_ge(centered, 1 + ("wkd", "wk", "wq").index(name))
                    else:
                        act.wait_ge(loaded[name], 32 if name == "yd" else 16)
                    nc.scalar.activation(target[name][0][:, :, :], source[name], ACT.Copy).then_inc(hi_ready, 1)

                act.wait_ge(loaded["wkd"], 16)
                for n in range(len(order)):
                    hi(n)
                act.wait_ge(loaded["gates"], 32)
                nc.scalar.activation(gates[:, :], gate_raw[:, :], ACT.Tanh).then_inc(tanhs, 1)
                act.preload_act_table_set("natural_log_exp_and_others")
                for t in range(ND):
                    act.wait_ge(added, t + 1)
                    if t:
                        act.wait_ge(var_ready, t)
                    nc.scalar.activation(sq[:, :], kb[:, :], ACT.Square).then_inc(squared, 1)
                    act.wait_ge(var_ready, t + 1)
                    nc.scalar.activation(lnv[:, :], ve[:, :], ACT.Ln).then_inc(own_act, 1)
                    act.wait_ge(own_act, t + 1)
                    nc.scalar.activation(y[:, :], lnv[:, :], ACT.Exp, scale=-0.5).then_inc(y_ready, 1)

            @block.tensor
            def _(pe):
                def product(dst, name, t):
                    pairs = ((yd_hi, 0), (yd_hi, 1), (yd_lo, 0))
                    for n, (k, (y_part, part)) in enumerate((k, p) for k in range(KK) for p in pairs):
                        last = nc.tensor.matmul(dst[:, :], y_part[:, k, t * P:(t + 1) * P],
                                                wd[name][part][:, k, :], start=n == 0, stop=n == 3 * KK - 1)
                    return last

                pe.wait_ge(lo_ready, 3)
                pe.wait_ge(hi_ready, 3)
                pe.wait_ge(idents, 3)
                for t in range(ND):
                    if t:
                        pe.wait_ge(added, t)
                        pe.wait_ge(vd_used, t)
                    product(pk, "wkd", t).then_inc(kd_ready, 1)
                    product(pv, "wvd", t).then_inc(vd_ready, 1)
                    pe.wait_ge(stacked, t + 1)
                    for j in range(2):
                        if t:
                            pe.wait_ge(kept, 2 * (t - 1) + j + 1)
                        for h in range(8):
                            last = nc.tensor.transpose(pt[j][:, h, :], stack[:, 8 * j + h, :], identh[:, :])
                        last.then_inc(turned, 1)


def attend(nc, a, w, rows, norms, kdT, vd_dram, gates, identf, identh, x1_dram):
    with ExitStack() as ctx:
        def sb(name, shape, dt=F32):
            return ctx.enter_context(nc.sbuf_tensor(name, shape, dt))

        def sem(name):
            return ctx.enter_context(nc.semaphore(name))

        def bank(name):
            return ctx.enter_context(nc.psum_tensor(name, [P, 512], F32))

        x_raw = [sb(f"x_raw{i}", [T, C]) for i in range(2)]
        xb = [sb(f"xb{i}", [T, C]) for i in range(2)]
        y_raw = [sb(f"y_raw{i}", [P, KK, S]) for i in range(2)]
        y_hi, y_lo = sb("y_hi", [P, KK, S], F32R), sb("y_lo", [P, KK, S], F32R)
        xn = sb("xn", [T, C])
        x_hi, x_lo = sb("x_hi", [P, KC, T], F32R), sb("x_lo", [P, KC, T], F32R)
        bn, mv, xve, xln, xy, xr = (sb(n, [T, k]) for n, k in
                                    (("bn", 6), ("mv", 2), ("xve", 1), ("xln", 1), ("xy", 1), ("xr", 1)))
        kb, sq, kn, ka = (sb(f"t_{n}", [P, C]) for n in ("kb", "sq", "kn", "ka"))
        ve, lnv, y, r = (sb(f"t_{n}", [P, H]) for n in ("ve", "lnv", "y", "r"))
        stacks = {n: sb(f"stack_{n}", [P, H, P], F16) for n in CHAIN}
        kT = [sb(f"kT{i}", [P, H, S + 1], F16) for i in range(2)]
        qT = [sb(f"qT{i}", [P, H, T], F16) for i in range(2)]
        v_main = [sb(f"v_main{i}", [P, 2, H, VW]) for i in range(2)]
        v_last = [sb(f"v_last{i}", [P, H, VW]) for i in range(2)]
        nmax = sb("nmax", [T, G, 2])
        shift = sb("shift", [T, H, HD], F16)
        p = [[sb(f"p{i}{k}", [P, G * T]) for k in range(3)] for i in range(2)]
        ctxT_raw = sb("ctxT_raw", [VW, H, T])
        inv = sb("inv", [T, G, 2])
        cm, cd = sb("cm", [T, G, HD]), sb("cd", [T, G, HD])
        ctxn = sb("ctxn", [T, H, HD])
        c_hi, c_lo = sb("c_hi", [P, KC, T], F32R), sb("c_lo", [P, KC, T], F32R)
        x1 = [sb(f"x1_{i}", [T, C + 2]) for i in range(2)]

        work = [bank(f"work{i}") for i in range(BANKS)]
        top = [bank(f"top{i}") for i in range(2)]
        score = [bank(f"score{i}") for i in range(2)]
        pv = bank("pv_acc")

        w_ready = [sem(f"work_ready{i}") for i in range(BANKS)]
        w_free = [sem(f"work_free{i}") for i in range(BANKS)]
        x_in, y_in, vd_in, x1_out = ([sem(f"{n}{i}") for i in range(2)] for n in ("x_in", "y_in", "vd_in", "x1_out"))
        consts = sem("consts_ready")
        own_v, own_a, own_p = sem("vector_own2"), sem("scalar_own2"), sem("pool_own2")
        names = ["x_var", "x_rsqrt", "x_normed", "x_hi_ready", "y_hi_ready", "y_lo_ready", "xb_ready", "squared",
                 "var_ready", "rsqrt_ready", "normed", "affine_ready", "high_ready", "copied_ready", "low_ready",
                 "kd_copied", "top_ready", "top_free", "shift_ready", "score_ready", "exp_ready", "pv_ready",
                 "ctx_copied", "ctx_ready", "c_hi_ready", "x1_ready"]
        s = {n: sem(n) for n in names}

        def wait_free(pe, st, use):
            at_least(pe, w_free[st.bank(use)], st.before(use))

        def wait_ready(eng, st, use):
            eng.wait_ge(w_ready[st.bank(use)], st.before(use) + 1)

        def wait_read(pe, st, use):
            pe.wait_ge(w_free[st.bank(use)], st.before(use) + 1)

        def halves(use, st, n):
            return work[st.bank(use)][:, :].bitcast(F16).rearrange("p (h k) -> p h k", h=8)[:, :, 0:n]

        def rstd(nv, link, out_, v, guess):
            link(nv.tensor_tensor(out_, guess, guess, ALU.mult))
            link(nv.tensor_tensor(out_, out_, v, ALU.mult))
            link(nv.tensor_scalar(out_, out_, -0.5, 1.5, ALU.mult, ALU.add))
            link(nv.tensor_tensor(out_, out_, guess, ALU.mult))

        with nc.Block() as block:
            @block.sync
            def _(sp):
                def load(n, par):
                    at_least(sp, s["x_normed"], n - 1)
                    at_least(sp, s["xb_ready"], n - 1)
                    sp.dma_start(x_raw[par][:, :], a["x"].rearrange("b t c -> (b t) c")[one(n, T), :])\
                        .then_inc(x_in[par], 16)
                    at_least(sp, s["y_lo_ready"], n - 1)
                    sp.dma_start(y_raw[par][:, :, :], a["ctxT"].rearrange("b (k p) m -> p (b k) m", p=P)
                                 [:, one(n, KK), :]).then_inc(y_in[par], 16)

                def dca_values(n, par):
                    at_least(sp, s["pv_ready"], NG * (n - 1))
                    sp.dma_start(v_last[par][ROWS[2]:KEYS[2], :, :],
                                 vd_dram[one(n, DCA), :].rearrange("k (h v) -> k h v", h=H)).then_inc(vd_in[par], 16)

                def store(n, par):
                    sp.wait_ge(s["x1_ready"], n + 1)
                    sp.dma_start(x1_dram[one(n, T), :], x1[par][:, :]).then_inc(x1_out[par], 16)

                for par in range(2):
                    sp.sem_inc(x1_out[par], 1)
                sp.wait_ge(consts, 1)
                for n in range(2):
                    load(n, n)
                    dca_values(n, n)
                with sp.Fori(0, (B - 2) // 2) as i:
                    for par in range(2):
                        n = i * 2 + (2 + par)
                        load(n, par)
                        dca_values(n, par)
                        store(i * 2 + par, par)
                for n in (B - 2, B - 1):
                    store(n, n % 2)
                for par in range(2):
                    sp.wait_ge(x1_out[par], 16 * (B // 2) + 1)

            @block.vector
            def _(dve):
                chain = Chain(dve, own_v, VECTOR_OWN)
                link = chain.link
                nv = nc.vector

                for n in CHAIN:
                    link(nv.memset(stacks[n][:, :, 3 * HD:], 0.0))
                    if n != "Q":
                        link(nv.memset(stacks[n][:, :, 3 * HD:3 * HD + 3:2], UNIT))
                link(nv.memset(shift[:, :, :], 0.0))
                for i in range(2):
                    link(nv.memset(v_main[i][:, :, :, HD + 1:], 0.0))
                    link(nv.memset(v_main[i][:, :, :, HD:HD + 1], 1.0))
                    link(nv.memset(v_last[i][:, :, HD + 1:], 0.0))
                    last = nv.memset(v_last[i][:, :, HD:HD + 1], 1.0)
                    if i == 0:
                        link(last)
                last.then_inc(consts, 1)

                def row_norm(n, par):
                    dve.wait_ge(x_in[par], transfers(n, par, 1))
                    link(nv.bn_stats(bn[:, :], x_raw[par][:, :]))
                    nv.memset(xve[:, :], 0.0)
                    link(nv.bn_aggr(mv[:, :], bn[:, :]))
                    nv.tensor_scalar(xve[:, :], mv[:, 1:2], EPS_ROW, None, ALU.add).then_inc(s["x_var"], 1)
                    dve.wait_ge(s["x_rsqrt"], n + 1)
                    rstd(nv, link, xr[:, :], xve[:, :], xy[:, :])
                    nv.tensor_scalar(xn[:, :], x_raw[par][:, :], mv[:, 0:1], xr[:, :], ALU.subtract, ALU.mult)\
                        .then_inc(s["x_normed"], 1)

                def add_bias(st, tile):
                    m = T if tile == "Q" else ROWS[int(tile[1])]
                    wait_ready(dve, st, tile)
                    nv.tensor_tensor(kb[0:m, :], work[st.bank(tile)][0:m, :],
                                     rows["bq" if tile == "Q" else "bk"][0:m, :], ALU.add)\
                        .then_inc(w_free[st.bank(tile)], 1)

                def head_norm(st, tile):
                    m, n = (T if tile == "Q" else ROWS[int(tile[1])]), 4 * (st.b + 1) + CHAIN.index(tile)
                    dve.wait_ge(s["squared"], n + 1)
                    link(nv.tensor_reduce(r[0:m, :], heads(sq[0:m, :]), AX.X, ALU.add))
                    nv.tensor_scalar(ve[0:m, :], r[0:m, :], 1.0 / HD, EPS_HEAD, ALU.mult, ALU.add)\
                        .then_inc(s["var_ready"], 1)
                    dve.wait_ge(s["rsqrt_ready"], n + 1)
                    rstd(nv, link, r[0:m, :], ve[0:m, :], y[0:m, :])
                    at_least(dve, s["affine_ready"], n)
                    nv.tensor_tensor(heads(kn[0:m, :]), heads(kb[0:m, :]),
                                     r[0:m, :].unsqueeze(2).to_broadcast([m, H, HD]), ALU.mult)\
                        .then_inc(s["normed"], 1)

                def high(st, tile):
                    m, n = (T if tile == "Q" else ROWS[int(tile[1])]), 4 * (st.b + 1) + CHAIN.index(tile)
                    stack, second = stacks[tile], 2 * HD if tile == "Q" else HD
                    dve.wait_ge(s["affine_ready"], n + 1)
                    nv.tensor_copy(stack[0:m, :, 0:HD], heads(ka[0:m, :])).then_inc(s["high_ready"], 1)
                    dve.wait_ge(s["high_ready"], n + 1)
                    nv.tensor_copy(stack[0:m, :, second:second + HD], stack[0:m, :, 0:HD])\
                        .then_inc(s["copied_ready"], 1)

                def maxima(b, g, lo, up):
                    for h in range(lo, up):
                        n = b * H + (G * g + h)
                        dve.wait_ge(s["top_ready"], n + 1)
                        nv.tensor_reduce(nmax[:, h, 0:1], top[h % 2][0:T, 0:M], AX.X, ALU.max, negate=True)
                        nv.tensor_reduce(nmax[:, h, 1:2], top[h % 2][0:T, M:S], AX.X, ALU.max, negate=True)\
                            .then_inc(s["top_free"], 1)

                def shifts(b, g):
                    dve.wait_ge(s["top_free"], b * H + G * (g + 1))
                    hs = shift[:, G * g:G * g + G, :]
                    link(nv.tensor_scalar(hs[:, :, 0:2], nmax[:, :, :], 1.0 / UNIT, None, ALU.mult))
                    nv.scalar_tensor_tensor(out=hs[:, :, 2:4], in0=nmax[:, :, :], scalar=1.0 / UNIT,
                                            in1=hs[:, :, 0:2], op0=ALU.mult, op1=ALU.subtract)\
                        .then_inc(s["shift_ready"], 1)

                def context(st, use, g):
                    wait_ready(dve, st, use)
                    ct = work[st.bank(use)][0:T, 0:G * VW].rearrange("t (h v) -> t h v", v=VW)
                    wide = [T, G, HD]
                    link(nv.reciprocal(inv[:, :, :], ct[:, :, HD:VW:HD + 1]))
                    link(nv.tensor_tensor(cm[:, :, :], ct[:, :, 0:HD], inv[:, :, 0:1].to_broadcast(wide), ALU.mult))
                    nv.tensor_tensor(cd[:, :, :], ct[:, :, HD + 1:VW - 1], inv[:, :, 1:2].to_broadcast(wide),
                                     ALU.mult).then_inc(w_free[st.bank(use)], 1)
                    link(nv.tensor_tensor(cm[:, :, :], cm[:, :, :], heads(rows["bv"][0:T, :])[:, G * g:G * g + G, :],
                                          ALU.add))
                    dve.wait_ge(w_free[st.bank(use)], st.before(use) + 1)
                    nv.tensor_tensor(ctxn[:, G * g:G * g + G, :], cm[:, :, :], cd[:, :, :], ALU.add)\
                        .then_inc(s["ctx_ready"], 1)

                def key_copy(st, tile):
                    k = int(tile[2])
                    wait_ready(dve, st, tile)
                    nv.tensor_copy(kT[1 - st.parity][:, 8:16, k * P:k * P + ROWS[k]], halves(tile, st, ROWS[k]))\
                        .then_inc(w_free[st.bank(tile)], 1)

                def low_rows(st, use, lo, hi, hi_sem, value):
                    wait_ready(dve, st, use)
                    dve.wait_ge(hi_sem, value)
                    nv.tensor_tensor(lo[:, :, :].rearrange("p k t -> p (k t)"), work[st.bank(use)][:, 0:KC * T],
                                     hi[:, :, :].rearrange("p k t -> p (k t)"), ALU.subtract)\
                        .then_inc(w_free[st.bank(use)], 1)

                def body(st):
                    n, npar = st.b + 1, 1 - st.parity
                    if not st.c and st.a:
                        row_norm(0, 0)
                    if st.d:
                        context(st, "ct3", NG - 1)
                    if st.c:
                        maxima(st.b, 1, 0, 2)
                    if st.a:
                        low_rows(st, "xT", x_lo, x_hi, s["x_hi_ready"], n + 1)
                        add_bias(st, "K0")
                    if st.a:
                        head_norm(st, "K0")
                    if st.c:
                        maxima(st.b, 1, 2, 4)
                        shifts(st.b, 1)
                    if st.a:
                        high(st, "K0")
                    if st.d:
                        d = st.b - 1
                        low_rows(st, "cT", c_lo, c_hi, s["c_hi_ready"], st.b)
                        wait_ready(dve, st, "Wo")
                        dve.wait_ge(x1_out[npar], transfers(d, npar, 0) + 1)
                        dve.wait_ge(s["xb_ready"], st.b)
                        nv.scalar_tensor_tensor(out=x1[npar][:, 0:C], in0=work[st.bank("Wo")][0:T, :],
                                                scalar=gates[0:T, 0:1], in1=xb[npar][:, :],
                                                op0=ALU.mult, op1=ALU.add).then_inc(w_free[st.bank("Wo")], 1)
                        dve.wait_ge(w_free[st.bank("Wo")], st.before("Wo") + 1)
                        link(nv.bn_stats(bn[:, :], x1[npar][:, 0:C]))
                        nv.memset(xve[:, :], 0.0)
                        nv.bn_aggr(x1[npar][:, C:C + 2], bn[:, :]).then_inc(s["x1_ready"], 1)
                        dve.wait_ge(s["x1_ready"], st.b)
                    if st.c:
                        context(st, "ct0", 0)
                        maxima(st.b, 2, 0, 2)
                    if st.a:
                        add_bias(st, "Q")
                        head_norm(st, "Q")
                        high(st, "Q")
                    if st.c:
                        maxima(st.b, 2, 2, 4)
                        shifts(st.b, 2)
                    if st.a:
                        add_bias(st, "K1")
                        head_norm(st, "K1")
                        high(st, "K1")
                    if st.c:
                        context(st, "ct1", 1)
                        maxima(st.b, 3, 0, 2)
                    if st.a:
                        key_copy(st, "kt01")
                        add_bias(st, "K2")
                        head_norm(st, "K2")
                    if st.c:
                        maxima(st.b, 3, 2, 4)
                        shifts(st.b, 3)
                    if st.a:
                        high(st, "K2")
                    if st.c:
                        context(st, "ct2", 2)
                    if st.a:
                        key_copy(st, "kt11")
                        key_copy(st, "kt21")
                        if st.pre:
                            row_norm(n + 1, 1 - npar)
                        maxima(n, 0, 0, 4)
                        shifts(n, 0)

                run_steps(dve, body, chain)

            @block.scalar
            def _(act):
                chain = Chain(act, own_a, SCALAR_OWN)
                link = chain.link
                ns = nc.scalar
                act.preload_act_table_set("natural_log_exp_and_others")

                def square(st, tile):
                    m, n = (T if tile == "Q" else ROWS[int(tile[1])]), 4 * (st.b + 1) + CHAIN.index(tile)
                    wait_read(act, st, tile)
                    at_least(act, s["var_ready"], n)
                    ns.activation(sq[0:m, :], kb[0:m, :], ACT.Square).then_inc(s["squared"], 1)

                def guess(st, tile):
                    m, n = (T if tile == "Q" else ROWS[int(tile[1])]), 4 * (st.b + 1) + CHAIN.index(tile)
                    act.wait_ge(s["var_ready"], n + 1)
                    link(ns.activation(lnv[0:m, :], ve[0:m, :], ACT.Ln))
                    ns.activation(y[0:m, :], lnv[0:m, :], ACT.Exp, scale=-0.5).then_inc(s["rsqrt_ready"], 1)

                def row_guess(n):
                    act.wait_ge(s["x_var"], n + 1)
                    link(ns.activation(xln[:, :], xve[:, :], ACT.Ln))
                    ns.activation(xy[:, :], xln[:, :], ACT.Exp, scale=-0.5).then_inc(s["x_rsqrt"], 1)

                def context_high(n, par):
                    act.wait_ge(y_in[par], transfers(n, par, 1))
                    ns.activation(y_hi[:, :, :], y_raw[par][:, :, :], ACT.Copy).then_inc(s["y_hi_ready"], 1)

                def copy_pv(b, g):
                    act.wait_ge(s["pv_ready"], b * NG + (g + 1))
                    ns.activation(ctxT_raw[:, G * g:G * g + G, :],
                                  pv[0:VW, 0:G * T].rearrange("v (h t) -> v h t", h=G), ACT.Copy)\
                        .then_inc(s["ctx_copied"], 1)

                def shift_rows(st, g):
                    use = f"mt{g}"
                    wait_ready(act, st, use)
                    ns.activation(qT[st.parity][3 * HD:P, G * g:G * g + G, :],
                                  work[st.bank(use)][3 * HD:P, :].bitcast(F16)[:, 0:G * T]
                                  .rearrange("p (h t) -> p h t", h=G), ACT.Copy).then_inc(w_free[st.bank(use)], 1)

                def exps(b, g):
                    at_least(act, s["pv_ready"], b * NG + (g - 1))
                    for k in range(3):
                        n = b * (3 * NG) + (3 * g + k)
                        act.wait_ge(s["score_ready"], n + 1)
                        ns.activation(p[g % 2][k][0:KEYS[k], :], score[(3 * g + k) % 2][0:KEYS[k], 0:G * T],
                                      ACT.Exp, scale=SCALE).then_inc(s["exp_ready"], 1)

                def values(st, tile):
                    k, par = int(tile[1]), 1 - st.parity
                    wait_ready(act, st, tile)
                    dst = v_last[par][0:ROWS[2], :, 0:HD] if k == 2 else v_main[par][:, k, :, 0:HD]
                    ns.activation(dst, heads(work[st.bank(tile)][0:ROWS[k], :]), ACT.Copy)\
                        .then_inc(w_free[st.bank(tile)], 1)

                def key_copy(st, tile):
                    k = int(tile[2])
                    wait_ready(act, st, tile)
                    ns.activation(kT[1 - st.parity][:, 0:8, k * P:k * P + ROWS[k]], halves(tile, st, ROWS[k]),
                                  ACT.Copy).then_inc(w_free[st.bank(tile)], 1)

                def query_copy(st, j):
                    use = f"qt{j}"
                    wait_ready(act, st, use)
                    ns.activation(qT[1 - st.parity][:, 8 * j:8 * j + 8, :], halves(use, st, T), ACT.Copy)\
                        .then_inc(w_free[st.bank(use)], 1)

                def high_rows(st, use, hi, done):
                    wait_ready(act, st, use)
                    ns.activation(hi[:, :, :].rearrange("p k t -> p (k t)"), work[st.bank(use)][:, 0:KC * T],
                                  ACT.Copy).then_inc(done, 1)

                def body(st):
                    n, npar = st.b + 1, 1 - st.parity
                    if not st.c and st.a:
                        context_high(0, 0)
                        row_guess(0)
                    if st.d:
                        copy_pv(st.b - 1, NG - 1)
                    if st.c:
                        shift_rows(st, 0)
                        exps(st.b, 0)
                    if st.a:
                        high_rows(st, "xT", x_hi, s["x_hi_ready"])
                        square(st, "K0")
                        guess(st, "K0")
                        values(st, "V0")
                    if st.d:
                        high_rows(st, "cT", c_hi, s["c_hi_ready"])
                    if st.c:
                        copy_pv(st.b, 0)
                        shift_rows(st, 1)
                        exps(st.b, 1)
                    if st.a:
                        square(st, "Q")
                        guess(st, "Q")
                        square(st, "K1")
                        guess(st, "K1")
                        values(st, "V1")
                    if st.c:
                        copy_pv(st.b, 1)
                        shift_rows(st, 2)
                        exps(st.b, 2)
                    if st.a:
                        key_copy(st, "kt00")
                        query_copy(st, 0)
                        query_copy(st, 1)
                        square(st, "K2")
                        guess(st, "K2")
                        values(st, "V2")
                    if st.c:
                        copy_pv(st.b, 2)
                        shift_rows(st, 3)
                        exps(st.b, 3)
                    if st.a:
                        key_copy(st, "kt10")
                        key_copy(st, "kt20")
                        if st.pre:
                            context_high(n + 1, 1 - npar)
                            row_guess(n + 1)

                run_steps(act, body, chain)

            @block.gpsimd
            def _(pool):
                chain = Chain(pool, own_p, POOL_OWN)
                link = chain.link
                ng = nc.gpsimd

                def affine(st, tile):
                    m, n = (T if tile == "Q" else ROWS[int(tile[1])]), 4 * (st.b + 1) + CHAIN.index(tile)
                    kind = "qn" if tile == "Q" else "kn"
                    pool.wait_ge(s["normed"], n + 1)
                    at_least(pool, s["high_ready"], n)
                    link(ng.tensor_tensor(heads(ka[0:m, :]), heads(kn[0:m, :]),
                                          norms[kind + "_w"][0:m, :].unsqueeze(1).to_broadcast([m, H, HD]), ALU.mult))
                    ng.tensor_tensor(heads(ka[0:m, :]), heads(ka[0:m, :]),
                                     norms[kind + "_b"][0:m, :].unsqueeze(1).to_broadcast([m, H, HD]), ALU.add)\
                        .then_inc(s["affine_ready"], 1)
                    pool.wait_ge(s["affine_ready"], n + 1)
                    pool.wait_ge(s["high_ready"], n + 1)
                    at = HD if tile == "Q" else 2 * HD
                    ng.tensor_tensor(stacks[tile][0:m, :, at:at + HD], heads(ka[0:m, :]),
                                     stacks[tile][0:m, :, 0:HD], ALU.subtract).then_inc(s["low_ready"], 1)
                    pool.wait_ge(s["low_ready"], n + 1)

                def context_low(n, par):
                    pool.wait_ge(s["y_hi_ready"], n + 1)
                    ng.tensor_tensor(y_lo[:, :, :], y_raw[par][:, :, :], y_hi[:, :, :], ALU.subtract)\
                        .then_inc(s["y_lo_ready"], 1)

                def body(st):
                    if not st.a:
                        return
                    n, npar = st.b + 1, 1 - st.parity
                    if not st.c:
                        context_low(0, 0)
                    affine(st, "K0")
                    if st.c:
                        at_least(pool, s["x1_ready"], st.b)
                    pool.wait_ge(x_in[npar], transfers(n, npar, 1))
                    ng.tensor_tensor(xb[npar][:, :], x_raw[npar][:, :], rows["bo"][0:T, :], ALU.add)\
                        .then_inc(s["xb_ready"], 1)
                    affine(st, "Q")
                    affine(st, "K1")
                    ng.tensor_copy(kT[npar][:, :, M:S],
                                   kdT[:, :, one(n, DCA)]).then_inc(s["kd_copied"], 1)
                    affine(st, "K2")
                    if st.pre:
                        context_low(n + 1, 1 - npar)

                run_steps(pool, body, chain)

            @block.tensor
            def _(pe):
                nt = nc.tensor

                def three(dst, m, left, right, depth, cols):
                    parts = [(k, i, j) for k in range(depth) for i, j in ((0, 0), (0, 1), (1, 0))]
                    for n, (k, i, j) in enumerate(parts):
                        last = nt.matmul(dst, left[i][:, k, cols[0]:cols[0] + m], right[j][:, k, :],
                                         start=n == 0, stop=n == len(parts) - 1)
                    return last

                def turn_rows(st, use, src):
                    wait_free(pe, st, use)
                    for k in range(KC):
                        last = nt.transpose(work[st.bank(use)][:, k * T:(k + 1) * T], src[:, k * P:(k + 1) * P],
                                            identf[0:T, 0:T])
                    last.then_inc(w_ready[st.bank(use)], 1)

                def project(st, tile):
                    k = int(tile[1])
                    wait_free(pe, st, tile)
                    three(work[st.bank(tile)][0:ROWS[k], :], ROWS[k], (y_hi, y_lo), w["w" + tile[0].lower()], KK,
                          (k * P,)).then_inc(w_ready[st.bank(tile)], 1)

                def turn_stack(st, use, tile, j):
                    m, n = (T if tile == "Q" else ROWS[int(tile[1])]), 4 * (st.b + 1) + CHAIN.index(tile)
                    pe.wait_ge(s["copied_ready"], n + 1)
                    pe.wait_ge(s["low_ready"], n + 1)
                    wait_free(pe, st, use)
                    dst = halves(use, st, m)
                    for h in range(8):
                        last = nt.transpose(dst[:, h, :], stacks[tile][0:m, 8 * j + h, :], identh[0:m, 0:m])
                    last.then_inc(w_ready[st.bank(use)], 1)

                def tops(b, par, g, lo, up):
                    for h in range(lo, up):
                        n = b * H + (G * g + h)
                        at_least(pe, s["top_free"], n - 1)
                        nt.matmul(top[h % 2][0:T, 0:S], qT[par][:, G * g + h, :], kT[par][:, G * g + h, 0:S],
                                  start=True, stop=True).then_inc(s["top_ready"], 1)

                def turn_shift(st, g):
                    use = f"mt{g}"
                    pe.wait_ge(s["shift_ready"], st.b * NG + (g + 1))
                    wait_free(pe, st, use)
                    dst = work[st.bank(use)][3 * HD:P, :].bitcast(F16)
                    for h in range(G):
                        last = nt.transpose(dst[:, h * T:(h + 1) * T], shift[:, G * g + h, :], identh[0:T, 0:T])
                    last.then_inc(w_ready[st.bank(use)], 1)

                def scores(st, g):
                    wait_read(pe, st, f"mt{g}")
                    for k in range(3):
                        n = st.b * (3 * NG) + (3 * g + k)
                        at_least(pe, s["exp_ready"], n - 1)
                        for h in range(G):
                            last = nt.matmul(score[(3 * g + k) % 2][0:KEYS[k], h * T:(h + 1) * T],
                                             kT[st.parity][:, G * g + h, k * P:k * P + KEYS[k]],
                                             qT[st.parity][:, G * g + h, :], start=True, stop=True)
                        last.then_inc(s["score_ready"], 1)

                def weigh(st, g):
                    pe.wait_ge(s["exp_ready"], st.b * (3 * NG) + 3 * (g + 1))
                    at_least(pe, s["ctx_copied"], st.b * NG + g)
                    if g == 0:
                        pe.wait_ge(vd_in[st.parity], transfers(st.b, st.parity, 1))
                    for h in range(G):
                        cols = slice(h * T, (h + 1) * T)
                        nt.matmul(pv[0:VW, cols], v_last[st.parity][0:KEYS[2], G * g + h, :],
                                  p[g % 2][2][0:KEYS[2], cols], start=True, stop=False)
                        for k in range(2):
                            last = nt.matmul(pv[0:VW, cols], v_main[st.parity][:, k, G * g + h, :],
                                             p[g % 2][k][:, cols], start=False, stop=k == 1)
                    last.then_inc(s["pv_ready"], 1)

                def turn_context(st, use, b, g):
                    pe.wait_ge(s["ctx_copied"], b * NG + (g + 1))
                    wait_free(pe, st, use)
                    for h in range(G):
                        last = nt.transpose(work[st.bank(use)][0:T, h * VW:(h + 1) * VW],
                                            ctxT_raw[:, G * g + h, :], identf[0:VW, 0:VW])
                    last.then_inc(w_ready[st.bank(use)], 1)

                def body(st):
                    n, npar = st.b + 1, 1 - st.parity
                    if st.c:
                        turn_shift(st, 0)
                        scores(st, 0)
                    if st.d:
                        turn_context(st, "ct3", st.b - 1, NG - 1)
                    if st.c:
                        tops(st.b, st.parity, 1, 0, 2)
                    if st.a:
                        pe.wait_ge(s["x_normed"], n + 1)
                        turn_rows(st, "xT", xn)
                        pe.wait_ge(s["y_hi_ready"], n + 1)
                        pe.wait_ge(s["y_lo_ready"], n + 1)
                        project(st, "K0")
                        project(st, "V0")
                    if st.c:
                        tops(st.b, st.parity, 1, 2, 4)
                    if st.d:
                        pe.wait_ge(s["ctx_ready"], st.b * NG)
                        turn_rows(st, "cT", ctxn[:, :, :].rearrange("t h d -> t (h d)"))
                        wait_free(pe, st, "Wo")
                        wait_read(pe, st, "cT")
                        pe.wait_ge(s["c_hi_ready"], st.b)
                        three(work[st.bank("Wo")][0:T, :], T, (c_hi, c_lo), w["wo"], KC, (0,))\
                            .then_inc(w_ready[st.bank("Wo")], 1)
                    if st.c:
                        weigh(st, 0)
                    if st.c:
                        turn_shift(st, 1)
                        scores(st, 1)
                        turn_context(st, "ct0", st.b, 0)
                        tops(st.b, st.parity, 2, 0, 2)
                    if st.a:
                        wait_free(pe, st, "Q")
                        wait_read(pe, st, "xT")
                        pe.wait_ge(s["x_hi_ready"], n + 1)
                        three(work[st.bank("Q")][0:T, :], T, (x_hi, x_lo), w["wq"], KC, (0,))\
                            .then_inc(w_ready[st.bank("Q")], 1)
                        project(st, "K1")
                        project(st, "V1")
                    if st.c:
                        tops(st.b, st.parity, 2, 2, 4)
                        weigh(st, 1)
                    if st.c:
                        turn_shift(st, 2)
                        scores(st, 2)
                        turn_context(st, "ct1", st.b, 1)
                        tops(st.b, st.parity, 3, 0, 2)
                    if st.a:
                        turn_stack(st, "kt00", "K0", 0)
                        turn_stack(st, "kt01", "K0", 1)
                        turn_stack(st, "qt0", "Q", 0)
                        turn_stack(st, "qt1", "Q", 1)
                        project(st, "K2")
                        project(st, "V2")
                    if st.c:
                        tops(st.b, st.parity, 3, 2, 4)
                        weigh(st, 2)
                    if st.c:
                        turn_shift(st, 3)
                        scores(st, 3)
                        turn_context(st, "ct2", st.b, 2)
                    if st.a:
                        turn_stack(st, "kt10", "K1", 0)
                        turn_stack(st, "kt11", "K1", 1)
                        turn_stack(st, "kt20", "K2", 0)
                        turn_stack(st, "kt21", "K2", 1)
                    if st.c:
                        weigh(st, 3)
                    if st.a:
                        pe.wait_ge(s["kd_copied"], n + 1)
                        for use in ("kt11", "kt20", "kt21"):
                            wait_read(pe, st, use)
                        tops(n, npar, 0, 0, 4)

                run_steps(pe, body, None)


def experts(nc, a, gates, identf, x1_dram, out):
    N = G * T
    TURNS = B // G // 2
    SLOTS = 4
    NQ = 2 * KF
    with ExitStack() as ctx:
        def sb(name, shape, dt=F32):
            return ctx.enter_context(nc.sbuf_tensor(name, shape, dt))

        def sem(name):
            return ctx.enter_context(nc.semaphore(name))

        def bank(name):
            return ctx.enter_context(nc.psum_tensor(name, [P, 512], F32))

        up_w = [[sb(f"up{e}_{part}", [P, KC, F], F32R) for part in ("hi", "lo")] for e in range(2)]
        down_w = [[sb(f"down{e}_{part}", [P, KF, C], F32R) for part in ("hi", "lo")] for e in range(2)]
        raw = [sb(f"w_raw{i}", [P, 1024]) for i in range(2)]
        up_b = sb("up_b", [P, 2, KF])
        b0, b1, wg = sb("b0", [T, C]), sb("b1", [T, C]), sb("wg", [T, C])
        stats, rs = sb("stats", [T, B, 2]), sb("rs", [T, B])
        rs_ve, rs_ln, rs_y = sb("rs_ve", [T, B]), sb("rs_ln", [T, B]), sb("rs_y", [T, B])
        x1 = [sb(f"x1g{i}", [T, G, C + 2]) for i in range(2)]
        x2 = sb("x2", [T, G, C])
        junk = sb("junk", [T, C])
        score = sb("route", [T, G])
        scale = [sb(f"scale{i}", [T, 2, G]) for i in range(2)]
        rg = sb("rg", [T, G])
        t_hi, t_lo = sb("t_hi", [P, KC, N], F32R), sb("t_lo", [P, KC, N], F32R)
        act_out = [sb(f"act_out{i}", [P, N]) for i in range(2)]
        h_hi, h_lo = sb("h_hi", [P, SLOTS, N], F32R), sb("h_lo", [P, SLOTS, N], F32R)
        turn = [bank(f"turn{i}") for i in range(2)]
        hidden = [bank(f"hidden{i}") for i in range(2)]
        result = [bank(f"result{i}") for i in range(G)]

        names = ["w_in0", "w_in1", "w_hi_ready", "w_lo_ready", "rows_in", "stats_in", "x1_in0", "x1_in1", "out_done0", "out_done1",
                 "rs_var", "rs_guess", "own_v3", "own_a3", "rows_ready", "x2_ready", "biased", "based", "turned",
                 "t_hi_ready", "t_lo_ready", "hidden_ready", "act_ready", "h_ready", "down_ready", "result_free",
                 "final"]
        s = {n: sem(n) for n in names}

        CREDIT = {"h_ready": 2, "act_ready": 2, "t_lo_ready": 2, "down_ready": SLOTS, "final": 1}

        chunks = [(e, kind, k) for e in range(2) for kind in ("up", "down") for k in range(4)]

        def chunk(which, part):
            e, kind, k = which
            if kind == "up":
                return up_w[e][part][:, k, :]
            return down_w[e][part][:, 2 * k:2 * k + 2, :].rearrange("p k n -> p (k n)")

        def chunks_before(e, kind, k):
            return chunks.index((e, kind, k)) + 1

        with nc.Block() as block:
            @block.sync
            def _(sp):
                sp.dma_start(stats[:, :, :], x1_dram.rearrange("(b t) c -> t b c", t=T)[:, :, C:C + 2])\
                    .then_inc(s["stats_in"], 16)
                for par in range(2):
                    sp.sem_inc(s[f"out_done{par}"], 1)
                for e in range(2):
                    sp.dma_start(up_b[:, e, :], a[f"b{e}a"]).then_inc(s["rows_in"], 16)
                sp.dma_start(b0[:, :], a["b0b"].unsqueeze(0).to_broadcast([T, C])).then_inc(s["rows_in"], 16)
                sp.dma_start(b1[:, :], a["b1b"].unsqueeze(0).to_broadcast([T, C])).then_inc(s["rows_in"], 16)
                sp.dma_start(wg[:, :], a["Wg"][0:1, :].to_broadcast([T, C])).then_inc(s["rows_in"], 16)
                sp.dma_start(junk[:, :], a["Wg"][1:2, :].to_broadcast([T, C])).then_inc(s["rows_in"], 16)
                for n, (e, kind, k) in enumerate(chunks):
                    if n >= 2:
                        sp.wait_ge(s["w_lo_ready"], n - 1)
                    src = a[f"W{e}aT"][k * P:(k + 1) * P, :] if kind == "up" else \
                        a[f"W{e}bT"][2 * k * P:2 * (k + 1) * P, :].rearrange("(j p) n -> p j n", p=P)
                    dst = raw[n % 2][:, :] if kind == "up" else raw[n % 2][:, :].rearrange("p (j n) -> p j n", j=2)
                    sp.dma_start(dst, src).then_inc(s[f"w_in{n % 2}"], 16)
                with sp.Fori(0, TURNS) as i:
                    for par in range(2):
                        sp.wait_ge(s[f"out_done{par}"], i * (16 * G) + 1)
                        sp.dma_start(x1[par][:, :, :], x1_dram.rearrange("(b t) c -> t b c", t=T)
                                     [:, bass.ds(i * (2 * G) + par * G, G), :]).then_inc(s[f"x1_in{par}"], 16)
                    for par in range(2):
                        for t in range(G):
                            sp.wait_ge(s["final"], i * (2 * G) + (par * G + t + 1 + CREDIT["final"]))
                            sp.dma_start(out.rearrange("b t c -> (b t) c")
                                         [bass.ds((i * (2 * G) + (par * G + t)) * T, T), :], x1[par][:, t, 0:C])\
                                .then_inc(s[f"out_done{par}"], 16)
                for par in range(2):
                    sp.wait_ge(s[f"out_done{par}"], TURNS * 16 * G + 1)

            @block.vector
            def _(dve):
                nv = nc.vector
                chain = Chain(dve, s["own_v3"], 46)
                link = chain.link
                for n in ("h_ready", "t_lo_ready", "final"):
                    dve.sem_inc(s[n], CREDIT[n])

                def prelude(i, par):
                    link(nv.tensor_copy(rg[:, :], rs[:, bass.ds(i * (2 * G) + par * G, G)]))
                    dve.wait_ge(s[f"x1_in{par}"], i * 16 + 16)
                    for t in range(G):
                        n = i * (2 * G) + (par * G + t)
                        row = x1[par][:, t, :]
                        nv.tensor_scalar(x2[:, t, :], row[:, 0:C], row[:, C:C + 1], rg[:, t:t + 1],
                                         ALU.subtract, ALU.mult).then_inc(s["x2_ready"], 1)
                        dve.wait_ge(s["x2_ready"], n + 1)
                        link(nv.tensor_tensor_reduce(out=junk[:, :], in0=x2[:, t, :], in1=wg[:, :], scale=1.0,
                                                     scalar=0.0, op0=ALU.mult, op1=ALU.add,
                                                     accum_out=score[:, t:t + 1]))
                    link(nv.tensor_scalar(scale[par][:, 0, :], score[:, :], 0.0, gates[0:T, 1:2],
                                          ALU.is_ge, ALU.mult))
                    link(nv.tensor_scalar(scale[par][:, 1, :], scale[par][:, 0, :], -1.0, gates[0:T, 1:2],
                                          ALU.mult, ALU.add))
                    for t in range(G):
                        dve.wait_ge(s["biased"], i * (2 * G) + (par * G + t + 1))
                        nv.scalar_tensor_tensor(out=x1[par][:, t, 0:C], in0=b0[:, :],
                                                scalar=scale[par][:, 0, t:t + 1], in1=x1[par][:, t, 0:C],
                                                op0=ALU.mult, op1=ALU.add).then_inc(s["based"], 1)

                def split_weights(n):
                    dve.wait_ge(s["w_hi_ready"], n + 1)
                    nv.tensor_tensor(chunk(chunks[n], 1), raw[n % 2][:, :], chunk(chunks[n], 0), ALU.subtract)\
                        .then_inc(s["w_lo_ready"], 1)

                dve.wait_ge(s["stats_in"], 16)
                nv.tensor_scalar(rs_ve[:, :], stats[:, :, 1], EPS_ROW, None, ALU.add).then_inc(s["rs_var"], 1)
                dve.wait_ge(s["rs_guess"], 1)
                link(nv.tensor_tensor(rs[:, :], rs_y[:, :], rs_y[:, :], ALU.mult))
                link(nv.tensor_tensor(rs[:, :], rs[:, :], rs_ve[:, :], ALU.mult))
                link(nv.tensor_scalar(rs[:, :], rs[:, :], -0.5, 1.5, ALU.mult, ALU.add))
                link(nv.tensor_tensor(rs[:, :], rs[:, :], rs_y[:, :], ALU.mult))
                dve.wait_ge(s["rows_in"], 16 * 6)
                link(nv.tensor_tensor(wg[:, :], wg[:, :], junk[:, :], ALU.subtract))
                link(nv.tensor_tensor(b0[:, :], b0[:, :], b1[:, :], ALU.subtract))
                nv.tensor_scalar(b1[:, :], b1[:, :], gates[0:T, 1:2], None, ALU.mult).then_inc(s["rows_ready"], 1)
                for n in range(len(chunks)):
                    split_weights(n)

                def low_tokens(i, par):
                    for t in range(G):
                        n = i * (2 * G) + (par * G + t)
                        dve.wait_ge(s["t_hi_ready"], n + 1)
                        nv.tensor_tensor(t_lo[:, :, t * T:(t + 1) * T],
                                         turn[t % 2][:, 0:KC * T].rearrange("p (k t) -> p k t", k=KC),
                                         t_hi[:, :, t * T:(t + 1) * T], ALU.subtract).then_inc(s["t_lo_ready"], 1)

                def split_hidden(i, par, q):
                    n = i * (2 * NQ) + (par * NQ + q)
                    dve.wait_ge(s["act_ready"], n + (CREDIT["act_ready"] + 1))
                    dve.wait_ge(s["down_ready"], n + 1)
                    link(nv.tensor_copy(h_hi[:, q % SLOTS, :], act_out[q % 2][:, :]))
                    nv.tensor_tensor(h_lo[:, q % SLOTS, :], act_out[q % 2][:, :], h_hi[:, q % SLOTS, :],
                                     ALU.subtract).then_inc(s["h_ready"], 1)

                def gather(i, par, e):
                    dve.wait_ge(s["down_ready"], i * (2 * NQ) + (par * NQ + (e + 1) * KF + CREDIT["down_ready"]))
                    for t in range(G):
                        nv.scalar_tensor_tensor(out=x1[par][:, t, 0:C], in0=result[t][0:T, :],
                                                scalar=scale[par][:, e, t:t + 1], in1=x1[par][:, t, 0:C],
                                                op0=ALU.mult, op1=ALU.add)\
                            .then_inc(s["final" if e else "result_free"], 1)

                with dve.Fori(0, TURNS) as i:
                    chain.enter(i)
                    prelude(i, 0)
                    for par in range(2):
                        low_tokens(i, par)
                        for q in range(NQ):
                            split_hidden(i, par, q)
                            if q == KF:
                                gather(i, par, 0)
                            if q == KF + 2 and par == 0:
                                prelude(i, 1)
                        gather(i, par, 1)
                    chain.leave(TURNS)

            @block.gpsimd
            def _(pool):
                pool.wait_ge(s["rows_ready"], 1)
                with pool.Fori(0, TURNS) as i:
                    for par in range(2):
                        for t in range(G):
                            pool.wait_ge(s["x2_ready"], i * (2 * G) + (par * G + t + 1))
                            nc.gpsimd.tensor_tensor(x1[par][:, t, 0:C], x1[par][:, t, 0:C], b1[:, :], ALU.add)\
                                .then_inc(s["biased"], 1)

            @block.scalar
            def _(act):
                ns = nc.scalar
                act.sem_inc(s["act_ready"], CREDIT["act_ready"])
                act.preload_act_table_set("natural_log_exp_and_others")
                act.wait_ge(s["rs_var"], 1)
                ns.activation(rs_ln[:, :], rs_ve[:, :], ACT.Ln).then_inc(s["own_a3"], 1)
                act.wait_ge(s["own_a3"], 1)
                ns.activation(rs_y[:, :], rs_ln[:, :], ACT.Exp, scale=-0.5).then_inc(s["rs_guess"], 1)
                act.preload_act_table_set("gelu_and_others")
                for n in range(len(chunks)):
                    act.wait_ge(s[f"w_in{n % 2}"], 16 * (n // 2 + 1))
                    ns.activation(chunk(chunks[n], 0), raw[n % 2][:, :], ACT.Copy).then_inc(s["w_hi_ready"], 1)
                act.wait_ge(s["rows_in"], 16 * 6)
                with act.Fori(0, TURNS) as i:
                    for par in range(2):
                        for t in range(G):
                            act.wait_ge(s["turned"], i * (2 * G) + (par * G + t + 1))
                            ns.activation(t_hi[:, :, t * T:(t + 1) * T],
                                          turn[t % 2][:, 0:KC * T].rearrange("p (k t) -> p k t", k=KC),
                                          ACT.Copy).then_inc(s["t_hi_ready"], 1)
                        for q in range(NQ):
                            n = i * (2 * NQ) + (par * NQ + q)
                            act.wait_ge(s["hidden_ready"], n + 1)
                            act.wait_ge(s["h_ready"], n + (CREDIT["h_ready"] - 1))
                            ns.activation(act_out[q % 2][:, :], hidden[q % 2][:, 0:N],
                                          ACT.Relu if q >= KF else ACT.Gelu,
                                          bias=up_b[:, q // KF, q % KF:q % KF + 1]).then_inc(s["act_ready"], 1)

            @block.tensor
            def _(pe):
                nt = nc.tensor
                pe.sem_inc(s["down_ready"], CREDIT["down_ready"])

                def up(i, par, q):
                    e, f = q // KF, q % KF
                    n = i * (2 * NQ) + (par * NQ + q)
                    pe.wait_ge(s["act_ready"], n + (CREDIT["act_ready"] - 1))
                    if f == 0:
                        pe.wait_ge(s["w_lo_ready"], chunks_before(e, "up", 3))
                    parts = [(k, x, y) for k in range(KC) for x, y in ((0, 0), (0, 1), (1, 0))]
                    for m, (k, x, y) in enumerate(parts):
                        last = nt.matmul(hidden[q % 2][:, 0:N], up_w[e][x][:, k, f * P:(f + 1) * P],
                                         (t_hi, t_lo)[y][:, k, :], start=m == 0, stop=m == len(parts) - 1)
                    last.then_inc(s["hidden_ready"], 1)

                def down(i, par, q):
                    e, f = q // KF, q % KF
                    pe.wait_ge(s["h_ready"], i * (2 * NQ) + (par * NQ + q + 1 + CREDIT["h_ready"]))
                    if f % 2 == 0:
                        pe.wait_ge(s["w_lo_ready"], chunks_before(e, "down", f // 2))
                    if f == 0:
                        if e:
                            pe.wait_ge(s["result_free"], i * (2 * G) + (par * G + G))
                        else:
                            pe.wait_ge(s["final"], i * (2 * G) + (par * G + CREDIT["final"]))
                    for t in range(G):
                        for x, y in ((0, 0), (0, 1), (1, 0)):
                            last = nt.matmul(result[t][0:T, :], (h_hi, h_lo)[x][:, q % SLOTS, t * T:(t + 1) * T],
                                             down_w[e][y][:, f, :], start=f == 0 and (x, y) == (0, 0),
                                             stop=f == KF - 1 and x == 1)
                    last.then_inc(s["down_ready"], 1)

                with pe.Fori(0, TURNS) as i:
                    for par in range(2):
                        for t in range(G):
                            n = i * (2 * G) + (par * G + t)
                            pe.wait_ge(s["x2_ready"], n + 1)
                            pe.wait_ge(s["t_lo_ready"], n + (CREDIT["t_lo_ready"] - 1))
                            for k in range(KC):
                                last = nt.transpose(turn[t % 2][:, k * T:(k + 1) * T], x2[:, t, k * P:(k + 1) * P],
                                                    identf[0:T, 0:T])
                            last.then_inc(s["turned"], 1)
                        pe.wait_ge(s["t_lo_ready"], i * (2 * G) + (par * G + G + CREDIT["t_lo_ready"]))
                        for q in range(NQ):
                            up(i, par, q)
                            if q:
                                down(i, par, q - 1)
                        down(i, par, NQ - 1)


def kernel(**inputs):
    import numpy as np
    import concourse.bacc as bacc
    from concourse.bass_utils import run_bass_kernel_spmd

    x = {n.replace("L0_xattn_", "").replace("L0_ffn_", ""): np.asarray(v) for n, v in inputs.items()}
    kv = np.concatenate([x["Wk"], x["Wv"]], axis=1).reshape(CK, H, 2, HD)
    kv_b = np.concatenate([x["bk"], x["bv"]]).reshape(H, 2, HD)
    laid = {"x": x["x"], "ctxT": x["ctx_1024"].transpose(0, 2, 1), "g_xattn": x["g_xattn"], "g_ffn": x["g_ffn"],
            "Wq": x["Wq"], "bq": x["bq"], "Wk_heads": kv[:, :, 0].reshape(CK, C), "Wv_heads": kv[:, :, 1].reshape(CK, C),
            "bk_heads": kv_b[:, 0].reshape(C), "bv_heads": kv_b[:, 1].reshape(C), "Wg": x["Wg"]}
    for n in ("Wkv_dca", "bkv_dca", "qn_w", "qn_b", "kn_w", "kn_b", "kn_dca_w", "kn_dca_b", "Wo", "bo",
              "b0b", "b1b"):
        laid[n] = x[n]
    for n in ("b0a", "b1a"):
        laid[n] = x[n].reshape(KF, P).T
    for n in ("W0a", "W0b", "W1a", "W1b"):
        laid[n + "T"] = x[n].T

    nc = bacc.Bacc("TRN2", target_bir_lowering=False, num_devices=1)
    arrays, aps = {}, {}
    for n, v in laid.items():
        arrays[f"in_{n}"] = np.ascontiguousarray(v)
        aps[n] = nc.dram_tensor(f"in_{n}", v.shape, mybir.dt.from_np(v.dtype), kind="ExternalInput").ap()
    out = nc.dram_tensor("out", (B, T, C), F32, kind="ExternalOutput").ap()
    build(nc, aps, out)
    got = run_bass_kernel_spmd(nc, [arrays], core_ids=[0])
    return got.results[0]["out"]
```

```python
from contextlib import ExitStack

import concourse.bass as bass
from concourse import mybir

F32 = mybir.dt.float32
F32R = mybir.dt.float32r
F16 = mybir.dt.float16
ALU = mybir.AluOpType
ACT = mybir.ActivationFunctionType
AX = mybir.AxisListType

P = 128
B, T, C = 16, 112, 512
S, CK, DCA = 375, 256, 16
H, HD = 16, 32
M = S - DCA
SCALE = HD ** -0.5
EPS_HEAD, EPS_ROW = 1e-6, 1e-5
F = 1024
KC, KK, KF = C // P, CK // P, F // P
ROWS = [P, P, M - 2 * P]
KEYS = [P, P, S - 2 * P]
G = 4
NG = H // G
UNIT = 64.0
VW = 66

USES = ["ct3", "V0", "V1", "cT", "K2", "V2", "kt00", "kt01", "mt1",
        "ct0", "qt0", "qt1", "xT", "Wo", "kt10", "kt11", "K0", "mt2",
        "ct1", "kt20", "kt21", "Q", "mt3",
        "ct2", "K1", "mt0"]
OF_C = {"mt1", "mt2", "mt3", "ct0", "ct1", "ct2"}
OF_D = {"ct3", "cT", "Wo"}
OF_E = {"xT", "K0", "Q", "K1"}
BANKS = 3
VECTOR_OWN, SCALAR_OWN, POOL_OWN = 76, 10, 8
CHAIN = ["K0", "Q", "K1", "K2"]


class Step:

    def __init__(self, b, parity, parts, base):
        self.b, self.parity, self.base = b, parity, base
        self.a, self.c, self.d, self.e = (x in parts for x in "acde")
        self.uses = [u for u in USES if (self.c if u in OF_C else self.d if u in OF_D else
                                         self.e if u in OF_E else self.a)]

    @staticmethod
    def bank(use):
        return USES.index(use) % BANKS

    def before(self, use):
        bank = self.bank(use)
        return self.base[bank] + sum(self.bank(u) == bank for u in self.uses[:self.uses.index(use)])

    def after(self):
        return [self.base[k] + sum(self.bank(u) == k for u in self.uses) for k in range(BANKS)]


def at_least(eng, sem, value):
    if not (isinstance(value, int) and value <= 0):
        eng.wait_ge(sem, value)


PAIRS = (B - 4) // 2


def run_steps(eng, body, chain=None):
    st = Step(-2, 0, "e", [0] * BANKS)
    body(st)
    st = Step(-1, 1, "ae", st.after())
    body(st)
    st = Step(0, 0, "ace", st.after())
    body(st)
    per = [sum(Step.bank(u) == k for u in USES) for k in range(BANKS)]
    start = st.after()
    with eng.Fori(0, PAIRS) as i:
        if chain:
            chain.enter(i)
        for second in (0, 1):
            base = [i * (2 * per[k]) + (start[k] + second * per[k]) for k in range(BANKS)]
            body(Step(i * 2 + (1 + second), 1 - second, "acde", base))
        if chain:
            chain.leave(PAIRS)
    st = Step(B - 3, 1, "acde", [start[k] + 2 * PAIRS * per[k] for k in range(BANKS)])
    body(st)
    st = Step(B - 2, 0, "acd", st.after())
    body(st)
    st = Step(B - 1, 1, "cd", st.after())
    body(st)
    body(Step(B, 0, "d", st.after()))


class Chain:

    def __init__(self, eng, sem, per_turn=0):
        self.eng, self.sem, self.n, self.base, self.per_turn = eng, sem, 0, 0, per_turn

    def enter(self, i):
        self.before, self.n, self.base = self.n, 0, i * self.per_turn + self.n

    def leave(self, turns):
        assert self.n == self.per_turn, f"{self.n} own results a turn"
        self.n, self.base = self.before + turns * self.per_turn, 0

    def link(self, ins):
        ins.then_inc(self.sem, 1)
        self.n += 1
        self.eng.wait_ge(self.sem, self.base + self.n)


def one(n, size):
    return slice(n * size, (n + 1) * size) if isinstance(n, int) else bass.ds(n * size, size)


def transfers(n, par, more):
    return n * 8 + (16 * more - 8 * par)


def heads(ap):
    return ap.rearrange("p (h d) -> p h d", d=HD)


def build(nc, a, out):
    x1_dram = nc.dram_tensor("x1_scratch", (B * T, C + 2), F32, kind="Internal").ap()
    vd_dram = nc.dram_tensor("vd_scratch", (B * DCA, H * VW), F32, kind="Internal").ap()

    with ExitStack() as whole:
        def sem(name):
            return whole.enter_context(nc.semaphore(name))

        def sbuf(name, shape, dt=F32):
            return whole.enter_context(nc.sbuf_tensor(name, shape, dt))

        gates = sbuf("gates", [P, 2])
        identf = sbuf("identf", [P, P])
        identh = sbuf("identh", [P, P], F16)

        with ExitStack() as attention:
            def asb(name, shape, dt=F32):
                return attention.enter_context(nc.sbuf_tensor(name, shape, dt))

            w = {n: [asb(f"{n}_{part}", [P, k, C], F32R) for part in ("hi", "lo")]
                 for n, k in (("wq", KC), ("wk", KK), ("wv", KK), ("wo", KC))}
            rows = {n: asb(f"row_{n}", [P, C]) for n in ("bq", "bk", "bv", "bo")}
            norms = {n: asb(f"row_{n}", [P, HD]) for n in ("qn_w", "qn_b", "kn_w", "kn_b")}
            kdT = asb("kdT", [P, H, B * DCA], F16)
            prepare(nc, a, w, rows, norms, kdT, vd_dram, gates, identf, identh)
            attend(nc, a, w, rows, norms, kdT, vd_dram, gates, identf, identh, x1_dram)

        experts(nc, a, gates, identf, x1_dram, out)


def prepare(nc, a, w, rows, norms, kdT, vd_dram, gates, identf, identh):
    with ExitStack() as ctx:
        def sb(name, shape, dt=F32):
            return ctx.enter_context(nc.sbuf_tensor(name, shape, dt))

        def sem(name):
            return ctx.enter_context(nc.semaphore(name))

        def bank(name):
            return ctx.enter_context(nc.psum_tensor(name, [P, 512], F32))

        ND = B * DCA // P
        raw = {n: sb(f"raw_{n}", [P, k, C]) for n, k in
               (("wq", KC), ("wk", KK), ("wkd", KK), ("wv", KK), ("wvd", KK), ("wo", KC))}
        bkd, bvd = sb("bkd", [P, C]), sb("bvd", [P, C])
        vd = sb("vd", [P, ND, H, VW])
        kd_w, kd_b = sb("kd_w", [P, HD]), sb("kd_b", [P, HD])
        wd = {n: [sb(f"{n}_{part}", [P, KK, C], F32R) for part in ("hi", "lo")] for n in ("wkd", "wvd")}
        yd = sb("yd", [P, KK, B, DCA])
        yd_hi, yd_lo = sb("yd_hi", [P, KK, B * DCA], F32R), sb("yd_lo", [P, KK, B * DCA], F32R)
        mean = sb("mean", [P, KC * H])
        kb, sq, kn = sb("kb", [P, C]), sb("sq", [P, C]), sb("kn", [P, C])
        ve, lnv, y, r = (sb(n, [P, H]) for n in ("ve", "lnv", "y", "r"))
        stack = sb("stack", [P, H, P], F16)
        gate_raw = sb("gate_raw", [P, 2])
        pk, pv = bank("pk"), bank("pv")
        pt = [ctx.enter_context(nc.psum_tensor(f"pt{j}", [P, 8, P], F16)) for j in range(2)]

        loaded = {n: sem(f"loaded_{n}") for n in
                  ("wkd", "yd", "bkd", "wvd", "wk", "wq", "wv", "wo", "kd", "rows", "gates")}
        idents, tanhs = sem("idents_ready"), sem("tanhs_ready")
        own, own_act = sem("vector_own"), sem("scalar_own")
        hi_ready, lo_ready = sem("prep_hi_ready"), sem("prep_lo_ready")
        centered = sem("prep_centered")
        kd_ready, vd_ready, kd_used, vd_used = (sem(n) for n in ("kd_ready", "vd_ready", "kd_used", "vd_used"))
        added, squared, var_ready, y_ready = (sem(n) for n in ("pre_added", "pre_squared", "pre_var", "pre_y"))
        vd_stored = sem("vd_stored")
        stacked, turned, kept = sem("pre_stacked"), sem("pre_turned"), sem("pre_kept")

        order = ["wkd", "yd", "wvd", "wk", "wq", "wv", "wo"]
        source = {n: raw[n][:, :, :] for n in raw}
        source["yd"] = yd[:, :, :, :].rearrange("p k b d -> p k (b d)")
        target = {**{n: w[n] for n in w}, **{n: wd[n] for n in wd}, "yd": (yd_hi, yd_lo)}

        with nc.Block() as block:
            @block.sync
            def _(sp):
                def load(name, dst, src):
                    sp.dma_start(dst, src).then_inc(loaded[name], 16)

                def wide(name):
                    return a[name].rearrange("(k p) n -> p k n", p=P)

                def spread(ap):
                    return ap.unsqueeze(0).to_broadcast([P, ap.shape[0]])

                load("wkd", raw["wkd"][:, :, :], wide("Wkv_dca")[:, :, 0:C])
                for k in range(KK):
                    load("yd", yd[:, k, :, :], a["ctxT"][:, k * P:(k + 1) * P, M:S].rearrange("b p d -> p b d"))
                load("bkd", bkd[:, :], spread(a["bkv_dca"][0:C]))
                load("wvd", raw["wvd"][:, :, :], wide("Wkv_dca")[:, :, C:2 * C])
                load("kd", kd_w[:, :], spread(a["kn_dca_w"]))
                load("kd", kd_b[:, :], spread(a["kn_dca_b"]))
                load("wk", raw["wk"][:, :, :], wide("Wk_heads"))
                load("wq", raw["wq"][:, :, :], wide("Wq"))
                load("wv", raw["wv"][:, :, :], wide("Wv_heads"))
                load("wo", raw["wo"][:, :, :], wide("Wo"))
                load("gates", gate_raw[:, 0:1], spread(a["g_xattn"]))
                load("gates", gate_raw[:, 1:2], spread(a["g_ffn"]))
                load("rows", rows["bq"][:, :], spread(a["bq"]))
                load("rows", rows["bk"][:, :], spread(a["bk_heads"]))
                load("rows", rows["bv"][:, :], spread(a["bv_heads"]))
                load("rows", bvd[:, :], spread(a["bkv_dca"][C:2 * C]))
                load("rows", rows["bo"][:, :], spread(a["bo"]))
                for n in norms:
                    load("rows", norms[n][:, :], spread(a[n]))
                sp.wait_ge(vd_used, ND)
                sp.dma_start(vd_dram.rearrange("(t p) v -> p t v", p=P),
                             vd[:, :, :, :].rearrange("p t h v -> p t (h v)")).then_inc(vd_stored, 16)
                sp.wait_ge(vd_stored, 16)

            @block.gpsimd
            def _(pool):
                nc.gpsimd.memset(identf[:, :], 0.0).then_inc(idents, 1)
                pool.wait_ge(idents, 1)
                nc.gpsimd.affine_select(out=identf[:, :], in_=identf[:, :], compare_op=ALU.not_equal, fill=1.0,
                                        base=0, pattern=[[-1, P]], channel_multiplier=1).then_inc(idents, 1)
                pool.wait_ge(idents, 2)
                nc.gpsimd.tensor_copy(identh[:, :], identf[:, :]).then_inc(idents, 1)

            @block.vector
            def _(dve):
                chain = Chain(dve, own)
                link = chain.link

                def center(ap, k):
                    m = mean[:, 0:k * H]
                    link(nc.vector.tensor_reduce(m, ap, AX.X, ALU.add))
                    link(nc.vector.tensor_scalar(m, m, -1.0 / HD, None, ALU.mult))
                    return nc.vector.tensor_tensor(ap, ap, m.unsqueeze(2).to_broadcast([P, k * H, HD]), ALU.add)

                link(nc.vector.memset(stack[:, :, 3 * HD:], 0.0))
                link(nc.vector.memset(stack[:, :, 3 * HD + 1:3 * HD + 4:2], UNIT))
                link(nc.vector.memset(vd[:, :, :, 0:HD + 1], 0.0))
                link(nc.vector.memset(vd[:, :, :, VW - 1:VW], 1.0))
                for n, name in enumerate(order):
                    dve.wait_ge(loaded[name], 32 if name == "yd" else 16)
                    if name in ("wkd", "wk", "wq"):
                        k = KC if name == "wq" else KK
                        center(raw[name][:, :, :].rearrange("p k (h d) -> p (k h) d", d=HD), k).then_inc(centered, 1)
                    dve.wait_ge(hi_ready, n + 1)
                    nc.vector.tensor_tensor(target[name][1][:, :, :], source[name], target[name][0][:, :, :],
                                            ALU.subtract).then_inc(lo_ready, 1)
                dve.wait_ge(loaded["bkd"], 16)
                dve.wait_ge(loaded["kd"], 32)
                dve.wait_ge(loaded["rows"], 16 * (5 + len(norms)))
                link(center(heads(bkd[:, :]), 1))
                link(center(heads(rows["bq"][:, :]), 1))
                link(center(heads(rows["bk"][:, :]), 1))
                link(nc.vector.tensor_tensor(rows["bv"][:, :], rows["bv"][:, :], bvd[:, :], ALU.add))
                dve.wait_ge(tanhs, 1)
                link(nc.vector.tensor_scalar(rows["bo"][:, :], rows["bo"][:, :], gates[:, 0:1], None, ALU.mult))
                for t in range(ND):
                    dve.wait_ge(kd_ready, t + 1)
                    nc.vector.tensor_tensor(kb[:, :], pk[:, :], bkd[:, :], ALU.add).then_inc(added, 1)
                    dve.wait_ge(vd_ready, t + 1)
                    nc.vector.tensor_copy(vd[:, t, :, HD + 1:2 * HD + 1], heads(pv[:, :])).then_inc(vd_used, 1)
                    dve.wait_ge(squared, t + 1)
                    link(nc.vector.tensor_reduce(r[:, :], heads(sq[:, :]), AX.X, ALU.add))
                    nc.vector.tensor_scalar(ve[:, :], r[:, :], 1.0 / HD, EPS_HEAD, ALU.mult, ALU.add)\
                        .then_inc(var_ready, 1)
                    dve.wait_ge(y_ready, t + 1)
                    link(nc.vector.tensor_tensor(r[:, :], y[:, :], y[:, :], ALU.mult))
                    link(nc.vector.tensor_tensor(r[:, :], r[:, :], ve[:, :], ALU.mult))
                    link(nc.vector.tensor_scalar(r[:, :], r[:, :], -0.5, 1.5, ALU.mult, ALU.add))
                    link(nc.vector.tensor_tensor(r[:, :], r[:, :], y[:, :], ALU.mult))
                    dve.wait_ge(added, t + 1)
                    link(nc.vector.tensor_tensor(heads(kn[:, :]), heads(kb[:, :]),
                                                 r[:, :].unsqueeze(2).to_broadcast([P, H, HD]), ALU.mult))
                    link(nc.vector.tensor_tensor(heads(kn[:, :]), heads(kn[:, :]),
                                                 kd_w[:, :].unsqueeze(1).to_broadcast([P, H, HD]), ALU.mult))
                    link(nc.vector.tensor_tensor(heads(kn[:, :]), heads(kn[:, :]),
                                                 kd_b[:, :].unsqueeze(1).to_broadcast([P, H, HD]), ALU.add))
                    if t:
                        dve.wait_ge(turned, 2 * t)
                    link(nc.vector.tensor_copy(stack[:, :, 0:HD], heads(kn[:, :])))
                    link(nc.vector.tensor_copy(stack[:, :, HD:2 * HD], stack[:, :, 0:HD]))
                    nc.vector.tensor_tensor(stack[:, :, 2 * HD:3 * HD], heads(kn[:, :]), stack[:, :, 0:HD],
                                            ALU.subtract).then_inc(stacked, 1)
                    for j in range(2):
                        dve.wait_ge(turned, 2 * t + j + 1)
                        nc.vector.tensor_copy(kdT[:, 8 * j:8 * j + 8, t * P:(t + 1) * P], pt[j][:, :, :])\
                            .then_inc(kept, 1)

            @block.scalar
            def _(act):
                def hi(n):
                    name = order[n]
                    if name in ("wkd", "wk", "wq"):
                        act.wait_ge(centered, 1 + ("wkd", "wk", "wq").index(name))
                    else:
                        act.wait_ge(loaded[name], 32 if name == "yd" else 16)
                    nc.scalar.activation(target[name][0][:, :, :], source[name], ACT.Copy).then_inc(hi_ready, 1)

                act.wait_ge(loaded["wkd"], 16)
                for n in range(len(order)):
                    hi(n)
                act.wait_ge(loaded["gates"], 32)
                nc.scalar.activation(gates[:, :], gate_raw[:, :], ACT.Tanh).then_inc(tanhs, 1)
                act.preload_act_table_set("natural_log_exp_and_others")
                for t in range(ND):
                    act.wait_ge(added, t + 1)
                    if t:
                        act.wait_ge(var_ready, t)
                    nc.scalar.activation(sq[:, :], kb[:, :], ACT.Square).then_inc(squared, 1)
                    act.wait_ge(var_ready, t + 1)
                    nc.scalar.activation(lnv[:, :], ve[:, :], ACT.Ln).then_inc(own_act, 1)
                    act.wait_ge(own_act, t + 1)
                    nc.scalar.activation(y[:, :], lnv[:, :], ACT.Exp, scale=-0.5).then_inc(y_ready, 1)

            @block.tensor
            def _(pe):
                def product(dst, name, t):
                    pairs = ((yd_hi, 0), (yd_hi, 1), (yd_lo, 0))
                    for n, (k, (y_part, part)) in enumerate((k, p) for k in range(KK) for p in pairs):
                        last = nc.tensor.matmul(dst[:, :], y_part[:, k, t * P:(t + 1) * P],
                                                wd[name][part][:, k, :], start=n == 0, stop=n == 3 * KK - 1)
                    return last

                pe.wait_ge(lo_ready, 3)
                pe.wait_ge(hi_ready, 3)
                pe.wait_ge(idents, 3)
                for t in range(ND):
                    if t:
                        pe.wait_ge(added, t)
                        pe.wait_ge(vd_used, t)
                    product(pk, "wkd", t).then_inc(kd_ready, 1)
                    product(pv, "wvd", t).then_inc(vd_ready, 1)
                    pe.wait_ge(stacked, t + 1)
                    for j in range(2):
                        if t:
                            pe.wait_ge(kept, 2 * (t - 1) + j + 1)
                        for h in range(8):
                            last = nc.tensor.transpose(pt[j][:, h, :], stack[:, 8 * j + h, :], identh[:, :])
                        last.then_inc(turned, 1)


def attend(nc, a, w, rows, norms, kdT, vd_dram, gates, identf, identh, x1_dram):
    with ExitStack() as ctx:
        def sb(name, shape, dt=F32):
            return ctx.enter_context(nc.sbuf_tensor(name, shape, dt))

        def sem(name):
            return ctx.enter_context(nc.semaphore(name))

        def bank(name):
            return ctx.enter_context(nc.psum_tensor(name, [P, 512], F32))

        x_raw = [sb(f"x_raw{i}", [T, C]) for i in range(2)]
        xb = [sb(f"xb{i}", [T, C]) for i in range(2)]
        y_raw = [sb(f"y_raw{i}", [P, KK, S]) for i in range(2)]
        y_hi, y_lo = sb("y_hi", [P, KK, S], F32R), sb("y_lo", [P, KK, S], F32R)
        xn = sb("xn", [T, C])
        x_hi, x_lo = sb("x_hi", [P, KC, T], F32R), sb("x_lo", [P, KC, T], F32R)
        bn, mv, xve, xln, xy, xr = (sb(n, [T, k]) for n, k in
                                    (("bn", 6), ("mv", 2), ("xve", 1), ("xln", 1), ("xy", 1), ("xr", 1)))
        kb, sq, kn, ka = (sb(f"t_{n}", [P, C]) for n in ("kb", "sq", "kn", "ka"))
        ve, lnv, y, r = (sb(f"t_{n}", [P, H]) for n in ("ve", "lnv", "y", "r"))
        stacks = {n: sb(f"stack_{n}", [P, H, P], F16) for n in CHAIN}
        kT = [sb(f"kT{i}", [P, H, S + 1], F16) for i in range(2)]
        qT = [sb(f"qT{i}", [P, H, T], F16) for i in range(2)]
        v_main = [sb(f"v_main{i}", [P, 2, H, VW]) for i in range(2)]
        v_last = [sb(f"v_last{i}", [P, H, VW]) for i in range(2)]
        nmax = sb("nmax", [T, G, 2])
        shift = sb("shift", [T, H, HD], F16)
        p = [[sb(f"p{i}{k}", [P, G * T]) for k in range(3)] for i in range(2)]
        ctxT_raw = sb("ctxT_raw", [VW, H, T])
        inv = sb("inv", [T, G, 2])
        cm, cd = sb("cm", [T, G, HD]), sb("cd", [T, G, HD])
        ctxn = sb("ctxn", [T, H, HD])
        c_hi, c_lo = sb("c_hi", [P, KC, T], F32R), sb("c_lo", [P, KC, T], F32R)
        x1 = [sb(f"x1_{i}", [T, C + 2]) for i in range(2)]

        work = [bank(f"work{i}") for i in range(BANKS)]
        top = [bank(f"top{i}") for i in range(2)]
        score = [bank(f"score{i}") for i in range(2)]
        pv = bank("pv_acc")

        w_ready = [sem(f"work_ready{i}") for i in range(BANKS)]
        w_free = [sem(f"work_free{i}") for i in range(BANKS)]
        x_in, y_in, vd_in, x1_out = ([sem(f"{n}{i}") for i in range(2)] for n in ("x_in", "y_in", "vd_in", "x1_out"))
        consts = sem("consts_ready")
        own_v, own_a, own_p = sem("vector_own2"), sem("scalar_own2"), sem("pool_own2")
        names = ["x_var", "x_rsqrt", "x_normed", "x_hi_ready", "y_hi_ready", "y_lo_ready", "xb_ready", "squared",
                 "var_ready", "rsqrt_ready", "normed", "affine_ready", "high_ready", "copied_ready", "low_ready",
                 "kd_copied", "top_ready", "top_free", "shift_ready", "score_ready", "exp_ready", "pv_ready",
                 "ctx_copied", "ctx_ready", "c_hi_ready", "x1_ready"]
        s = {n: sem(n) for n in names}

        def wait_free(pe, st, use):
            at_least(pe, w_free[st.bank(use)], st.before(use))

        def wait_ready(eng, st, use):
            eng.wait_ge(w_ready[st.bank(use)], st.before(use) + 1)

        def wait_read(pe, st, use):
            pe.wait_ge(w_free[st.bank(use)], st.before(use) + 1)

        def size_of(tile):
            return T if tile == "Q" else ROWS[int(tile[1])]

        def place(batch, tile):
            return 4 * batch + CHAIN.index(tile)

        def halves(use, st, n):
            return work[st.bank(use)][:, :].bitcast(F16).rearrange("p (h k) -> p h k", h=8)[:, :, 0:n]

        def rstd(nv, link, out_, v, guess):
            link(nv.scalar_tensor_tensor(out=out_, in0=v, scalar=-0.5, in1=guess, op0=ALU.mult, op1=ALU.mult))
            link(nv.tensor_tensor(out_, out_, guess, ALU.mult))
            link(nv.scalar_tensor_tensor(out=out_, in0=out_, scalar=1.5, in1=guess, op0=ALU.add, op1=ALU.mult))

        with nc.Block() as block:
            @block.sync
            def _(sp):
                def load(n, par):
                    at_least(sp, s["x_normed"], n - 1)
                    at_least(sp, s["xb_ready"], n - 1)
                    sp.dma_start(x_raw[par][:, :], a["x"].rearrange("b t c -> (b t) c")[one(n, T), :])\
                        .then_inc(x_in[par], 16)
                    at_least(sp, s["y_lo_ready"], n - 1)
                    sp.dma_start(y_raw[par][:, :, :], a["ctxT"].rearrange("b (k p) m -> p (b k) m", p=P)
                                 [:, one(n, KK), :]).then_inc(y_in[par], 16)

                def dca_values(n, par):
                    at_least(sp, s["pv_ready"], NG * (n - 1))
                    sp.dma_start(v_last[par][ROWS[2]:KEYS[2], :, :],
                                 vd_dram[one(n, DCA), :].rearrange("k (h v) -> k h v", h=H)).then_inc(vd_in[par], 16)

                def store(n, par):
                    sp.wait_ge(s["x1_ready"], n + 1)
                    sp.dma_start(x1_dram[one(n, T), :], x1[par][:, :]).then_inc(x1_out[par], 16)

                for par in range(2):
                    sp.sem_inc(x1_out[par], 1)
                sp.wait_ge(consts, 1)
                for n in range(2):
                    load(n, n)
                    dca_values(n, n)
                load(2, 0)
                load(3, 1)
                dca_values(2, 0)
                with sp.Fori(0, PAIRS) as i:
                    for par in range(2):
                        b = i * 2 + (1 + par)
                        store(i * 2 + par, par)
                        load(b + 3, par)
                        dca_values(b + 2, 1 - par)
                store(B - 4, 0)
                dca_values(B - 1, 1)
                for n in (B - 3, B - 2, B - 1):
                    store(n, n % 2)
                for par in range(2):
                    sp.wait_ge(x1_out[par], 16 * (B // 2) + 1)

            @block.vector
            def _(dve):
                chain = Chain(dve, own_v, VECTOR_OWN)
                link = chain.link
                nv = nc.vector

                for n in CHAIN:
                    link(nv.memset(stacks[n][:, :, 3 * HD:], 0.0))
                    if n != "Q":
                        link(nv.memset(stacks[n][:, :, 3 * HD:3 * HD + 3:2], UNIT))
                link(nv.memset(shift[:, :, :], 0.0))
                for i in range(2):
                    link(nv.memset(v_main[i][:, :, :, HD + 1:], 0.0))
                    link(nv.memset(v_main[i][:, :, :, HD:HD + 1], 1.0))
                    link(nv.memset(v_last[i][:, :, HD + 1:], 0.0))
                    last = nv.memset(v_last[i][:, :, HD:HD + 1], 1.0)
                    if i == 0:
                        link(last)
                last.then_inc(consts, 1)

                def row_stats(n, par):
                    dve.wait_ge(x_in[par], transfers(n, par, 1))
                    link(nv.bn_stats(bn[:, :], x_raw[par][:, :]))
                    nv.memset(xve[:, :], 0.0)
                    link(nv.bn_aggr(mv[:, :], bn[:, :]))
                    nv.tensor_scalar(xve[:, :], mv[:, 1:2], EPS_ROW, None, ALU.add).then_inc(s["x_var"], 1)

                def row_norm(n, par):
                    dve.wait_ge(s["x_rsqrt"], n + 1)
                    rstd(nv, link, xr[:, :], xve[:, :], xy[:, :])
                    nv.tensor_scalar(xn[:, :], x_raw[par][:, :], mv[:, 0:1], xr[:, :], ALU.subtract, ALU.mult)\
                        .then_inc(s["x_normed"], 1)

                def add_bias(st, batch, tile):
                    m = size_of(tile)
                    at_least(dve, s["normed"], place(batch, tile))
                    wait_ready(dve, st, tile)
                    nv.tensor_tensor(kb[0:m, :], work[st.bank(tile)][0:m, :],
                                     rows["bq" if tile == "Q" else "bk"][0:m, :], ALU.add)\
                        .then_inc(w_free[st.bank(tile)], 1)

                def head_var(batch, tile):
                    m, n = size_of(tile), place(batch, tile)
                    dve.wait_ge(s["squared"], n + 1)
                    link(nv.tensor_reduce(r[0:m, :], heads(sq[0:m, :]), AX.X, ALU.add))
                    nv.tensor_scalar(ve[0:m, :], r[0:m, :], 1.0 / HD, EPS_HEAD, ALU.mult, ALU.add)\
                        .then_inc(s["var_ready"], 1)

                def head_norm(batch, tile):
                    m, n = size_of(tile), place(batch, tile)
                    dve.wait_ge(s["rsqrt_ready"], n + 1)
                    rstd(nv, link, r[0:m, :], ve[0:m, :], y[0:m, :])
                    at_least(dve, s["affine_ready"], n)
                    nv.tensor_tensor(heads(kn[0:m, :]), heads(kb[0:m, :]),
                                     r[0:m, :].unsqueeze(2).to_broadcast([m, H, HD]), ALU.mult)\
                        .then_inc(s["normed"], 1)

                def high(batch, tile):
                    m, n = size_of(tile), place(batch, tile)
                    stack, second = stacks[tile], 2 * HD if tile == "Q" else HD
                    dve.wait_ge(s["affine_ready"], n + 1)
                    nv.tensor_copy(stack[0:m, :, 0:HD], heads(ka[0:m, :])).then_inc(s["high_ready"], 1)
                    dve.wait_ge(s["high_ready"], n + 1)
                    nv.tensor_copy(stack[0:m, :, second:second + HD], stack[0:m, :, 0:HD])\
                        .then_inc(s["copied_ready"], 1)

                def maxima(b, g, lo, up):
                    if lo == 0:
                        at_least(dve, s["shift_ready"], b * NG + g)
                    for h in range(lo, up):
                        n = b * H + (G * g + h)
                        dve.wait_ge(s["top_ready"], n + 1)
                        nv.tensor_reduce(nmax[:, h, 0:1], top[h % 2][0:T, 0:M], AX.X, ALU.max, negate=True)
                        nv.tensor_reduce(nmax[:, h, 1:2], top[h % 2][0:T, M:S], AX.X, ALU.max, negate=True)\
                            .then_inc(s["top_free"], 1)

                def shifts(b, g):
                    dve.wait_ge(s["top_free"], b * H + G * (g + 1))
                    hs = shift[:, G * g:G * g + G, :]
                    link(nv.tensor_scalar(hs[:, :, 0:2], nmax[:, :, :], 1.0 / UNIT, None, ALU.mult))
                    nv.scalar_tensor_tensor(out=hs[:, :, 2:4], in0=nmax[:, :, :], scalar=1.0 / UNIT,
                                            in1=hs[:, :, 0:2], op0=ALU.mult, op1=ALU.subtract)\
                        .then_inc(s["shift_ready"], 1)

                def context(st, use, g):
                    wait_ready(dve, st, use)
                    ct = work[st.bank(use)][0:T, 0:G * VW].rearrange("t (h v) -> t h v", v=VW)
                    wide = [T, G, HD]
                    link(nv.reciprocal(inv[:, :, :], ct[:, :, HD:VW:HD + 1]))
                    link(nv.tensor_tensor(cm[:, :, :], ct[:, :, 0:HD], inv[:, :, 0:1].to_broadcast(wide), ALU.mult))
                    nv.tensor_tensor(cd[:, :, :], ct[:, :, HD + 1:VW - 1], inv[:, :, 1:2].to_broadcast(wide),
                                     ALU.mult).then_inc(w_free[st.bank(use)], 1)
                    link(nv.tensor_tensor(cm[:, :, :], cm[:, :, :], heads(rows["bv"][0:T, :])[:, G * g:G * g + G, :],
                                          ALU.add))
                    dve.wait_ge(w_free[st.bank(use)], st.before(use) + 1)
                    nv.tensor_tensor(ctxn[:, G * g:G * g + G, :], cm[:, :, :], cd[:, :, :], ALU.add)\
                        .then_inc(s["ctx_ready"], 1)

                def low_rows(st, use, lo, hi, hi_sem, value):
                    wait_ready(dve, st, use)
                    dve.wait_ge(hi_sem, value)
                    nv.tensor_tensor(lo[:, :, :].rearrange("p k t -> p (k t)"), work[st.bank(use)][:, 0:KC * T],
                                     hi[:, :, :].rearrange("p k t -> p (k t)"), ALU.subtract)\
                        .then_inc(w_free[st.bank(use)], 1)

                def body(st):
                    n, npar = st.b + 1, 1 - st.parity
                    m = st.b + 2
                    if st.a:
                        high(n, "Q")
                    if st.d:
                        context(st, "ct3", NG - 1)
                    if st.c:
                        maxima(st.b, 1, 2, 4)
                    if st.a:
                        head_var(n, "K1")
                    if st.c:
                        shifts(st.b, 1)
                    if st.e:
                        row_stats(m, st.parity)
                    if st.d:
                        low_rows(st, "cT", c_lo, c_hi, s["c_hi_ready"], st.b)
                    if st.a:
                        head_norm(n, "K1")
                        add_bias(st, n, "K2")
                    if st.e:
                        row_norm(m, st.parity)
                    if st.c:
                        maxima(st.b, 2, 0, 2)
                    if st.a:
                        high(n, "K1")
                    if st.c:
                        maxima(st.b, 2, 2, 4)
                    if st.a:
                        head_var(n, "K2")
                    if st.c:
                        shifts(st.b, 2)
                        context(st, "ct0", 0)
                    if st.e:
                        low_rows(st, "xT", x_lo, x_hi, s["x_hi_ready"], m + 1)
                    if st.a:
                        head_norm(n, "K2")
                    if st.d:
                        d = st.b - 1
                        wait_ready(dve, st, "Wo")
                        dve.wait_ge(x1_out[npar], transfers(d, npar, 0) + 1)
                        dve.wait_ge(s["xb_ready"], st.b)
                        nv.scalar_tensor_tensor(out=x1[npar][:, 0:C], in0=work[st.bank("Wo")][0:T, :],
                                                scalar=gates[0:T, 0:1], in1=xb[npar][:, :],
                                                op0=ALU.mult, op1=ALU.add).then_inc(w_free[st.bank("Wo")], 1)
                        dve.wait_ge(w_free[st.bank("Wo")], st.before("Wo") + 1)
                        link(nv.bn_stats(bn[:, :], x1[npar][:, 0:C]))
                        nv.memset(xve[:, :], 0.0)
                        nv.bn_aggr(x1[npar][:, C:C + 2], bn[:, :]).then_inc(s["x1_ready"], 1)
                        dve.wait_ge(s["x1_ready"], st.b)
                    if st.e:
                        add_bias(st, m, "K0")
                    if st.c:
                        maxima(st.b, 3, 0, 2)
                    if st.a:
                        high(n, "K2")
                    if st.c:
                        maxima(st.b, 3, 2, 4)
                    if st.e:
                        head_var(m, "K0")
                    if st.c:
                        shifts(st.b, 3)
                        context(st, "ct1", 1)
                    if st.e:
                        head_norm(m, "K0")
                        add_bias(st, m, "Q")
                    if st.a:
                        maxima(n, 0, 0, 2)
                    if st.e:
                        high(m, "K0")
                    if st.a:
                        maxima(n, 0, 2, 4)
                    if st.e:
                        head_var(m, "Q")
                    if st.a:
                        shifts(n, 0)
                    if st.c:
                        context(st, "ct2", 2)
                    if st.e:
                        head_norm(m, "Q")
                        add_bias(st, m, "K1")
                    if st.a:
                        maxima(n, 1, 0, 2)

                run_steps(dve, body, chain)

            @block.scalar
            def _(act):
                chain = Chain(act, own_a, SCALAR_OWN)
                link = chain.link
                ns = nc.scalar
                act.preload_act_table_set("natural_log_exp_and_others")

                def square(st, batch, tile):
                    m, n = size_of(tile), place(batch, tile)
                    wait_read(act, st, tile)
                    at_least(act, s["var_ready"], n)
                    ns.activation(sq[0:m, :], kb[0:m, :], ACT.Square).then_inc(s["squared"], 1)

                def guess(batch, tile):
                    m, n = size_of(tile), place(batch, tile)
                    act.wait_ge(s["var_ready"], n + 1)
                    link(ns.activation(lnv[0:m, :], ve[0:m, :], ACT.Ln))
                    ns.activation(y[0:m, :], lnv[0:m, :], ACT.Exp, scale=-0.5).then_inc(s["rsqrt_ready"], 1)

                def row_guess(n):
                    act.wait_ge(s["x_var"], n + 1)
                    link(ns.activation(xln[:, :], xve[:, :], ACT.Ln))
                    ns.activation(xy[:, :], xln[:, :], ACT.Exp, scale=-0.5).then_inc(s["x_rsqrt"], 1)

                def context_high(n, par):
                    act.wait_ge(y_in[par], transfers(n, par, 1))
                    ns.activation(y_hi[:, :, :], y_raw[par][:, :, :], ACT.Copy).then_inc(s["y_hi_ready"], 1)

                def copy_pv(b, g):
                    act.wait_ge(s["pv_ready"], b * NG + (g + 1))
                    ns.activation(ctxT_raw[:, G * g:G * g + G, :],
                                  pv[0:VW, 0:G * T].rearrange("v (h t) -> v h t", h=G), ACT.Copy)\
                        .then_inc(s["ctx_copied"], 1)

                def shift_rows(st, use, g):
                    par = st.parity if g else 1 - st.parity
                    wait_ready(act, st, use)
                    ns.activation(qT[par][3 * HD:P, G * g:G * g + G, :],
                                  work[st.bank(use)][3 * HD:P, :].bitcast(F16)[:, 0:G * T]
                                  .rearrange("p (h t) -> p h t", h=G), ACT.Copy).then_inc(w_free[st.bank(use)], 1)

                def exps(b, g):
                    at_least(act, s["pv_ready"], b * NG + (g - 1))
                    for k in range(3):
                        n = b * (3 * NG) + (3 * g + k)
                        act.wait_ge(s["score_ready"], n + 1)
                        ns.activation(p[g % 2][k][0:KEYS[k], :], score[(3 * g + k) % 2][0:KEYS[k], 0:G * T],
                                      ACT.Exp, scale=SCALE).then_inc(s["exp_ready"], 1)

                def values(st, tile):
                    k, par = int(tile[1]), 1 - st.parity
                    wait_ready(act, st, tile)
                    dst = v_last[par][0:ROWS[2], :, 0:HD] if k == 2 else v_main[par][:, k, :, 0:HD]
                    ns.activation(dst, heads(work[st.bank(tile)][0:ROWS[k], :]), ACT.Copy)\
                        .then_inc(w_free[st.bank(tile)], 1)

                def key_copy(st, tile):
                    k, j = int(tile[2]), int(tile[3])
                    wait_ready(act, st, tile)
                    ns.activation(kT[1 - st.parity][:, 8 * j:8 * j + 8, k * P:k * P + ROWS[k]],
                                  halves(tile, st, ROWS[k]), ACT.Copy).then_inc(w_free[st.bank(tile)], 1)

                def query_copy(st, j):
                    use = f"qt{j}"
                    wait_ready(act, st, use)
                    ns.activation(qT[1 - st.parity][:, 8 * j:8 * j + 8, :], halves(use, st, T), ACT.Copy)\
                        .then_inc(w_free[st.bank(use)], 1)

                def high_rows(st, use, hi, done):
                    wait_ready(act, st, use)
                    ns.activation(hi[:, :, :].rearrange("p k t -> p (k t)"), work[st.bank(use)][:, 0:KC * T],
                                  ACT.Copy).then_inc(done, 1)

                def body(st):
                    n, npar, m = st.b + 1, 1 - st.parity, st.b + 2
                    if st.d:
                        copy_pv(st.b - 1, NG - 1)
                    if st.c:
                        exps(st.b, 0)
                    if st.a:
                        values(st, "V0")
                        guess(n, "K1")
                        values(st, "V1")
                    if st.d:
                        high_rows(st, "cT", c_hi, s["c_hi_ready"])
                    if st.a:
                        values(st, "V2")
                    if st.e:
                        context_high(m, st.parity)
                        row_guess(m)
                    if st.a:
                        key_copy(st, "kt00")
                        key_copy(st, "kt01")
                        square(st, n, "K2")
                    if st.c:
                        shift_rows(st, "mt1", 1)
                    if st.c:
                        copy_pv(st.b, 0)
                        exps(st.b, 1)
                    if st.a:
                        query_copy(st, 0)
                        query_copy(st, 1)
                        guess(n, "K2")
                    if st.e:
                        high_rows(st, "xT", x_hi, s["x_hi_ready"])
                    if st.a:
                        key_copy(st, "kt10")
                        key_copy(st, "kt11")
                    if st.e:
                        square(st, m, "K0")
                    if st.c:
                        shift_rows(st, "mt2", 2)
                    if st.c:
                        copy_pv(st.b, 1)
                        exps(st.b, 2)
                    if st.e:
                        guess(m, "K0")
                    if st.a:
                        key_copy(st, "kt20")
                        key_copy(st, "kt21")
                    if st.e:
                        square(st, m, "Q")
                    if st.c:
                        shift_rows(st, "mt3", 3)
                    if st.c:
                        copy_pv(st.b, 2)
                        exps(st.b, 3)
                    if st.e:
                        guess(m, "Q")
                        square(st, m, "K1")
                    if st.a:
                        shift_rows(st, "mt0", 0)

                run_steps(act, body, chain)

            @block.gpsimd
            def _(pool):
                chain = Chain(pool, own_p, POOL_OWN)
                link = chain.link
                ng = nc.gpsimd

                def affine(batch, tile):
                    m, n = size_of(tile), place(batch, tile)
                    kind = "qn" if tile == "Q" else "kn"
                    pool.wait_ge(s["normed"], n + 1)
                    at_least(pool, s["high_ready"], n)
                    link(ng.tensor_tensor(heads(ka[0:m, :]), heads(kn[0:m, :]),
                                          norms[kind + "_w"][0:m, :].unsqueeze(1).to_broadcast([m, H, HD]), ALU.mult))
                    ng.tensor_tensor(heads(ka[0:m, :]), heads(ka[0:m, :]),
                                     norms[kind + "_b"][0:m, :].unsqueeze(1).to_broadcast([m, H, HD]), ALU.add)\
                        .then_inc(s["affine_ready"], 1)

                def low(batch, tile):
                    m, n = size_of(tile), place(batch, tile)
                    pool.wait_ge(s["high_ready"], n + 1)
                    at = HD if tile == "Q" else 2 * HD
                    ng.tensor_tensor(stacks[tile][0:m, :, at:at + HD], heads(ka[0:m, :]),
                                     stacks[tile][0:m, :, 0:HD], ALU.subtract).then_inc(s["low_ready"], 1)
                    pool.wait_ge(s["low_ready"], n + 1)

                def context_low(n, par):
                    pool.wait_ge(s["y_hi_ready"], n + 1)
                    ng.tensor_tensor(y_lo[:, :, :], y_raw[par][:, :, :], y_hi[:, :, :], ALU.subtract)\
                        .then_inc(s["y_lo_ready"], 1)

                def body(st):
                    n, npar, m = st.b + 1, 1 - st.parity, st.b + 2
                    if st.a:
                        low(n, "Q")
                        affine(n, "K1")
                    if st.a:
                        low(n, "K1")
                    if st.e:
                        context_low(m, st.parity)
                    if st.a:
                        ng.tensor_copy(kT[npar][:, :, M:S],
                                       kdT[:, :, one(n, DCA)]).then_inc(s["kd_copied"], 1)
                        affine(n, "K2")
                    if st.a:
                        low(n, "K2")
                    if st.e:
                        affine(m, "K0")
                    if st.a:
                        at_least(pool, s["x1_ready"], st.b)
                        pool.wait_ge(x_in[npar], transfers(n, npar, 1))
                        ng.tensor_tensor(xb[npar][:, :], x_raw[npar][:, :], rows["bo"][0:T, :], ALU.add)\
                            .then_inc(s["xb_ready"], 1)
                    if st.e:
                        low(m, "K0")
                        affine(m, "Q")

                run_steps(pool, body, chain)

            @block.tensor
            def _(pe):
                nt = nc.tensor

                def three(dst, m, left, right, depth, cols):
                    parts = [(k, i, j) for k in range(depth) for i, j in ((0, 0), (0, 1), (1, 0))]
                    for n, (k, i, j) in enumerate(parts):
                        last = nt.matmul(dst, left[i][:, k, cols[0]:cols[0] + m], right[j][:, k, :],
                                         start=n == 0, stop=n == len(parts) - 1)
                    return last

                def turn_rows(st, use, src):
                    wait_free(pe, st, use)
                    for k in range(KC):
                        last = nt.transpose(work[st.bank(use)][:, k * T:(k + 1) * T], src[:, k * P:(k + 1) * P],
                                            identf[0:T, 0:T])
                    last.then_inc(w_ready[st.bank(use)], 1)

                def project(st, tile):
                    k = int(tile[1])
                    wait_free(pe, st, tile)
                    three(work[st.bank(tile)][0:ROWS[k], :], ROWS[k], (y_hi, y_lo), w["w" + tile[0].lower()], KK,
                          (k * P,)).then_inc(w_ready[st.bank(tile)], 1)

                def turn_stack(st, use, batch, tile, j):
                    m, n = size_of(tile), place(batch, tile)
                    pe.wait_ge(s["copied_ready"], n + 1)
                    pe.wait_ge(s["low_ready"], n + 1)
                    wait_free(pe, st, use)
                    dst = halves(use, st, m)
                    for h in range(8):
                        last = nt.transpose(dst[:, h, :], stacks[tile][0:m, 8 * j + h, :], identh[0:m, 0:m])
                    last.then_inc(w_ready[st.bank(use)], 1)

                def tops(b, par, g, lo, up):
                    for h in range(lo, up):
                        n = b * H + (G * g + h)
                        at_least(pe, s["top_free"], n - 1)
                        nt.matmul(top[h % 2][0:T, 0:S], qT[par][:, G * g + h, :], kT[par][:, G * g + h, 0:S],
                                  start=True, stop=True).then_inc(s["top_ready"], 1)

                def turn_shift(st, use, batch, g):
                    pe.wait_ge(s["shift_ready"], batch * NG + (g + 1))
                    wait_free(pe, st, use)
                    dst = work[st.bank(use)][3 * HD:P, :].bitcast(F16)
                    for h in range(G):
                        last = nt.transpose(dst[:, h * T:(h + 1) * T], shift[:, G * g + h, :], identh[0:T, 0:T])
                    last.then_inc(w_ready[st.bank(use)], 1)

                def scores(st, g, tiles):
                    for k in tiles:
                        n = st.b * (3 * NG) + (3 * g + k)
                        at_least(pe, s["exp_ready"], n - 1)
                        for h in range(G):
                            last = nt.matmul(score[(3 * g + k) % 2][0:KEYS[k], h * T:(h + 1) * T],
                                             kT[st.parity][:, G * g + h, k * P:k * P + KEYS[k]],
                                             qT[st.parity][:, G * g + h, :], start=True, stop=True)
                        last.then_inc(s["score_ready"], 1)

                def weigh(st, g):
                    pe.wait_ge(s["exp_ready"], st.b * (3 * NG) + 3 * (g + 1))
                    at_least(pe, s["ctx_copied"], st.b * NG + g)
                    if g == 0:
                        pe.wait_ge(vd_in[st.parity], transfers(st.b, st.parity, 1))
                    for h in range(G):
                        cols = slice(h * T, (h + 1) * T)
                        nt.matmul(pv[0:VW, cols], v_last[st.parity][0:KEYS[2], G * g + h, :],
                                  p[g % 2][2][0:KEYS[2], cols], start=True, stop=False)
                        for k in range(2):
                            last = nt.matmul(pv[0:VW, cols], v_main[st.parity][:, k, G * g + h, :],
                                             p[g % 2][k][:, cols], start=False, stop=k == 1)
                    last.then_inc(s["pv_ready"], 1)

                def turn_context(st, use, b, g):
                    pe.wait_ge(s["ctx_copied"], b * NG + (g + 1))
                    wait_free(pe, st, use)
                    for h in range(G):
                        last = nt.transpose(work[st.bank(use)][0:T, h * VW:(h + 1) * VW],
                                            ctxT_raw[:, G * g + h, :], identf[0:VW, 0:VW])
                    last.then_inc(w_ready[st.bank(use)], 1)

                def body(st):
                    n, npar, m = st.b + 1, 1 - st.parity, st.b + 2
                    if st.c:
                        scores(st, 0, (0, 1))
                        tops(st.b, st.parity, 1, 2, 4)
                    if st.d:
                        turn_context(st, "ct3", st.b - 1, NG - 1)
                    if st.c:
                        scores(st, 0, (2,))
                    if st.a:
                        project(st, "V0")
                        project(st, "V1")
                    if st.d:
                        pe.wait_ge(s["ctx_ready"], st.b * NG)
                        turn_rows(st, "cT", ctxn[:, :, :].rearrange("t h d -> t (h d)"))
                    if st.a:
                        project(st, "K2")
                        project(st, "V2")
                        turn_stack(st, "kt00", n, "K0", 0)
                        turn_stack(st, "kt01", n, "K0", 1)
                    if st.c:
                        tops(st.b, st.parity, 2, 0, 2)
                        turn_shift(st, "mt1", st.b, 1)
                        weigh(st, 0)
                        wait_read(pe, st, "mt1")
                    if st.c:
                        scores(st, 1, (0, 1))
                        tops(st.b, st.parity, 2, 2, 4)
                        turn_context(st, "ct0", st.b, 0)
                        scores(st, 1, (2,))
                    if st.a:
                        turn_stack(st, "qt0", n, "Q", 0)
                        turn_stack(st, "qt1", n, "Q", 1)
                    if st.e:
                        pe.wait_ge(s["x_normed"], m + 1)
                        turn_rows(st, "xT", xn)
                    if st.d:
                        wait_free(pe, st, "Wo")
                        pe.wait_ge(s["c_hi_ready"], st.b)
                        wait_read(pe, st, "cT")
                        three(work[st.bank("Wo")][0:T, :], T, (c_hi, c_lo), w["wo"], KC, (0,))\
                            .then_inc(w_ready[st.bank("Wo")], 1)
                    if st.a:
                        turn_stack(st, "kt10", n, "K1", 0)
                        turn_stack(st, "kt11", n, "K1", 1)
                    if st.e:
                        pe.wait_ge(s["y_hi_ready"], m + 1)
                        pe.wait_ge(s["y_lo_ready"], m + 1)
                        project(st, "K0")
                    if st.c:
                        tops(st.b, st.parity, 3, 0, 2)
                        turn_shift(st, "mt2", st.b, 2)
                        weigh(st, 1)
                        wait_read(pe, st, "mt2")
                    if st.c:
                        scores(st, 2, (0, 1))
                        tops(st.b, st.parity, 3, 2, 4)
                        turn_context(st, "ct1", st.b, 1)
                        scores(st, 2, (2,))
                    if st.a:
                        turn_stack(st, "kt20", n, "K2", 0)
                        turn_stack(st, "kt21", n, "K2", 1)
                    if st.e:
                        assert st.bank("Q") == st.bank("xT")
                        wait_free(pe, st, "Q")
                        pe.wait_ge(s["x_hi_ready"], m + 1)
                        three(work[st.bank("Q")][0:T, :], T, (x_hi, x_lo), w["wq"], KC, (0,))\
                            .then_inc(w_ready[st.bank("Q")], 1)
                    if st.a:
                        pe.wait_ge(s["kd_copied"], n + 1)
                        for use in ("kt11", "kt20", "kt21"):
                            wait_read(pe, st, use)
                        tops(n, npar, 0, 0, 2)
                    if st.c:
                        turn_shift(st, "mt3", st.b, 3)
                        weigh(st, 2)
                        wait_read(pe, st, "mt3")
                    if st.c:
                        scores(st, 3, (0, 1))
                    if st.a:
                        tops(n, npar, 0, 2, 4)
                    if st.c:
                        turn_context(st, "ct2", st.b, 2)
                        scores(st, 3, (2,))
                    if st.e:
                        project(st, "K1")
                    if st.a:
                        tops(n, npar, 1, 0, 2)
                        turn_shift(st, "mt0", n, 0)
                    if st.c:
                        weigh(st, 3)
                    if st.a:
                        wait_read(pe, st, "mt0")

                run_steps(pe, body, None)


def experts(nc, a, gates, identf, x1_dram, out):
    N = G * T
    GROUPS = B // G
    SLOTS = 4
    NQ = 2 * KF
    RAWS = 3
    with ExitStack() as ctx:
        def sb(name, shape, dt=F32):
            return ctx.enter_context(nc.sbuf_tensor(name, shape, dt))

        def sem(name):
            return ctx.enter_context(nc.semaphore(name))

        def bank(name):
            return ctx.enter_context(nc.psum_tensor(name, [P, 512], F32))

        up_w = [[sb(f"up{e}_{part}", [P, KC, F], F32R) for part in ("hi", "lo")] for e in range(2)]
        down_w = [[sb(f"down{e}_{part}", [P, KF, C], F32R) for part in ("hi", "lo")] for e in range(2)]
        raw = [sb(f"w_raw{i}", [P, 1024]) for i in range(RAWS)]
        up_b = sb("up_b", [P, 2, KF])
        b0, b1, wg = sb("b0", [T, C]), sb("b1", [T, C]), sb("wg", [T, C])
        stats, rs = sb("stats", [T, B, 2]), sb("rs", [T, B])
        rs_ve, rs_ln, rs_y = sb("rs_ve", [T, B]), sb("rs_ln", [T, B]), sb("rs_y", [T, B])
        x1 = sb("x1_group", [T, G, C + 2])
        x3 = sb("x3_group", [T, G, C])
        x2 = sb("x2", [T, G, C])
        junk = sb("junk", [T, C])
        score = sb("route", [T, G])
        scale = sb("scale", [T, 2, G])
        scale1 = sb("scale1", [T, G])
        rg = sb("rg", [T, G])
        t_hi, t_lo = sb("t_hi", [P, KC, N], F32R), sb("t_lo", [P, KC, N], F32R)
        act_out = [sb(f"act_out{i}", [P, N]) for i in range(2)]
        h_hi, h_lo = sb("h_hi", [P, SLOTS, N], F32R), sb("h_lo", [P, SLOTS, N], F32R)
        turn = [bank(f"turn{i}") for i in range(2)]
        hidden = [bank(f"hidden{i}") for i in range(2)]
        result = [bank(f"result{i}") for i in range(G)]

        names = ["w_hi_ready", "w_lo_ready", "pool_hi_ready", "pool_lo_ready", "rows_in", "stats_in", "x1_in", "out_done",
                 "rs_var", "rs_guess", "own_v3", "own_a3", "x2_ready", "biased", "based", "turned",
                 "t_hi_ready", "t_lo_ready", "hidden_ready", "act_ready", "h_ready", "down_ready", "result_free",
                 "final"]
        s = {n: sem(n) for n in names}

        CREDIT = {"h_ready": 2, "act_ready": 2, "t_lo_ready": 2, "down_ready": SLOTS, "final": 1}

        chunks = [(e, kind, k) for e in range(2) for kind in ("up", "down") for k in range(4)]
        w_in = [sem(f"w_in{n}") for n in range(len(chunks))]

        def chunk(which, part):
            e, kind, k = which
            if kind == "up":
                return up_w[e][part][:, k, :]
            return down_w[e][part][:, 2 * k:2 * k + 2, :].rearrange("p k n -> p (k n)")

        def wait_split(pe, e, kind, k):
            pe.wait_ge(s["pool_lo_ready" if e else "w_lo_ready"], chunks.index((0, kind, k)) + 1)

        HALF = len(chunks) // 2

        def load_chunk(eng, n):
            e, kind, k = chunks[n]
            if n >= RAWS:
                before = n - RAWS
                eng.wait_ge(s["w_lo_ready" if before < HALF else "pool_lo_ready"], before % HALF + 1)
            src = a[f"W{e}aT"][k * P:(k + 1) * P, :] if kind == "up" else \
                a[f"W{e}bT"][2 * k * P:2 * (k + 1) * P, :].rearrange("(j p) n -> p j n", p=P)
            dst = raw[n % RAWS][:, :] if kind == "up" else raw[n % RAWS][:, :].rearrange("p (j n) -> p j n", j=2)
            eng.dma_start(dst, src).then_inc(w_in[n], 16)

        with nc.Block() as block:
            @block.sync
            def _(sp):
                def load_group(g):
                    sp.dma_start(x1[:, :, :], x1_dram.rearrange("(b t) c -> t b c", t=T)[:, one(g, G), :])\
                        .then_inc(s["x1_in"], 16)

                def store_group(g):
                    for t in range(G):
                        sp.wait_ge(s["final"], g * G + (t + 1 + CREDIT["final"]))
                        sp.dma_start(out.rearrange("b t c -> (b t) c")[one(g * G + t, T), :], x3[:, t, :])\
                            .then_inc(s["out_done"], 16)

                sp.dma_start(stats[:, :, :], x1_dram.rearrange("(b t) c -> t b c", t=T)[:, :, C:C + 2])\
                    .then_inc(s["stats_in"], 16)
                sp.sem_inc(s["out_done"], 1)
                load_group(0)
                for e in range(2):
                    sp.dma_start(up_b[:, e, :], a[f"b{e}a"]).then_inc(s["rows_in"], 16)
                sp.dma_start(b0[:, :], a["b0b"].unsqueeze(0).to_broadcast([T, C])).then_inc(s["rows_in"], 16)
                sp.dma_start(b1[:, :], a["b1b"].unsqueeze(0).to_broadcast([T, C])).then_inc(s["rows_in"], 16)
                sp.dma_start(wg[:, :], a["Wg"][0:1, :].to_broadcast([T, C])).then_inc(s["rows_in"], 16)
                sp.dma_start(junk[:, :], a["Wg"][1:2, :].to_broadcast([T, C])).then_inc(s["rows_in"], 16)
                with sp.Fori(0, GROUPS - 1) as i:
                    sp.wait_ge(s["result_free"], i * G + G)
                    load_group(i + 1)
                    store_group(i)
                store_group(GROUPS - 1)
                sp.wait_ge(s["out_done"], GROUPS * 16 * G + 1)

            @block.vector
            def _(dve):
                nv = nc.vector
                chain = Chain(dve, s["own_v3"], 24)
                link = chain.link
                for n in ("h_ready", "t_lo_ready", "final"):
                    dve.sem_inc(s[n], CREDIT[n])

                def norm_batch(g, t):
                    if t == 0:
                        link(nv.tensor_copy(rg[:, :], rs[:, one(g, G)]))
                        dve.wait_ge(s["x1_in"], g * 16 + 16)
                    row = x1[:, t, :]
                    nv.tensor_scalar(x2[:, t, :], row[:, 0:C], row[:, C:C + 1], rg[:, t:t + 1],
                                     ALU.subtract, ALU.mult).then_inc(s["x2_ready"], 1)
                    dve.wait_ge(s["x2_ready"], g * G + (t + 1))
                    link(nv.tensor_tensor_reduce(out=junk[:, :], in0=x2[:, t, :], in1=wg[:, :], scale=1.0,
                                                 scalar=0.0, op0=ALU.mult, op1=ALU.add,
                                                 accum_out=score[:, t:t + 1]))
                    nv.tensor_tensor(row[:, 0:C], row[:, 0:C], b1[:, :], ALU.add).then_inc(s["biased"], 1)

                def add_biases(g):
                    link(nv.tensor_scalar(scale[:, 0, :], score[:, :], 0.0, gates[0:T, 1:2], ALU.is_ge, ALU.mult))
                    link(nv.tensor_scalar(scale[:, 1, :], scale[:, 0, :], -1.0, gates[0:T, 1:2],
                                          ALU.mult, ALU.add))
                    dve.wait_ge(s["biased"], g * G + G)
                    for t in range(G):
                        nv.scalar_tensor_tensor(out=x1[:, t, 0:C], in0=b0[:, :], scalar=scale[:, 0, t:t + 1],
                                                in1=x1[:, t, 0:C], op0=ALU.mult, op1=ALU.add)\
                            .then_inc(s["based"], 1)

                def split_weights(n):
                    dve.wait_ge(s["w_hi_ready"], n + 1)
                    nv.tensor_tensor(chunk(chunks[n], 1), raw[n % RAWS][:, :], chunk(chunks[n], 0), ALU.subtract)\
                        .then_inc(s["w_lo_ready"], 1)

                dve.wait_ge(s["stats_in"], 16)
                nv.tensor_scalar(rs_ve[:, :], stats[:, :, 1], EPS_ROW, None, ALU.add).then_inc(s["rs_var"], 1)
                dve.wait_ge(s["rs_guess"], 1)
                link(nv.tensor_tensor(rs[:, :], rs_y[:, :], rs_y[:, :], ALU.mult))
                link(nv.tensor_tensor(rs[:, :], rs[:, :], rs_ve[:, :], ALU.mult))
                link(nv.tensor_scalar(rs[:, :], rs[:, :], -0.5, 1.5, ALU.mult, ALU.add))
                link(nv.tensor_tensor(rs[:, :], rs[:, :], rs_y[:, :], ALU.mult))
                dve.wait_ge(s["rows_in"], 16 * 6)
                link(nv.tensor_tensor(wg[:, :], wg[:, :], junk[:, :], ALU.subtract))
                link(nv.tensor_tensor(b0[:, :], b0[:, :], b1[:, :], ALU.subtract))
                link(nv.tensor_scalar(b1[:, :], b1[:, :], gates[0:T, 1:2], None, ALU.mult))
                def low_tokens(g):
                    for t in range(G):
                        n = g * G + t
                        dve.wait_ge(s["t_hi_ready"], n + 1)
                        nv.tensor_tensor(t_lo[:, :, t * T:(t + 1) * T],
                                         turn[t % 2][:, 0:KC * T].rearrange("p (k t) -> p k t", k=KC),
                                         t_hi[:, :, t * T:(t + 1) * T], ALU.subtract).then_inc(s["t_lo_ready"], 1)

                def split_hidden(g, q):
                    n = g * NQ + q
                    dve.wait_ge(s["act_ready"], n + (CREDIT["act_ready"] + 1))
                    dve.wait_ge(s["down_ready"], n + 1)
                    link(nv.tensor_copy(h_hi[:, q % SLOTS, :], act_out[q % 2][:, :]))
                    nv.tensor_tensor(h_lo[:, q % SLOTS, :], act_out[q % 2][:, :], h_hi[:, q % SLOTS, :],
                                     ALU.subtract).then_inc(s["h_ready"], 1)

                def gather(g, e):
                    dve.wait_ge(s["down_ready"], g * NQ + ((e + 1) * KF + CREDIT["down_ready"]))
                    if e == 0:
                        dve.wait_ge(s["based"], g * G + G)
                        dve.wait_ge(s["out_done"], g * (16 * G) + 1)
                    else:
                        dve.wait_ge(s["result_free"], g * G + G)
                    for t in range(G):
                        nv.scalar_tensor_tensor(out=x3[:, t, :], in0=result[t][0:T, :],
                                                scalar=scale1[:, t:t + 1] if e else scale[:, 0, t:t + 1],
                                                in1=x3[:, t, :] if e else x1[:, t, 0:C],
                                                op0=ALU.mult, op1=ALU.add)\
                            .then_inc(s["final" if e else "result_free"], 1)
                    if e == 0:
                        link(nv.tensor_copy(scale1[:, :], scale[:, 1, :]))

                def group(g, more):
                    for q in range(NQ):
                        split_hidden(g, q)
                        if q == KF:
                            gather(g, 0)
                        if more and KF + 2 <= q < KF + 2 + G:
                            norm_batch(g + 1, q - KF - 2)
                        if more and q == KF + 2 + G:
                            add_biases(g + 1)
                    if more:
                        low_tokens(g + 1)
                    gather(g, 1)

                for t in range(G):
                    norm_batch(0, t)
                for n in range(HALF):
                    split_weights(n)
                low_tokens(0)
                add_biases(0)
                with dve.Fori(0, GROUPS - 1) as i:
                    chain.enter(i)
                    group(i, True)
                    chain.leave(GROUPS - 1)
                group(GROUPS - 1, False)

            @block.gpsimd
            def _(pool):
                for n in range(HALF, HALF + RAWS):
                    load_chunk(pool, n)
                for n in range(HALF, 2 * HALF):
                    hi, lo = (chunk(chunks[n], part) for part in range(2))
                    pool.wait_ge(w_in[n], 16)
                    nc.gpsimd.tensor_copy(hi, raw[n % RAWS][:, :]).then_inc(s["pool_hi_ready"], 1)
                    pool.wait_ge(s["pool_hi_ready"], n - HALF + 1)
                    nc.gpsimd.tensor_tensor(lo, raw[n % RAWS][:, :], hi, ALU.subtract).then_inc(s["pool_lo_ready"], 1)
                    if n + RAWS < 2 * HALF:
                        load_chunk(pool, n + RAWS)

            @block.scalar
            def _(act):
                ns = nc.scalar
                act.sem_inc(s["act_ready"], CREDIT["act_ready"])
                for n in range(RAWS):
                    load_chunk(act, n)
                act.preload_act_table_set("natural_log_exp_and_others")
                act.wait_ge(s["rs_var"], 1)
                ns.activation(rs_ln[:, :], rs_ve[:, :], ACT.Ln).then_inc(s["own_a3"], 1)
                act.wait_ge(s["own_a3"], 1)
                ns.activation(rs_y[:, :], rs_ln[:, :], ACT.Exp, scale=-0.5).then_inc(s["rs_guess"], 1)
                act.preload_act_table_set("gelu_and_others")
                for n in range(HALF):
                    act.wait_ge(w_in[n], 16)
                    ns.activation(chunk(chunks[n], 0), raw[n % RAWS][:, :], ACT.Copy).then_inc(s["w_hi_ready"], 1)
                    if n and n + RAWS - 1 < HALF:
                        load_chunk(act, n + RAWS - 1)
                act.wait_ge(s["rows_in"], 16 * 6)

                def high_tokens(g):
                    for t in range(G):
                        act.wait_ge(s["turned"], g * G + (t + 1))
                        ns.activation(t_hi[:, :, t * T:(t + 1) * T],
                                      turn[t % 2][:, 0:KC * T].rearrange("p (k t) -> p k t", k=KC),
                                      ACT.Copy).then_inc(s["t_hi_ready"], 1)

                def group(g, more):
                    for q in range(NQ):
                        n = g * NQ + q
                        act.wait_ge(s["hidden_ready"], n + 1)
                        act.wait_ge(s["h_ready"], n + (CREDIT["h_ready"] - 1))
                        ns.activation(act_out[q % 2][:, :], hidden[q % 2][:, 0:N],
                                      ACT.Relu if q >= KF else ACT.Gelu,
                                      bias=up_b[:, q // KF, q % KF:q % KF + 1]).then_inc(s["act_ready"], 1)
                    if more:
                        high_tokens(g + 1)

                high_tokens(0)
                with act.Fori(0, GROUPS - 1) as i:
                    group(i, True)
                group(GROUPS - 1, False)

            @block.tensor
            def _(pe):
                nt = nc.tensor
                pe.sem_inc(s["down_ready"], CREDIT["down_ready"])

                def up(g, q):
                    e, f = q // KF, q % KF
                    n = g * NQ + q
                    pe.wait_ge(s["act_ready"], n + (CREDIT["act_ready"] - 1))
                    if f == 0:
                        wait_split(pe, e, "up", 3)
                    parts = [(k, x, y) for k in range(KC) for x, y in ((0, 0), (0, 1), (1, 0))]
                    for m, (k, x, y) in enumerate(parts):
                        last = nt.matmul(hidden[q % 2][:, 0:N], up_w[e][x][:, k, f * P:(f + 1) * P],
                                         (t_hi, t_lo)[y][:, k, :], start=m == 0, stop=m == len(parts) - 1)
                    last.then_inc(s["hidden_ready"], 1)

                def down(g, q):
                    e, f = q // KF, q % KF
                    pe.wait_ge(s["h_ready"], g * NQ + (q + 1 + CREDIT["h_ready"]))
                    if f % 2 == 0:
                        wait_split(pe, e, "down", f // 2)
                    if f == 0:
                        if e:
                            pe.wait_ge(s["result_free"], g * G + G)
                        else:
                            pe.wait_ge(s["final"], g * G + CREDIT["final"])
                    for t in range(G):
                        for x, y in ((0, 0), (0, 1), (1, 0)):
                            last = nt.matmul(result[t][0:T, :], (h_hi, h_lo)[x][:, q % SLOTS, t * T:(t + 1) * T],
                                             down_w[e][y][:, f, :], start=f == 0 and (x, y) == (0, 0),
                                             stop=f == KF - 1 and x == 1)
                    last.then_inc(s["down_ready"], 1)

                def turn_batch(g, t):
                    n = g * G + t
                    pe.wait_ge(s["x2_ready"], n + 1)
                    pe.wait_ge(s["t_lo_ready"], n + (CREDIT["t_lo_ready"] - 1))
                    for k in range(KC):
                        last = nt.transpose(turn[t % 2][:, k * T:(k + 1) * T], x2[:, t, k * P:(k + 1) * P],
                                            identf[0:T, 0:T])
                    last.then_inc(s["turned"], 1)

                def group(g, more):
                    pe.wait_ge(s["t_lo_ready"], g * G + (G + CREDIT["t_lo_ready"]))
                    for q in range(NQ):
                        up(g, q)
                        if more and q == NQ - 1:
                            turn_batch(g + 1, 0)
                            turn_batch(g + 1, 1)
                        if q:
                            down(g, q - 1)
                    if more:
                        turn_batch(g + 1, 2)
                        turn_batch(g + 1, 3)
                    down(g, NQ - 1)

                for t in range(G):
                    turn_batch(0, t)
                with pe.Fori(0, GROUPS - 1) as i:
                    group(i, True)
                group(GROUPS - 1, False)


def kernel(**inputs):
    import numpy as np
    import concourse.bacc as bacc
    from concourse.bass_utils import run_bass_kernel_spmd

    x = {n.replace("L0_xattn_", "").replace("L0_ffn_", ""): np.asarray(v) for n, v in inputs.items()}
    kv = np.concatenate([x["Wk"], x["Wv"]], axis=1).reshape(CK, H, 2, HD)
    kv_b = np.concatenate([x["bk"], x["bv"]]).reshape(H, 2, HD)
    laid = {"x": x["x"], "ctxT": x["ctx_1024"].transpose(0, 2, 1), "g_xattn": x["g_xattn"], "g_ffn": x["g_ffn"],
            "Wq": x["Wq"], "bq": x["bq"], "Wk_heads": kv[:, :, 0].reshape(CK, C), "Wv_heads": kv[:, :, 1].reshape(CK, C),
            "bk_heads": kv_b[:, 0].reshape(C), "bv_heads": kv_b[:, 1].reshape(C), "Wg": x["Wg"]}
    for n in ("Wkv_dca", "bkv_dca", "qn_w", "qn_b", "kn_w", "kn_b", "kn_dca_w", "kn_dca_b", "Wo", "bo",
              "b0b", "b1b"):
        laid[n] = x[n]
    for n in ("b0a", "b1a"):
        laid[n] = x[n].reshape(KF, P).T
    for n in ("W0a", "W0b", "W1a", "W1b"):
        laid[n + "T"] = x[n].T

    nc = bacc.Bacc("TRN2", target_bir_lowering=False, num_devices=1)
    arrays, aps = {}, {}
    for n, v in laid.items():
        arrays[f"in_{n}"] = np.ascontiguousarray(v)
        aps[n] = nc.dram_tensor(f"in_{n}", v.shape, mybir.dt.from_np(v.dtype), kind="ExternalInput").ap()
    out = nc.dram_tensor("out", (B, T, C), F32, kind="ExternalOutput").ap()
    build(nc, aps, out)
    got = run_bass_kernel_spmd(nc, [arrays], core_ids=[0])
    return got.results[0]["out"]
```

```python
from contextlib import ExitStack

import concourse.bass as bass
from concourse import mybir

F32 = mybir.dt.float32
F32R = mybir.dt.float32r
F16 = mybir.dt.float16
ALU = mybir.AluOpType
ACT = mybir.ActivationFunctionType
AX = mybir.AxisListType

P = 128
B, T, C = 16, 112, 512
S, CK, DCA = 375, 256, 16
H, HD = 16, 32
M = S - DCA
SCALE = HD ** -0.5
EPS_HEAD, EPS_ROW = 1e-6, 1e-5
F = 1024
KC, KK, KF = C // P, CK // P, F // P
ROWS = [P, P, M - 2 * P]
KEYS = [P, P, S - 2 * P]
G = 4
NG = H // G
UNIT = 64.0
VW = 66

USES = ["ct3", "V0", "V1", "cT", "K2", "V2", "kt00", "kt01", "mt1",
        "ct0", "qt0", "qt1", "Wo", "xT", "kt10", "kt11", "K0", "mt2",
        "ct1", "Q", "kt20", "kt21", "mt3",
        "ct2", "K1", "mt0"]
OF_C = {"mt1", "mt2", "mt3", "ct0", "ct1", "ct2"}
OF_D = {"ct3", "cT", "Wo"}
OF_E = {"xT", "K0", "Q", "K1"}
BANKS = 3
VECTOR_OWN, SCALAR_OWN, POOL_OWN = 68, 10, 8
CHAIN = ["K0", "Q", "K1", "K2"]


class Step:

    def __init__(self, b, parity, parts, base):
        self.b, self.parity, self.base = b, parity, base
        self.a, self.c, self.d, self.e = (x in parts for x in "acde")
        self.uses = [u for u in USES if (self.c if u in OF_C else self.d if u in OF_D else
                                         self.e if u in OF_E else self.a)]

    @staticmethod
    def bank(use):
        return USES.index(use) % BANKS

    def before(self, use):
        bank = self.bank(use)
        return self.base[bank] + sum(self.bank(u) == bank for u in self.uses[:self.uses.index(use)])

    def after(self):
        return [self.base[k] + sum(self.bank(u) == k for u in self.uses) for k in range(BANKS)]


def at_least(eng, sem, value):
    if not (isinstance(value, int) and value <= 0):
        eng.wait_ge(sem, value)


PAIRS = (B - 4) // 2
RAWS = 3


def run_steps(eng, body, chain=None):
    st = Step(-2, 0, "e", [0] * BANKS)
    body(st)
    st = Step(-1, 1, "ae", st.after())
    body(st)
    st = Step(0, 0, "ace", st.after())
    body(st)
    per = [sum(Step.bank(u) == k for u in USES) for k in range(BANKS)]
    start = st.after()
    with eng.Fori(0, PAIRS) as i:
        if chain:
            chain.enter(i)
        for second in (0, 1):
            base = [i * (2 * per[k]) + (start[k] + second * per[k]) for k in range(BANKS)]
            body(Step(i * 2 + (1 + second), 1 - second, "acde", base))
        if chain:
            chain.leave(PAIRS)
    st = Step(B - 3, 1, "acde", [start[k] + 2 * PAIRS * per[k] for k in range(BANKS)])
    body(st)
    st = Step(B - 2, 0, "acd", st.after())
    body(st)
    st = Step(B - 1, 1, "cd", st.after())
    body(st)
    body(Step(B, 0, "d", st.after()))


class Chain:

    def __init__(self, eng, sem, per_turn=0):
        self.eng, self.sem, self.n, self.base, self.per_turn = eng, sem, 0, 0, per_turn

    def enter(self, i):
        self.before, self.n, self.base = self.n, 0, i * self.per_turn + self.n

    def leave(self, turns):
        assert self.n == self.per_turn, f"{self.n} own results a turn"
        self.n, self.base = self.before + turns * self.per_turn, 0

    def link(self, ins):
        ins.then_inc(self.sem, 1)
        self.n += 1
        self.eng.wait_ge(self.sem, self.base + self.n)


def one(n, size):
    return slice(n * size, (n + 1) * size) if isinstance(n, int) else bass.ds(n * size, size)


def transfers(n, par, more):
    return n * 8 + (16 * more - 8 * par)


def heads(ap):
    return ap.rearrange("p (h d) -> p h d", d=HD)


def build(nc, a, out):
    x1_dram = nc.dram_tensor("x1_scratch", (B * T, C + 2), F32, kind="Internal").ap()
    vd_dram = nc.dram_tensor("vd_scratch", (B * DCA, H * VW), F32, kind="Internal").ap()

    with ExitStack() as whole:
        def sem(name):
            return whole.enter_context(nc.semaphore(name))

        def sbuf(name, shape, dt=F32):
            return whole.enter_context(nc.sbuf_tensor(name, shape, dt))

        gates = sbuf("gates", [P, 2])
        identf = sbuf("identf", [P, P])
        identh = sbuf("identh", [P, P], F16)
        late = {n: sbuf(n, [T, C]) for n in ("wg", "b0", "b1")}
        raw = [sbuf(f"w_raw{i}", [P, F]) for i in range(RAWS)]
        first_in = [sem(f"w_in{n}") for n in range(RAWS)]

        with ExitStack() as attention:
            def asb(name, shape, dt=F32):
                return attention.enter_context(nc.sbuf_tensor(name, shape, dt))

            w = {n: [asb(f"{n}_{part}", [P, k, C], F32R) for part in ("hi", "lo")]
                 for n, k in (("wq", KC), ("wk", KK), ("wv", KK), ("wo", KC))}
            rows = {n: asb(f"row_{n}", [P, C]) for n in ("bq", "bk", "bv", "bo")}
            norms = {n: asb(f"row_{n}", [P, HD]) for n in ("qn_w", "qn_b", "kn_w", "kn_b")}
            kdT = asb("kdT", [P, H, B * DCA], F16)
            prepare(nc, a, w, rows, norms, late, kdT, vd_dram, gates, identf, identh)
            attend(nc, a, w, rows, norms, kdT, vd_dram, gates, identf, identh, x1_dram, raw, first_in)

        experts(nc, a, gates, late, identf, x1_dram, raw, first_in, out)


def prepare(nc, a, w, rows, norms, late, kdT, vd_dram, gates, identf, identh):
    with ExitStack() as ctx:
        def sb(name, shape, dt=F32):
            return ctx.enter_context(nc.sbuf_tensor(name, shape, dt))

        def sem(name):
            return ctx.enter_context(nc.semaphore(name))

        def bank(name):
            return ctx.enter_context(nc.psum_tensor(name, [P, 512], F32))

        ND = B * DCA // P
        raw = {n: sb(f"raw_{n}", [P, k, C]) for n, k in
               (("wq", KC), ("wk", KK), ("wkd", KK), ("wv", KK), ("wvd", KK), ("wo", KC))}
        bkd, bvd = sb("bkd", [P, C]), sb("bvd", [P, C])
        vd = sb("vd", [P, ND, H, VW])
        kd_w, kd_b = sb("kd_w", [P, HD]), sb("kd_b", [P, HD])
        wd = {n: [sb(f"{n}_{part}", [P, KK, C], F32R) for part in ("hi", "lo")] for n in ("wkd", "wvd")}
        yd = sb("yd", [P, KK, B, DCA])
        yd_hi, yd_lo = sb("yd_hi", [P, KK, B * DCA], F32R), sb("yd_lo", [P, KK, B * DCA], F32R)
        mean = sb("mean", [P, KC * H])
        kb, sq, kn = sb("kb", [P, C]), sb("sq", [P, C]), sb("kn", [P, C])
        ve, lnv, y, r = (sb(n, [P, H]) for n in ("ve", "lnv", "y", "r"))
        stack = sb("stack", [P, H, P], F16)
        gate_raw, wg1 = sb("gate_raw", [P, 2]), sb("wg1", [T, C])
        pk, pv = bank("pk"), bank("pv")
        pt = [ctx.enter_context(nc.psum_tensor(f"pt{j}", [P, 8, P], F16)) for j in range(2)]

        loaded = {n: sem(f"loaded_{n}") for n in
                  ("wkd", "yd", "bkd", "wvd", "wk", "wq", "wv", "wo", "kd", "rows", "gates", "late")}
        idents, tanhs = sem("idents_ready"), sem("tanhs_ready")
        own, own_act = sem("vector_own"), sem("scalar_own")
        hi_ready, lo_ready = sem("prep_hi_ready"), sem("prep_lo_ready")
        centered = sem("prep_centered")
        kd_ready, vd_ready, kd_used, vd_used = (sem(n) for n in ("kd_ready", "vd_ready", "kd_used", "vd_used"))
        added, squared, var_ready, y_ready = (sem(n) for n in ("pre_added", "pre_squared", "pre_var", "pre_y"))
        vd_stored, pooled, gaps_ready = sem("vd_stored"), sem("pool_prepared"), sem("gaps_ready")
        stacked, turned, kept = sem("pre_stacked"), sem("pre_turned"), sem("pre_kept")

        order = ["wkd", "yd", "wvd", "wk", "wv", "wo", "wq"]
        source = {n: raw[n][:, :, :] for n in raw}
        source["yd"] = yd[:, :, :, :].rearrange("p k b d -> p k (b d)")
        target = {**{n: w[n] for n in w}, **{n: wd[n] for n in wd}, "yd": (yd_hi, yd_lo)}

        with nc.Block() as block:
            @block.sync
            def _(sp):
                def load(name, dst, src):
                    sp.dma_start(dst, src).then_inc(loaded[name], 16)

                def wide(name):
                    return a[name].rearrange("(k p) n -> p k n", p=P)

                def spread(ap):
                    return ap.unsqueeze(0).to_broadcast([P, ap.shape[0]])

                load("wkd", raw["wkd"][:, :, :], wide("Wkv_dca")[:, :, 0:C])
                for k in range(KK):
                    load("yd", yd[:, k, :, :], a["ctxT"][:, k * P:(k + 1) * P, M:S].rearrange("b p d -> p b d"))
                load("bkd", bkd[:, :], spread(a["bkv_dca"][0:C]))
                load("wvd", raw["wvd"][:, :, :], wide("Wkv_dca")[:, :, C:2 * C])
                load("kd", kd_w[:, :], spread(a["kn_dca_w"]))
                load("kd", kd_b[:, :], spread(a["kn_dca_b"]))
                load("gates", gate_raw[:, 0:1], spread(a["g_xattn"]))
                load("gates", gate_raw[:, 1:2], spread(a["g_ffn"]))
                load("wk", raw["wk"][:, :, :], wide("Wk_heads"))
                load("wv", raw["wv"][:, :, :], wide("Wv_heads"))
                load("wo", raw["wo"][:, :, :], wide("Wo"))
                load("wq", raw["wq"][:, :, :], wide("Wq"))
                load("rows", rows["bq"][:, :], spread(a["bq"]))
                load("rows", rows["bk"][:, :], spread(a["bk_heads"]))
                load("rows", rows["bv"][:, :], spread(a["bv_heads"]))
                load("rows", bvd[:, :], spread(a["bkv_dca"][C:2 * C]))
                load("rows", rows["bo"][:, :], spread(a["bo"]))
                for n in norms:
                    load("rows", norms[n][:, :], spread(a[n]))
                load("late", late["wg"][:, :], a["Wg"][0:1, :].to_broadcast([T, C]))
                load("late", wg1[:, :], a["Wg"][1:2, :].to_broadcast([T, C]))
                load("late", late["b0"][:, :], a["b0b"].unsqueeze(0).to_broadcast([T, C]))
                load("late", late["b1"][:, :], a["b1b"].unsqueeze(0).to_broadcast([T, C]))
                sp.wait_ge(vd_used, ND)
                sp.dma_start(vd_dram.rearrange("(t p) v -> p t v", p=P),
                             vd[:, :, :, :].rearrange("p t h v -> p t (h v)")).then_inc(vd_stored, 16)
                sp.wait_ge(vd_stored, 16)

            @block.gpsimd
            def _(pool):
                nc.gpsimd.memset(identf[:, :], 0.0).then_inc(idents, 1)
                pool.wait_ge(idents, 1)
                nc.gpsimd.affine_select(out=identf[:, :], in_=identf[:, :], compare_op=ALU.not_equal, fill=1.0,
                                        base=0, pattern=[[-1, P]], channel_multiplier=1).then_inc(idents, 1)
                pool.wait_ge(idents, 2)
                nc.gpsimd.tensor_copy(identh[:, :], identf[:, :]).then_inc(idents, 1)
                for name in ("wk", "wv", "wo"):
                    pool.wait_ge(hi_ready, order.index(name) + 1)
                    nc.gpsimd.tensor_tensor(target[name][1][:, :, :], source[name], target[name][0][:, :, :],
                                            ALU.subtract).then_inc(pooled, 1)
                pool.wait_ge(loaded["rows"], 16 * (5 + len(norms)))
                nc.gpsimd.tensor_tensor(rows["bv"][:, :], rows["bv"][:, :], bvd[:, :], ALU.add).then_inc(pooled, 1)
                pool.wait_ge(tanhs, 1)
                nc.gpsimd.tensor_tensor(rows["bo"][:, :], rows["bo"][:, :], gates[:, 0:1].to_broadcast([P, C]),
                                        ALU.mult).then_inc(pooled, 1)
                pool.wait_ge(loaded["late"], 16 * 4)
                nc.gpsimd.tensor_tensor(late["wg"][:, :], late["wg"][:, :], wg1[:, :], ALU.subtract).then_inc(pooled, 1)
                nc.gpsimd.tensor_tensor(late["b0"][:, :], late["b0"][:, :], late["b1"][:, :], ALU.subtract)\
                    .then_inc(pooled, 1)
                pool.wait_ge(pooled, 7)
                nc.gpsimd.tensor_tensor(late["b1"][:, :], late["b1"][:, :], gates[0:T, 1:2].to_broadcast([T, C]),
                                        ALU.mult).then_inc(pooled, 1)

            @block.vector
            def _(dve):
                chain = Chain(dve, own)
                link = chain.link

                def center(ap, k):
                    m = mean[:, 0:k * H]
                    link(nc.vector.tensor_reduce(m, ap, AX.X, ALU.add))
                    link(nc.vector.tensor_scalar(m, m, -1.0 / HD, None, ALU.mult))
                    return nc.vector.tensor_tensor(ap, ap, m.unsqueeze(2).to_broadcast([P, k * H, HD]), ALU.add)

                link(nc.vector.memset(stack[:, :, 3 * HD:], 0.0))
                link(nc.vector.memset(stack[:, :, 3 * HD + 1:3 * HD + 4:2], UNIT))
                link(nc.vector.memset(vd[:, :, :, 0:HD + 1], 0.0))
                nc.vector.memset(vd[:, :, :, VW - 1:VW], 1.0).then_inc(gaps_ready, 1)
                def center_weight(name):
                    k = KC if name == "wq" else KK
                    dve.wait_ge(loaded[name], 16)
                    center(raw[name][:, :, :].rearrange("p k (h d) -> p (k h) d", d=HD), k).then_inc(centered, 1)

                def low(name):
                    dve.wait_ge(loaded[name], 32 if name == "yd" else 16)
                    dve.wait_ge(hi_ready, order.index(name) + 1)
                    nc.vector.tensor_tensor(target[name][1][:, :, :], source[name], target[name][0][:, :, :],
                                            ALU.subtract).then_inc(lo_ready, 1)

                def take(t):
                    dve.wait_ge(kd_ready, t + 1)
                    nc.vector.tensor_tensor(kb[:, :], pk[:, :], bkd[:, :], ALU.add).then_inc(added, 1)

                def variance(t):
                    dve.wait_ge(squared, t + 1)
                    link(nc.vector.tensor_reduce(r[:, :], heads(sq[:, :]), AX.X, ALU.add))
                    nc.vector.tensor_scalar(ve[:, :], r[:, :], 1.0 / HD, EPS_HEAD, ALU.mult, ALU.add)\
                        .then_inc(var_ready, 1)

                def norm(t):
                    dve.wait_ge(y_ready, t + 1)
                    link(nc.vector.scalar_tensor_tensor(out=r[:, :], in0=ve[:, :], scalar=-0.5, in1=y[:, :],
                                                        op0=ALU.mult, op1=ALU.mult))
                    link(nc.vector.tensor_tensor(r[:, :], r[:, :], y[:, :], ALU.mult))
                    link(nc.vector.scalar_tensor_tensor(out=r[:, :], in0=r[:, :], scalar=1.5, in1=y[:, :],
                                                        op0=ALU.add, op1=ALU.mult))
                    dve.wait_ge(added, t + 1)
                    link(nc.vector.tensor_tensor(heads(kn[:, :]), heads(kb[:, :]),
                                                 r[:, :].unsqueeze(2).to_broadcast([P, H, HD]), ALU.mult))
                    link(nc.vector.tensor_tensor(heads(kn[:, :]), heads(kn[:, :]),
                                                 kd_w[:, :].unsqueeze(1).to_broadcast([P, H, HD]), ALU.mult))
                    link(nc.vector.tensor_tensor(heads(kn[:, :]), heads(kn[:, :]),
                                                 kd_b[:, :].unsqueeze(1).to_broadcast([P, H, HD]), ALU.add))
                    if t:
                        dve.wait_ge(turned, 2 * t)
                    link(nc.vector.tensor_copy(stack[:, :, 0:HD], heads(kn[:, :])))
                    link(nc.vector.tensor_copy(stack[:, :, HD:2 * HD], stack[:, :, 0:HD]))
                    nc.vector.tensor_tensor(stack[:, :, 2 * HD:3 * HD], heads(kn[:, :]), stack[:, :, 0:HD],
                                            ALU.subtract).then_inc(stacked, 1)

                center_weight("wkd")
                low("wkd")
                low("yd")
                low("wvd")
                dve.wait_ge(loaded["bkd"], 16)
                link(center(heads(bkd[:, :]), 1))
                dve.wait_ge(loaded["kd"], 32)
                center_weight("wk")
                take(0)
                variance(0)
                center_weight("wq")
                norm(0)
                take(1)
                dve.wait_ge(loaded["rows"], 16 * (5 + len(norms)))
                link(center(heads(rows["bq"][:, :]), 1))
                variance(1)
                link(center(heads(rows["bk"][:, :]), 1))
                norm(1)
                low("wq")

            @block.scalar
            def _(act):
                def hi(n):
                    name = order[n]
                    if name in ("wkd", "wk", "wq"):
                        act.wait_ge(centered, 1 + ("wkd", "wk", "wq").index(name))
                    else:
                        act.wait_ge(loaded[name], 32 if name == "yd" else 16)
                    nc.scalar.activation(target[name][0][:, :, :], source[name], ACT.Copy).then_inc(hi_ready, 1)

                def square(t):
                    act.wait_ge(added, t + 1)
                    if t:
                        act.wait_ge(var_ready, t)
                    nc.scalar.activation(sq[:, :], kb[:, :], ACT.Square).then_inc(squared, 1)

                def values(t):
                    act.wait_ge(vd_ready, t + 1)
                    act.wait_ge(gaps_ready, 1)
                    nc.scalar.activation(vd[:, t, :, HD + 1:2 * HD + 1], heads(pv[:, :]), ACT.Copy)\
                        .then_inc(vd_used, 1)

                def keep(t):
                    for j in range(2):
                        act.wait_ge(turned, 2 * t + j + 1)
                        nc.scalar.activation(kdT[:, 8 * j:8 * j + 8, t * P:(t + 1) * P], pt[j][:, :, :], ACT.Copy)\
                            .then_inc(kept, 1)

                def guess(t):
                    act.wait_ge(var_ready, t + 1)
                    nc.scalar.activation(lnv[:, :], ve[:, :], ACT.Ln).then_inc(own_act, 1)
                    act.wait_ge(own_act, t + 1)
                    nc.scalar.activation(y[:, :], lnv[:, :], ACT.Exp, scale=-0.5).then_inc(y_ready, 1)

                for n in range(3):
                    hi(n)
                act.wait_ge(loaded["gates"], 32)
                nc.scalar.activation(gates[:, :], gate_raw[:, :], ACT.Tanh).then_inc(tanhs, 1)
                act.preload_act_table_set("natural_log_exp_and_others")
                hi(3)
                values(0)
                square(0)
                guess(0)
                hi(4)
                hi(5)
                values(1)
                square(1)
                hi(6)
                guess(1)
                keep(0)
                keep(1)

            @block.tensor
            def _(pe):
                def product(dst, name, t):
                    pairs = ((yd_hi, 0), (yd_hi, 1), (yd_lo, 0))
                    for n, (k, (y_part, part)) in enumerate((k, p) for k in range(KK) for p in pairs):
                        last = nc.tensor.matmul(dst[:, :], y_part[:, k, t * P:(t + 1) * P],
                                                wd[name][part][:, k, :], start=n == 0, stop=n == 3 * KK - 1)
                    return last

                pe.wait_ge(lo_ready, 3)
                pe.wait_ge(hi_ready, 3)
                pe.wait_ge(idents, 3)
                for t in range(ND):
                    if t:
                        pe.wait_ge(added, t)
                        pe.wait_ge(vd_used, t)
                    product(pk, "wkd", t).then_inc(kd_ready, 1)
                    product(pv, "wvd", t).then_inc(vd_ready, 1)
                for t in range(ND):
                    pe.wait_ge(stacked, t + 1)
                    for j in range(2):
                        if t:
                            pe.wait_ge(kept, 2 * (t - 1) + j + 1)
                        for h in range(8):
                            last = nc.tensor.transpose(pt[j][:, h, :], stack[:, 8 * j + h, :], identh[:, :])
                        last.then_inc(turned, 1)


CHUNKS = [(e, kind, k) for e in range(2) for kind in ("up", "down") for k in range(4)]


def load_raw(eng, a, n, raw, w_in):
    e, kind, k = CHUNKS[n]
    src = a[f"W{e}aT"][k * P:(k + 1) * P, :] if kind == "up" else \
        a[f"W{e}bT"][2 * k * P:2 * (k + 1) * P, :].rearrange("(j p) n -> p j n", p=P)
    dst = raw[n % RAWS][:, :] if kind == "up" else raw[n % RAWS][:, :].rearrange("p (j n) -> p j n", j=2)
    eng.dma_start(dst, src).then_inc(w_in[n], 16)


def attend(nc, a, w, rows, norms, kdT, vd_dram, gates, identf, identh, x1_dram, raw, first_in):
    with ExitStack() as ctx:
        def sb(name, shape, dt=F32):
            return ctx.enter_context(nc.sbuf_tensor(name, shape, dt))

        def sem(name):
            return ctx.enter_context(nc.semaphore(name))

        def bank(name):
            return ctx.enter_context(nc.psum_tensor(name, [P, 512], F32))

        x_raw = [sb(f"x_raw{i}", [T, C]) for i in range(2)]
        xb = [sb(f"xb{i}", [T, C]) for i in range(2)]
        y_raw = [sb(f"y_raw{i}", [P, KK, S]) for i in range(2)]
        y_hi, y_lo = sb("y_hi", [P, KK, S], F32R), sb("y_lo", [P, KK, S], F32R)
        xn = sb("xn", [T, C])
        x_hi, x_lo = sb("x_hi", [P, KC, T], F32R), sb("x_lo", [P, KC, T], F32R)
        bn, mv, xve, xln, xy, xr = (sb(n, [T, k]) for n, k in
                                    (("bn", 6), ("mv", 2), ("xve", 1), ("xln", 1), ("xy", 1), ("xr", 1)))
        kbs, rs = ([sb(f"t_{n}{i}", [P, k]) for i in range(2)] for n, k in (("kb", C), ("r", H)))
        sq, ka = (sb(f"t_{n}", [P, C]) for n in ("sq", "ka"))
        ve, lnv, y = (sb(f"t_{n}", [P, H]) for n in ("ve", "lnv", "y"))
        stack_q, stack_k = (sb(f"stack_{n}", [P, H, P], F16) for n in "qk")
        stacks = {n: stack_q if n == "Q" else stack_k for n in CHAIN}
        kT = [sb(f"kT{i}", [P, H, S + 1], F16) for i in range(2)]
        qT = [sb(f"qT{i}", [P, H, T], F16) for i in range(2)]
        v_first = [sb(f"v_first{i}", [P, H, VW]) for i in range(2)]
        v_mid = [sb(f"v_mid{i}", [P, H, HD + 1]) for i in range(2)]
        v_last = [sb(f"v_last{i}", [P, H, VW]) for i in range(2)]
        nmax = sb("nmax", [T, G, 2])
        shift = sb("shift", [T, H, HD], F16)
        p = [[sb(f"p{i}{k}", [P, G * T]) for k in range(3)] for i in range(2)]
        ctxT_raw = sb("ctxT_raw", [VW, H, T])
        inv = sb("inv", [T, G, 2])
        cm, cd = sb("cm", [T, G, HD]), sb("cd", [T, G, HD])
        ctxn = sb("ctxn", [T, H, HD])
        c_hi, c_lo = sb("c_hi", [P, KC, T], F32R), sb("c_lo", [P, KC, T], F32R)
        x1 = [sb(f"x1_{i}", [T, C + 2]) for i in range(2)]

        work = [bank(f"work{i}") for i in range(BANKS)]
        top = [bank(f"top{i}") for i in range(2)]
        score = [bank(f"score{i}") for i in range(2)]
        pv = bank("pv_acc")

        w_ready = [sem(f"work_ready{i}") for i in range(BANKS)]
        w_free = [sem(f"work_free{i}") for i in range(BANKS)]
        x_in, y_in, vd_in, x1_out = ([sem(f"{n}{i}") for i in range(2)] for n in ("x_in", "y_in", "vd_in", "x1_out"))
        consts = sem("consts_ready")
        own_v, own_a, own_p = sem("vector_own2"), sem("scalar_own2"), sem("pool_own2")
        names = ["x_var", "x_rsqrt", "x_normed", "x_hi_ready", "y_hi_ready", "y_lo_ready", "xb_ready", "squared",
                 "var_ready", "rsqrt_ready", "deviated", "scaled", "affine_ready",
                 "high_ready", "copied_ready", "low_ready",
                 "kd_copied", "top_ready", "top_free", "shift_ready", "score_ready", "exp_ready", "pv_ready",
                 "ctx_copied", "ctx_ready", "c_hi_ready", "x1_ready"]
        s = {n: sem(n) for n in names}

        def wait_free(pe, st, use):
            at_least(pe, w_free[st.bank(use)], st.before(use))

        def wait_ready(eng, st, use):
            eng.wait_ge(w_ready[st.bank(use)], st.before(use) + 1)

        def wait_read(pe, st, use):
            pe.wait_ge(w_free[st.bank(use)], st.before(use) + 1)

        def size_of(tile):
            return T if tile == "Q" else ROWS[int(tile[1])]

        def place(batch, tile):
            return 4 * batch + CHAIN.index(tile)

        def halves(use, st, n):
            return work[st.bank(use)][:, :].bitcast(F16).rearrange("p (h k) -> p h k", h=8)[:, :, 0:n]

        def rstd(nv, link, out_, v, guess):
            link(nv.scalar_tensor_tensor(out=out_, in0=v, scalar=-0.5, in1=guess, op0=ALU.mult, op1=ALU.mult))
            link(nv.tensor_tensor(out_, out_, guess, ALU.mult))
            return nv.scalar_tensor_tensor(out=out_, in0=out_, scalar=1.5, in1=guess, op0=ALU.add, op1=ALU.mult)

        with nc.Block() as block:
            @block.sync
            def _(sp):
                def load(n, par):
                    at_least(sp, s["x_normed"], n - 1)
                    at_least(sp, s["xb_ready"], n - 1)
                    sp.dma_start(x_raw[par][:, :], a["x"].rearrange("b t c -> (b t) c")[one(n, T), :])\
                        .then_inc(x_in[par], 16)
                    at_least(sp, s["y_lo_ready"], n - 1)
                    sp.dma_start(y_raw[par][:, :, :], a["ctxT"].rearrange("b (k p) m -> p (b k) m", p=P)
                                 [:, one(n, KK), :]).then_inc(y_in[par], 16)

                def dca_values(n, par):
                    at_least(sp, s["pv_ready"], NG * (n - 1))
                    sp.dma_start(v_last[par][ROWS[2]:KEYS[2], :, :],
                                 vd_dram[one(n, DCA), :].rearrange("k (h v) -> k h v", h=H)).then_inc(vd_in[par], 16)

                def store(n, par):
                    sp.wait_ge(s["x1_ready"], n + 1)
                    sp.dma_start(x1_dram[one(n, T), :], x1[par][:, :]).then_inc(x1_out[par], 16)

                for par in range(2):
                    sp.sem_inc(x1_out[par], 1)
                for n in range(2):
                    load(n, n)
                sp.wait_ge(consts, 10)
                for n in range(2):
                    dca_values(n, n)
                load(2, 0)
                load(3, 1)
                dca_values(2, 0)
                for n in range(RAWS):
                    load_raw(sp, a, n, raw, first_in)
                with sp.Fori(0, PAIRS) as i:
                    for par in range(2):
                        b = i * 2 + (1 + par)
                        store(i * 2 + par, par)
                        load(b + 3, par)
                        dca_values(b + 2, 1 - par)
                store(B - 4, 0)
                dca_values(B - 1, 1)
                for n in (B - 3, B - 2, B - 1):
                    store(n, n % 2)
                for par in range(2):
                    sp.wait_ge(x1_out[par], 16 * (B // 2) + 1)

            @block.vector
            def _(dve):
                chain = Chain(dve, own_v, VECTOR_OWN)
                link = chain.link
                nv = nc.vector

                link(nv.memset(stack_q[:, :, 3 * HD:], 0.0))
                link(nv.memset(stack_k[:, :, 3 * HD:], 0.0))
                link(nv.memset(stack_k[:, :, 3 * HD:3 * HD + 3:2], UNIT))
                link(nv.memset(shift[:, :, :], 0.0))
                def row_stats(n, par):
                    dve.wait_ge(x_in[par], transfers(n, par, 1))
                    link(nv.bn_stats(bn[:, :], x_raw[par][:, :]))
                    nv.memset(xve[:, :], 0.0)
                    link(nv.bn_aggr(mv[:, :], bn[:, :]))
                    nv.tensor_scalar(xve[:, :], mv[:, 1:2], EPS_ROW, None, ALU.add).then_inc(s["x_var"], 1)

                def row_norm(n, par):
                    dve.wait_ge(s["x_rsqrt"], n + 1)
                    link(rstd(nv, link, xr[:, :], xve[:, :], xy[:, :]))
                    nv.tensor_scalar(xn[:, :], x_raw[par][:, :], mv[:, 0:1], xr[:, :], ALU.subtract, ALU.mult)\
                        .then_inc(s["x_normed"], 1)

                def add_bias(st, batch, tile):
                    m, kb = size_of(tile), kbs[CHAIN.index(tile) % 2]
                    at_least(dve, s["scaled"], place(batch, tile) - 1)
                    wait_ready(dve, st, tile)
                    nv.tensor_tensor(kb[0:m, :], work[st.bank(tile)][0:m, :],
                                     rows["bq" if tile == "Q" else "bk"][0:m, :], ALU.add)\
                        .then_inc(w_free[st.bank(tile)], 1)

                def head_var(batch, tile):
                    m, n, r = size_of(tile), place(batch, tile), rs[CHAIN.index(tile) % 2]
                    at_least(dve, s["scaled"], n - 1)
                    dve.wait_ge(s["squared"], n + 1)
                    link(nv.tensor_reduce(r[0:m, :], heads(sq[0:m, :]), AX.X, ALU.add))
                    nv.tensor_scalar(ve[0:m, :], r[0:m, :], 1.0 / HD, EPS_HEAD, ALU.mult, ALU.add)\
                        .then_inc(s["var_ready"], 1)

                def head_norm(batch, tile):
                    m, n, r = size_of(tile), place(batch, tile), rs[CHAIN.index(tile) % 2]
                    dve.wait_ge(s["rsqrt_ready"], n + 1)
                    rstd(nv, link, r[0:m, :], ve[0:m, :], y[0:m, :]).then_inc(s["deviated"], 1)

                def maxima(b, g, lo, up):
                    if lo == 0:
                        at_least(dve, s["shift_ready"], b * NG + g)
                    for h in range(lo, up):
                        n = b * H + (G * g + h)
                        dve.wait_ge(s["top_ready"], n + 1)
                        nv.tensor_reduce(nmax[:, h, 0:1], top[h % 2][0:T, 0:M], AX.X, ALU.max, negate=True)
                        nv.tensor_reduce(nmax[:, h, 1:2], top[h % 2][0:T, M:S], AX.X, ALU.max, negate=True)\
                            .then_inc(s["top_free"], 1)

                def shifts(b, g):
                    dve.wait_ge(s["top_free"], b * H + G * (g + 1))
                    hs = shift[:, G * g:G * g + G, :]
                    link(nv.tensor_scalar(hs[:, :, 0:2], nmax[:, :, :], 1.0 / UNIT, None, ALU.mult))
                    nv.scalar_tensor_tensor(out=hs[:, :, 2:4], in0=nmax[:, :, :], scalar=1.0 / UNIT,
                                            in1=hs[:, :, 0:2], op0=ALU.mult, op1=ALU.subtract)\
                        .then_inc(s["shift_ready"], 1)

                def context(st, use, g):
                    wait_ready(dve, st, use)
                    ct = work[st.bank(use)][0:T, 0:G * VW].rearrange("t (h v) -> t h v", v=VW)
                    wide = [T, G, HD]
                    link(nv.reciprocal(inv[:, :, :], ct[:, :, HD:VW:HD + 1]))
                    link(nv.tensor_tensor(cm[:, :, :], ct[:, :, 0:HD], inv[:, :, 0:1].to_broadcast(wide), ALU.mult))
                    nv.tensor_tensor(cd[:, :, :], ct[:, :, HD + 1:VW - 1], inv[:, :, 1:2].to_broadcast(wide),
                                     ALU.mult).then_inc(w_free[st.bank(use)], 1)
                    link(nv.tensor_tensor(cm[:, :, :], cm[:, :, :], heads(rows["bv"][0:T, :])[:, G * g:G * g + G, :],
                                          ALU.add))
                    dve.wait_ge(w_free[st.bank(use)], st.before(use) + 1)
                    nv.tensor_tensor(ctxn[:, G * g:G * g + G, :], cm[:, :, :], cd[:, :, :], ALU.add)\
                        .then_inc(s["ctx_ready"], 1)

                def low_rows(st, use, lo, hi, hi_sem, value):
                    wait_ready(dve, st, use)
                    dve.wait_ge(hi_sem, value)
                    nv.tensor_tensor(lo[:, :, :].rearrange("p k t -> p (k t)"), work[st.bank(use)][:, 0:KC * T],
                                     hi[:, :, :].rearrange("p k t -> p (k t)"), ALU.subtract)\
                        .then_inc(w_free[st.bank(use)], 1)

                def body(st):
                    n, npar = st.b + 1, 1 - st.parity
                    m = st.b + 2
                    if st.d:
                        context(st, "ct3", NG - 1)
                    if st.c:
                        maxima(st.b, 1, 2, 4)
                    if st.a:
                        head_var(n, "K1")
                    if st.c:
                        shifts(st.b, 1)
                    if st.e:
                        row_stats(m, st.parity)
                    if st.d:
                        low_rows(st, "cT", c_lo, c_hi, s["c_hi_ready"], st.b)
                    if st.a:
                        add_bias(st, n, "K2")
                        head_norm(n, "K1")
                    if st.e:
                        row_norm(m, st.parity)
                    if st.c:
                        maxima(st.b, 2, 0, 2)
                    if st.c:
                        maxima(st.b, 2, 2, 4)
                        context(st, "ct0", 0)
                    if st.a:
                        head_var(n, "K2")
                    if st.c:
                        shifts(st.b, 2)
                    if st.a:
                        head_norm(n, "K2")
                    if st.d:
                        d = st.b - 1
                        wait_ready(dve, st, "Wo")
                        dve.wait_ge(x1_out[npar], transfers(d, npar, 0) + 1)
                        dve.wait_ge(s["xb_ready"], st.b)
                        nv.scalar_tensor_tensor(out=x1[npar][:, 0:C], in0=work[st.bank("Wo")][0:T, :],
                                                scalar=gates[0:T, 0:1], in1=xb[npar][:, :],
                                                op0=ALU.mult, op1=ALU.add).then_inc(w_free[st.bank("Wo")], 1)
                    if st.e:
                        low_rows(st, "xT", x_lo, x_hi, s["x_hi_ready"], m + 1)
                    if st.d:
                        dve.wait_ge(w_free[st.bank("Wo")], st.before("Wo") + 1)
                        link(nv.bn_stats(bn[:, :], x1[npar][:, 0:C]))
                        nv.memset(xve[:, :], 0.0)
                        nv.bn_aggr(x1[npar][:, C:C + 2], bn[:, :]).then_inc(s["x1_ready"], 1)
                        dve.wait_ge(s["x1_ready"], st.b)
                    if st.e:
                        add_bias(st, m, "K0")
                    if st.c:
                        maxima(st.b, 3, 0, 2)
                    if st.c:
                        maxima(st.b, 3, 2, 4)
                    if st.e:
                        head_var(m, "K0")
                    if st.c:
                        shifts(st.b, 3)
                        context(st, "ct1", 1)
                    if st.e:
                        add_bias(st, m, "Q")
                        head_norm(m, "K0")
                    if st.a:
                        maxima(n, 0, 0, 2)
                    if st.a:
                        maxima(n, 0, 2, 4)
                    if st.e:
                        head_var(m, "Q")
                    if st.a:
                        shifts(n, 0)
                    if st.c:
                        context(st, "ct2", 2)
                    if st.e:
                        head_norm(m, "Q")
                        add_bias(st, m, "K1")
                    if st.a:
                        maxima(n, 1, 0, 2)

                run_steps(dve, body, chain)

            @block.scalar
            def _(act):
                chain = Chain(act, own_a, SCALAR_OWN)
                link = chain.link
                ns = nc.scalar
                act.preload_act_table_set("natural_log_exp_and_others")

                def square(st, batch, tile):
                    m, n = size_of(tile), place(batch, tile)
                    wait_read(act, st, tile)
                    at_least(act, s["var_ready"], n)
                    ns.activation(sq[0:m, :], kbs[CHAIN.index(tile) % 2][0:m, :], ACT.Square).then_inc(s["squared"], 1)

                def guess(batch, tile):
                    m, n = size_of(tile), place(batch, tile)
                    act.wait_ge(s["var_ready"], n + 1)
                    link(ns.activation(lnv[0:m, :], ve[0:m, :], ACT.Ln))
                    ns.activation(y[0:m, :], lnv[0:m, :], ACT.Exp, scale=-0.5).then_inc(s["rsqrt_ready"], 1)

                def high(batch, tile):
                    m, n = size_of(tile), place(batch, tile)
                    stack, second = stacks[tile], 2 * HD if tile == "Q" else HD
                    act.wait_ge(s["affine_ready"], n + 1)
                    ns.activation(stack[0:m, :, 0:HD], heads(ka[0:m, :]), ACT.Copy).then_inc(s["high_ready"], 1)
                    ns.activation(stack[0:m, :, second:second + HD], heads(ka[0:m, :]), ACT.Copy)\
                        .then_inc(s["copied_ready"], 1)

                def row_guess(n):
                    act.wait_ge(s["x_var"], n + 1)
                    link(ns.activation(xln[:, :], xve[:, :], ACT.Ln))
                    ns.activation(xy[:, :], xln[:, :], ACT.Exp, scale=-0.5).then_inc(s["x_rsqrt"], 1)

                def context_high(n, par):
                    act.wait_ge(y_in[par], transfers(n, par, 1))
                    ns.activation(y_hi[:, :, :], y_raw[par][:, :, :], ACT.Copy).then_inc(s["y_hi_ready"], 1)

                def copy_pv(b, g):
                    act.wait_ge(s["pv_ready"], b * NG + (g + 1))
                    ns.activation(ctxT_raw[:, G * g:G * g + G, :],
                                  pv[0:VW, 0:G * T].rearrange("v (h t) -> v h t", h=G), ACT.Copy)\
                        .then_inc(s["ctx_copied"], 1)

                def shift_rows(st, use, g):
                    par = st.parity if g else 1 - st.parity
                    wait_ready(act, st, use)
                    ns.activation(qT[par][3 * HD:P, G * g:G * g + G, :],
                                  work[st.bank(use)][3 * HD:P, :].bitcast(F16)[:, 0:G * T]
                                  .rearrange("p (h t) -> p h t", h=G), ACT.Copy).then_inc(w_free[st.bank(use)], 1)

                def exps(b, g):
                    at_least(act, s["pv_ready"], b * NG + (g - 1))
                    for k in range(3):
                        n = b * (3 * NG) + (3 * g + k)
                        act.wait_ge(s["score_ready"], n + 1)
                        ns.activation(p[g % 2][k][0:KEYS[k], :], score[(3 * g + k) % 2][0:KEYS[k], 0:G * T],
                                      ACT.Exp, scale=SCALE).then_inc(s["exp_ready"], 1)

                def values(st, tile):
                    k, par = int(tile[1]), 1 - st.parity
                    wait_ready(act, st, tile)
                    dst = (v_first, v_mid, v_last)[k][par][0:ROWS[k], :, 0:HD]
                    ns.activation(dst, heads(work[st.bank(tile)][0:ROWS[k], :]), ACT.Copy)\
                        .then_inc(w_free[st.bank(tile)], 1)

                def key_copy(st, tile):
                    k, j = int(tile[2]), int(tile[3])
                    wait_ready(act, st, tile)
                    ns.activation(kT[1 - st.parity][:, 8 * j:8 * j + 8, k * P:k * P + ROWS[k]],
                                  halves(tile, st, ROWS[k]), ACT.Copy).then_inc(w_free[st.bank(tile)], 1)

                def query_copy(st, j):
                    use = f"qt{j}"
                    wait_ready(act, st, use)
                    ns.activation(qT[1 - st.parity][:, 8 * j:8 * j + 8, :], halves(use, st, T), ACT.Copy)\
                        .then_inc(w_free[st.bank(use)], 1)

                def high_rows(st, use, hi, done):
                    wait_ready(act, st, use)
                    ns.activation(hi[:, :, :].rearrange("p k t -> p (k t)"), work[st.bank(use)][:, 0:KC * T],
                                  ACT.Copy).then_inc(done, 1)

                def body(st):
                    n, npar, m = st.b + 1, 1 - st.parity, st.b + 2
                    if st.d:
                        copy_pv(st.b - 1, NG - 1)
                    if st.c:
                        exps(st.b, 0)
                    if st.a:
                        high(n, "Q")
                        values(st, "V0")
                        guess(n, "K1")
                        values(st, "V1")
                    if st.d:
                        high_rows(st, "cT", c_hi, s["c_hi_ready"])
                    if st.a:
                        values(st, "V2")
                    if st.e:
                        context_high(m, st.parity)
                        row_guess(m)
                    if st.a:
                        key_copy(st, "kt00")
                        key_copy(st, "kt01")
                    if st.c:
                        shift_rows(st, "mt1", 1)
                    if st.a:
                        square(st, n, "K2")
                    if st.c:
                        copy_pv(st.b, 0)
                        exps(st.b, 1)
                    if st.a:
                        high(n, "K1")
                        query_copy(st, 0)
                        query_copy(st, 1)
                        guess(n, "K2")
                    if st.e:
                        high_rows(st, "xT", x_hi, s["x_hi_ready"])
                    if st.a:
                        key_copy(st, "kt10")
                        key_copy(st, "kt11")
                    if st.c:
                        shift_rows(st, "mt2", 2)
                    if st.e:
                        square(st, m, "K0")
                    if st.c:
                        copy_pv(st.b, 1)
                        exps(st.b, 2)
                    if st.a:
                        high(n, "K2")
                    if st.e:
                        guess(m, "K0")
                    if st.a:
                        key_copy(st, "kt20")
                        key_copy(st, "kt21")
                    if st.c:
                        shift_rows(st, "mt3", 3)
                    if st.e:
                        square(st, m, "Q")
                    if st.c:
                        copy_pv(st.b, 2)
                        exps(st.b, 3)
                    if st.e:
                        high(m, "K0")
                        guess(m, "Q")
                    if st.a:
                        shift_rows(st, "mt0", 0)
                    if st.e:
                        square(st, m, "K1")

                run_steps(act, body, chain)

            @block.gpsimd
            def _(pool):
                chain = Chain(pool, own_p, POOL_OWN)
                link = chain.link
                ng = nc.gpsimd

                def affine(batch, tile):
                    m, n, k = size_of(tile), place(batch, tile), CHAIN.index(tile) % 2
                    kind = "qn" if tile == "Q" else "kn"
                    pool.wait_ge(s["deviated"], n + 1)
                    at_least(pool, s["copied_ready"], n)
                    ng.tensor_tensor(heads(ka[0:m, :]), heads(kbs[k][0:m, :]),
                                     rs[k][0:m, :].unsqueeze(2).to_broadcast([m, H, HD]), ALU.mult)\
                        .then_inc(s["scaled"], 1)
                    pool.wait_ge(s["scaled"], n + 1)
                    link(ng.tensor_tensor(heads(ka[0:m, :]), heads(ka[0:m, :]),
                                          norms[kind + "_w"][0:m, :].unsqueeze(1).to_broadcast([m, H, HD]), ALU.mult))
                    ng.tensor_tensor(heads(ka[0:m, :]), heads(ka[0:m, :]),
                                     norms[kind + "_b"][0:m, :].unsqueeze(1).to_broadcast([m, H, HD]), ALU.add)\
                        .then_inc(s["affine_ready"], 1)

                def low(batch, tile):
                    m, n = size_of(tile), place(batch, tile)
                    pool.wait_ge(s["high_ready"], n + 1)
                    at = HD if tile == "Q" else 2 * HD
                    ng.tensor_tensor(stacks[tile][0:m, :, at:at + HD], heads(ka[0:m, :]),
                                     stacks[tile][0:m, :, 0:HD], ALU.subtract).then_inc(s["low_ready"], 1)
                    pool.wait_ge(s["low_ready"], n + 1)

                def context_low(n, par):
                    pool.wait_ge(s["y_hi_ready"], n + 1)
                    ng.tensor_tensor(y_lo[:, :, :], y_raw[par][:, :, :], y_hi[:, :, :], ALU.subtract)\
                        .then_inc(s["y_lo_ready"], 1)

                def body(st):
                    n, npar, m = st.b + 1, 1 - st.parity, st.b + 2
                    if st.a:
                        low(n, "Q")
                        ng.tensor_copy(kT[npar][:, :, M:S],
                                       kdT[:, :, one(n, DCA)]).then_inc(s["kd_copied"], 1)
                        affine(n, "K1")
                    if st.a:
                        low(n, "K1")
                    if st.e:
                        context_low(m, st.parity)
                    if st.a:
                        affine(n, "K2")
                    if st.a:
                        low(n, "K2")
                    if st.e:
                        affine(m, "K0")
                    if st.a:
                        at_least(pool, s["x1_ready"], st.b)
                        pool.wait_ge(x_in[npar], transfers(n, npar, 1))
                        ng.tensor_tensor(xb[npar][:, :], x_raw[npar][:, :], rows["bo"][0:T, :], ALU.add)\
                            .then_inc(s["xb_ready"], 1)
                    if st.e:
                        low(m, "K0")
                        affine(m, "Q")

                for i in range(2):
                    parts = ((v_first[i][:, :, HD:], 0.0), (v_first[i][:, :, HD:HD + 1], 1.0),
                             (v_mid[i][:, :, HD:], 1.0),
                             (v_last[i][:, :, HD:], 0.0), (v_last[i][:, :, HD:HD + 1], 1.0))
                    for j, (ap, value) in enumerate(parts):
                        ng.memset(ap, value).then_inc(consts, 1)
                        pool.wait_ge(consts, 5 * i + j + 1)
                run_steps(pool, body, chain)

            @block.tensor
            def _(pe):
                nt = nc.tensor

                def three(dst, m, left, right, depth, cols):
                    parts = [(k, i, j) for k in range(depth) for i, j in ((0, 0), (0, 1), (1, 0))]
                    for n, (k, i, j) in enumerate(parts):
                        last = nt.matmul(dst, left[i][:, k, cols[0]:cols[0] + m], right[j][:, k, :],
                                         start=n == 0, stop=n == len(parts) - 1)
                    return last

                def turn_rows(st, use, src):
                    wait_free(pe, st, use)
                    for k in range(KC):
                        last = nt.transpose(work[st.bank(use)][:, k * T:(k + 1) * T], src[:, k * P:(k + 1) * P],
                                            identf[0:T, 0:T])
                    last.then_inc(w_ready[st.bank(use)], 1)

                def project(st, tile):
                    k = int(tile[1])
                    wait_free(pe, st, tile)
                    three(work[st.bank(tile)][0:ROWS[k], :], ROWS[k], (y_hi, y_lo), w["w" + tile[0].lower()], KK,
                          (k * P,)).then_inc(w_ready[st.bank(tile)], 1)

                def turn_stack(st, use, batch, tile, j):
                    m, n = size_of(tile), place(batch, tile)
                    pe.wait_ge(s["copied_ready"], n + 1)
                    pe.wait_ge(s["low_ready"], n + 1)
                    wait_free(pe, st, use)
                    dst = halves(use, st, m)
                    for h in range(8):
                        last = nt.transpose(dst[:, h, :], stacks[tile][0:m, 8 * j + h, :], identh[0:m, 0:m])
                    last.then_inc(w_ready[st.bank(use)], 1)

                def tops(b, par, g, lo, up):
                    for h in range(lo, up):
                        n = b * H + (G * g + h)
                        at_least(pe, s["top_free"], n - 1)
                        nt.matmul(top[h % 2][0:T, 0:S], qT[par][:, G * g + h, :], kT[par][:, G * g + h, 0:S],
                                  start=True, stop=True).then_inc(s["top_ready"], 1)

                def turn_shift(st, use, batch, g):
                    pe.wait_ge(s["shift_ready"], batch * NG + (g + 1))
                    wait_free(pe, st, use)
                    dst = work[st.bank(use)][3 * HD:P, :].bitcast(F16)
                    for h in range(G):
                        last = nt.transpose(dst[:, h * T:(h + 1) * T], shift[:, G * g + h, :], identh[0:T, 0:T])
                    last.then_inc(w_ready[st.bank(use)], 1)

                def scores(st, g, tiles):
                    for k in tiles:
                        n = st.b * (3 * NG) + (3 * g + k)
                        at_least(pe, s["exp_ready"], n - 1)
                        for h in range(G):
                            last = nt.matmul(score[(3 * g + k) % 2][0:KEYS[k], h * T:(h + 1) * T],
                                             kT[st.parity][:, G * g + h, k * P:k * P + KEYS[k]],
                                             qT[st.parity][:, G * g + h, :], start=True, stop=True)
                        last.then_inc(s["score_ready"], 1)

                def weigh(st, g):
                    pe.wait_ge(s["exp_ready"], st.b * (3 * NG) + 3 * (g + 1))
                    at_least(pe, s["ctx_copied"], st.b * NG + g)
                    if g == 0:
                        pe.wait_ge(vd_in[st.parity], transfers(st.b, st.parity, 1))
                    for h in range(G):
                        cols = slice(h * T, (h + 1) * T)
                        for k, (v, width) in enumerate(((v_first, VW), (v_mid, HD + 1), (v_last, VW))):
                            last = nt.matmul(pv[0:width, cols], v[st.parity][0:KEYS[k], G * g + h, :],
                                             p[g % 2][k][0:KEYS[k], cols], start=k == 0, stop=k == 2)
                    last.then_inc(s["pv_ready"], 1)

                def turn_context(st, use, b, g):
                    pe.wait_ge(s["ctx_copied"], b * NG + (g + 1))
                    wait_free(pe, st, use)
                    for h in range(G):
                        last = nt.transpose(work[st.bank(use)][0:T, h * VW:(h + 1) * VW],
                                            ctxT_raw[:, G * g + h, :], identf[0:VW, 0:VW])
                    last.then_inc(w_ready[st.bank(use)], 1)

                def body(st):
                    n, npar, m = st.b + 1, 1 - st.parity, st.b + 2
                    if st.c:
                        scores(st, 0, (0, 1))
                        tops(st.b, st.parity, 1, 2, 4)
                    if st.d:
                        turn_context(st, "ct3", st.b - 1, NG - 1)
                    if st.c:
                        scores(st, 0, (2,))
                    if st.a:
                        project(st, "V0")
                        project(st, "V1")
                    if st.d:
                        pe.wait_ge(s["ctx_ready"], st.b * NG)
                        turn_rows(st, "cT", ctxn[:, :, :].rearrange("t h d -> t (h d)"))
                    if st.a:
                        project(st, "K2")
                        project(st, "V2")
                        turn_stack(st, "kt00", n, "K0", 0)
                        turn_stack(st, "kt01", n, "K0", 1)
                    if st.c:
                        tops(st.b, st.parity, 2, 0, 2)
                        turn_shift(st, "mt1", st.b, 1)
                        weigh(st, 0)
                        wait_read(pe, st, "mt1")
                    if st.c:
                        scores(st, 1, (0, 1))
                        tops(st.b, st.parity, 2, 2, 4)
                        turn_context(st, "ct0", st.b, 0)
                        scores(st, 1, (2,))
                    if st.a:
                        turn_stack(st, "qt0", n, "Q", 0)
                        turn_stack(st, "qt1", n, "Q", 1)
                    if st.d:
                        wait_free(pe, st, "Wo")
                        pe.wait_ge(s["c_hi_ready"], st.b)
                        assert st.bank("Wo") == st.bank("cT")
                        three(work[st.bank("Wo")][0:T, :], T, (c_hi, c_lo), w["wo"], KC, (0,))\
                            .then_inc(w_ready[st.bank("Wo")], 1)
                    if st.e:
                        pe.wait_ge(s["x_normed"], m + 1)
                        turn_rows(st, "xT", xn)
                    if st.a:
                        turn_stack(st, "kt10", n, "K1", 0)
                        turn_stack(st, "kt11", n, "K1", 1)
                    if st.e:
                        pe.wait_ge(s["y_hi_ready"], m + 1)
                        pe.wait_ge(s["y_lo_ready"], m + 1)
                        project(st, "K0")
                    if st.c:
                        tops(st.b, st.parity, 3, 0, 2)
                        turn_shift(st, "mt2", st.b, 2)
                        weigh(st, 1)
                        wait_read(pe, st, "mt2")
                    if st.c:
                        scores(st, 2, (0, 1))
                        tops(st.b, st.parity, 3, 2, 4)
                        turn_context(st, "ct1", st.b, 1)
                        scores(st, 2, (2,))
                    if st.e:
                        assert st.bank("Q") == st.bank("xT")
                        wait_free(pe, st, "Q")
                        pe.wait_ge(s["x_hi_ready"], m + 1)
                        three(work[st.bank("Q")][0:T, :], T, (x_hi, x_lo), w["wq"], KC, (0,))\
                            .then_inc(w_ready[st.bank("Q")], 1)
                    if st.a:
                        turn_stack(st, "kt20", n, "K2", 0)
                        turn_stack(st, "kt21", n, "K2", 1)
                    if st.c:
                        turn_shift(st, "mt3", st.b, 3)
                        weigh(st, 2)
                        wait_read(pe, st, "mt3")
                    if st.a:
                        pe.wait_ge(s["kd_copied"], n + 1)
                        for use in ("kt20", "kt21"):
                            wait_read(pe, st, use)
                        tops(n, npar, 0, 0, 2)
                    if st.c:
                        scores(st, 3, (0, 1))
                    if st.a:
                        tops(n, npar, 0, 2, 4)
                    if st.c:
                        turn_context(st, "ct2", st.b, 2)
                        scores(st, 3, (2,))
                    if st.e:
                        project(st, "K1")
                    if st.a:
                        tops(n, npar, 1, 0, 2)
                        turn_shift(st, "mt0", n, 0)
                    if st.c:
                        weigh(st, 3)
                    if st.a:
                        wait_read(pe, st, "mt0")

                run_steps(pe, body, None)


def experts(nc, a, gates, late, identf, x1_dram, raw, first_in, out):
    N = G * T
    GROUPS = B // G
    SLOTS = 4
    NQ = 2 * KF
    with ExitStack() as ctx:
        def sb(name, shape, dt=F32):
            return ctx.enter_context(nc.sbuf_tensor(name, shape, dt))

        def sem(name):
            return ctx.enter_context(nc.semaphore(name))

        def bank(name):
            return ctx.enter_context(nc.psum_tensor(name, [P, 512], F32))

        up_w = [[sb(f"up{e}_{part}", [P, KC, F], F32R) for part in ("hi", "lo")] for e in range(2)]
        down_w = [[sb(f"down{e}_{part}", [P, KF, C], F32R) for part in ("hi", "lo")] for e in range(2)]
        up_b = sb("up_b", [P, 2, KF])
        stats, rs = sb("stats", [T, B, 2]), sb("rs", [T, B])
        rs_ve, rs_ln, rs_y = sb("rs_ve", [T, B]), sb("rs_ln", [T, B]), sb("rs_y", [T, B])
        x1 = sb("x1_group", [T, G, C + 2])
        x3 = sb("x3_group", [T, G, C])
        x2 = sb("x2", [T, G, C])
        junk = sb("junk", [T, C])
        score = sb("route", [T, G])
        scale = sb("scale", [T, 2, G])
        scale1 = sb("scale1", [T, G])
        rg = sb("rg", [T, G])
        t_hi, t_lo = sb("t_hi", [P, KC, N], F32R), sb("t_lo", [P, KC, N], F32R)
        act_out = [sb(f"act_out{i}", [P, N]) for i in range(2)]
        h_hi, h_lo = sb("h_hi", [P, SLOTS, N], F32R), sb("h_lo", [P, SLOTS, N], F32R)
        turn = [bank(f"turn{i}") for i in range(2)]
        hidden = [bank(f"hidden{i}") for i in range(2)]
        result = [bank(f"result{i}") for i in range(G)]

        names = ["w_hi_ready", "w_lo_ready", "pool_hi_ready", "pool_lo_ready", "rows_in", "stats_in", "x1_in",
                 "out_done",
                 "rs_var", "rs_guess", "own_v3", "own_a3", "x2_ready", "biased", "based", "turned",
                 "t_hi_ready", "t_lo_ready", "hidden_ready", "act_ready", "h_ready", "down_ready", "result_free",
                 "final"]
        s = {n: sem(n) for n in names}

        CREDIT = {"h_ready": 2, "act_ready": 2, "t_lo_ready": 2, "down_ready": SLOTS, "final": 1}

        chunks = CHUNKS
        w_in = first_in + [sem(f"w_in{n}") for n in range(RAWS, len(chunks))]
        wg, b0, b1 = (late[n] for n in ("wg", "b0", "b1"))

        def chunk(which, part):
            e, kind, k = which
            if kind == "up":
                return up_w[e][part][:, k, :]
            return down_w[e][part][:, 2 * k:2 * k + 2, :].rearrange("p k n -> p (k n)")

        def wait_split(pe, e, kind, k):
            n = chunks.index((e, kind, k))
            pe.wait_ge(s["w_lo_ready"], min(n + 1, FIRST))
            if n >= FIRST:
                pe.wait_ge(s["pool_lo_ready"], n - FIRST + 1)

        FIRST = 7

        def load_chunk(eng, n):
            before = n - RAWS
            if before < FIRST:
                eng.wait_ge(s["w_lo_ready"], before + 1)
            else:
                eng.wait_ge(s["pool_lo_ready"], before - FIRST + 1)
            load_raw(eng, a, n, raw, w_in)

        with nc.Block() as block:
            @block.sync
            def _(sp):
                def load_group(g):
                    sp.dma_start(x1[:, :, :], x1_dram.rearrange("(b t) c -> t b c", t=T)[:, one(g, G), :])\
                        .then_inc(s["x1_in"], 16)

                def store_group(g):
                    for t in range(G):
                        sp.wait_ge(s["final"], g * G + (t + 1 + CREDIT["final"]))
                        sp.dma_start(out.rearrange("b t c -> (b t) c")[one(g * G + t, T), :], x3[:, t, :])\
                            .then_inc(s["out_done"], 16)

                sp.dma_start(stats[:, :, :], x1_dram.rearrange("(b t) c -> t b c", t=T)[:, :, C:C + 2])\
                    .then_inc(s["stats_in"], 16)
                sp.sem_inc(s["out_done"], 1)
                load_group(0)
                for e in range(2):
                    sp.dma_start(up_b[:, e, :], a[f"b{e}a"]).then_inc(s["rows_in"], 16)
                with sp.Fori(0, GROUPS - 1) as i:
                    sp.wait_ge(s["result_free"], i * G + G)
                    load_group(i + 1)
                    store_group(i)
                store_group(GROUPS - 1)
                sp.wait_ge(s["out_done"], GROUPS * 16 * G + 1)

            @block.vector
            def _(dve):
                nv = nc.vector
                chain = Chain(dve, s["own_v3"], 24)
                link = chain.link
                for n in ("h_ready", "t_lo_ready", "final"):
                    dve.sem_inc(s[n], CREDIT[n])

                def norm_batch(g, t):
                    if t == 0:
                        link(nv.tensor_copy(rg[:, :], rs[:, one(g, G)]))
                        dve.wait_ge(s["x1_in"], g * 16 + 16)
                    row = x1[:, t, :]
                    nv.tensor_scalar(x2[:, t, :], row[:, 0:C], row[:, C:C + 1], rg[:, t:t + 1],
                                     ALU.subtract, ALU.mult).then_inc(s["x2_ready"], 1)
                    dve.wait_ge(s["x2_ready"], g * G + (t + 1))
                    link(nv.tensor_tensor_reduce(out=junk[:, :], in0=x2[:, t, :], in1=wg[:, :], scale=1.0,
                                                 scalar=0.0, op0=ALU.mult, op1=ALU.add,
                                                 accum_out=score[:, t:t + 1]))
                    nv.tensor_tensor(row[:, 0:C], row[:, 0:C], b1[:, :], ALU.add).then_inc(s["biased"], 1)

                def add_biases(g):
                    link(nv.tensor_scalar(scale[:, 0, :], score[:, :], 0.0, gates[0:T, 1:2], ALU.is_ge, ALU.mult))
                    link(nv.tensor_scalar(scale[:, 1, :], scale[:, 0, :], -1.0, gates[0:T, 1:2],
                                          ALU.mult, ALU.add))
                    dve.wait_ge(s["biased"], g * G + G)
                    for t in range(G):
                        nv.scalar_tensor_tensor(out=x1[:, t, 0:C], in0=b0[:, :], scalar=scale[:, 0, t:t + 1],
                                                in1=x1[:, t, 0:C], op0=ALU.mult, op1=ALU.add)\
                            .then_inc(s["based"], 1)

                def split_weights(n):
                    dve.wait_ge(s["w_hi_ready"], n + 1)
                    nv.tensor_tensor(chunk(chunks[n], 1), raw[n % RAWS][:, :], chunk(chunks[n], 0), ALU.subtract)\
                        .then_inc(s["w_lo_ready"], 1)

                for n in range(RAWS):
                    split_weights(n)
                dve.wait_ge(s["stats_in"], 16)
                nv.tensor_scalar(rs_ve[:, :], stats[:, :, 1], EPS_ROW, None, ALU.add).then_inc(s["rs_var"], 1)
                dve.wait_ge(s["rs_guess"], 1)
                link(nv.tensor_tensor(rs[:, :], rs_y[:, :], rs_y[:, :], ALU.mult))
                link(nv.tensor_tensor(rs[:, :], rs[:, :], rs_ve[:, :], ALU.mult))
                link(nv.tensor_scalar(rs[:, :], rs[:, :], -0.5, 1.5, ALU.mult, ALU.add))
                link(nv.tensor_tensor(rs[:, :], rs[:, :], rs_y[:, :], ALU.mult))

                def low_tokens(g, t):
                    dve.wait_ge(s["t_hi_ready"], g * G + (t + 1))
                    nv.tensor_tensor(t_lo[:, :, t * T:(t + 1) * T],
                                     turn[t % 2][:, 0:KC * T].rearrange("p (k t) -> p k t", k=KC),
                                     t_hi[:, :, t * T:(t + 1) * T], ALU.subtract).then_inc(s["t_lo_ready"], 1)

                def split_hidden(g, q):
                    n = g * NQ + q
                    dve.wait_ge(s["act_ready"], n + (CREDIT["act_ready"] + 1))
                    dve.wait_ge(s["down_ready"], n + 1)
                    link(nv.tensor_copy(h_hi[:, q % SLOTS, :], act_out[q % 2][:, :]))
                    nv.tensor_tensor(h_lo[:, q % SLOTS, :], act_out[q % 2][:, :], h_hi[:, q % SLOTS, :],
                                     ALU.subtract).then_inc(s["h_ready"], 1)

                def gather(g, e):
                    dve.wait_ge(s["down_ready"], g * NQ + ((e + 1) * KF + CREDIT["down_ready"]))
                    if e == 0:
                        dve.wait_ge(s["based"], g * G + G)
                        dve.wait_ge(s["out_done"], g * (16 * G) + 1)
                    else:
                        dve.wait_ge(s["result_free"], g * G + G)
                    for t in range(G):
                        nv.scalar_tensor_tensor(out=x3[:, t, :], in0=result[t][0:T, :],
                                                scalar=scale1[:, t:t + 1] if e else scale[:, 0, t:t + 1],
                                                in1=x3[:, t, :] if e else x1[:, t, 0:C],
                                                op0=ALU.mult, op1=ALU.add)\
                            .then_inc(s["final" if e else "result_free"], 1)
                    if e == 0:
                        link(nv.tensor_copy(scale1[:, :], scale[:, 1, :]))

                def group(g, more):
                    for q in range(NQ):
                        split_hidden(g, q)
                        if q == KF:
                            gather(g, 0)
                        if more and KF + 2 <= q < KF + 2 + G:
                            norm_batch(g + 1, q - KF - 2)
                        if more and q == KF + 2 + G:
                            add_biases(g + 1)
                    if more:
                        for t in range(G):
                            low_tokens(g + 1, t)
                    gather(g, 1)

                for t in range(G):
                    norm_batch(0, t)
                    if t:
                        low_tokens(0, t - 1)
                split_weights(3)
                low_tokens(0, G - 1)
                for n in range(4, FIRST):
                    split_weights(n)
                add_biases(0)
                with dve.Fori(0, GROUPS - 1) as i:
                    chain.enter(i)
                    group(i, True)
                    chain.leave(GROUPS - 1)
                group(GROUPS - 1, False)

            @block.gpsimd
            def _(pool):
                for n in range(FIRST, FIRST + RAWS):
                    load_chunk(pool, n)
                for n in range(FIRST, len(chunks)):
                    hi, lo = (chunk(chunks[n], part) for part in range(2))
                    pool.wait_ge(w_in[n], 16)
                    nc.gpsimd.tensor_copy(hi, raw[n % RAWS][:, :]).then_inc(s["pool_hi_ready"], 1)
                    pool.wait_ge(s["pool_hi_ready"], n - FIRST + 1)
                    nc.gpsimd.tensor_tensor(lo, raw[n % RAWS][:, :], hi, ALU.subtract).then_inc(s["pool_lo_ready"], 1)
                    if n + RAWS < len(chunks):
                        load_chunk(pool, n + RAWS)

            @block.scalar
            def _(act):
                ns = nc.scalar
                act.sem_inc(s["act_ready"], CREDIT["act_ready"])

                def high_tokens(g, batches=range(G)):
                    for t in batches:
                        act.wait_ge(s["turned"], g * G + (t + 1))
                        ns.activation(t_hi[:, :, t * T:(t + 1) * T],
                                      turn[t % 2][:, 0:KC * T].rearrange("p (k t) -> p k t", k=KC),
                                      ACT.Copy).then_inc(s["t_hi_ready"], 1)

                def high_weights(n):
                    act.wait_ge(w_in[n], 16)
                    ns.activation(chunk(chunks[n], 0), raw[n % RAWS][:, :], ACT.Copy).then_inc(s["w_hi_ready"], 1)

                for n in range(RAWS):
                    high_weights(n)
                act.preload_act_table_set("natural_log_exp_and_others")
                act.wait_ge(s["rs_var"], 1)
                ns.activation(rs_ln[:, :], rs_ve[:, :], ACT.Ln).then_inc(s["own_a3"], 1)
                act.wait_ge(s["own_a3"], 1)
                ns.activation(rs_y[:, :], rs_ln[:, :], ACT.Exp, scale=-0.5).then_inc(s["rs_guess"], 1)
                for n in range(RAWS, 2 * RAWS):
                    load_chunk(act, n)
                    if n == RAWS:
                        act.preload_act_table_set("gelu_and_others")
                high_tokens(0, range(2))
                for n in range(RAWS, FIRST):
                    if n == 4:
                        high_tokens(0, range(2, G))
                    high_weights(n)
                    if n > RAWS and n + RAWS - 1 < FIRST:
                        load_chunk(act, n + RAWS - 1)
                act.wait_ge(s["rows_in"], 16 * 2)

                def group(g, more):
                    for q in range(NQ):
                        n = g * NQ + q
                        act.wait_ge(s["hidden_ready"], n + 1)
                        act.wait_ge(s["h_ready"], n + (CREDIT["h_ready"] - 1))
                        ns.activation(act_out[q % 2][:, :], hidden[q % 2][:, 0:N],
                                      ACT.Relu if q >= KF else ACT.Gelu,
                                      bias=up_b[:, q // KF, q % KF:q % KF + 1]).then_inc(s["act_ready"], 1)
                    if more:
                        high_tokens(g + 1)

                with act.Fori(0, GROUPS - 1) as i:
                    group(i, True)
                group(GROUPS - 1, False)

            @block.tensor
            def _(pe):
                nt = nc.tensor
                pe.sem_inc(s["down_ready"], CREDIT["down_ready"])

                def up(g, q):
                    e, f = q // KF, q % KF
                    n = g * NQ + q
                    pe.wait_ge(s["act_ready"], n + (CREDIT["act_ready"] - 1))
                    if f == 0:
                        wait_split(pe, e, "up", 3)
                    parts = [(k, x, y) for k in range(KC) for x, y in ((0, 0), (0, 1), (1, 0))]
                    for m, (k, x, y) in enumerate(parts):
                        last = nt.matmul(hidden[q % 2][:, 0:N], up_w[e][x][:, k, f * P:(f + 1) * P],
                                         (t_hi, t_lo)[y][:, k, :], start=m == 0, stop=m == len(parts) - 1)
                    last.then_inc(s["hidden_ready"], 1)

                def down(g, q):
                    e, f = q // KF, q % KF
                    pe.wait_ge(s["h_ready"], g * NQ + (q + 1 + CREDIT["h_ready"]))
                    if f % 2 == 0:
                        wait_split(pe, e, "down", f // 2)
                    if f == 0:
                        if e:
                            pe.wait_ge(s["result_free"], g * G + G)
                        else:
                            pe.wait_ge(s["final"], g * G + CREDIT["final"])
                    for t in range(G):
                        for x, y in ((0, 0), (0, 1), (1, 0)):
                            last = nt.matmul(result[t][0:T, :], (h_hi, h_lo)[x][:, q % SLOTS, t * T:(t + 1) * T],
                                             down_w[e][y][:, f, :], start=f == 0 and (x, y) == (0, 0),
                                             stop=f == KF - 1 and x == 1)
                    last.then_inc(s["down_ready"], 1)

                def turn_batch(g, t):
                    n = g * G + t
                    pe.wait_ge(s["x2_ready"], n + 1)
                    pe.wait_ge(s["t_lo_ready"], n + (CREDIT["t_lo_ready"] - 1))
                    for k in range(KC):
                        last = nt.transpose(turn[t % 2][:, k * T:(k + 1) * T], x2[:, t, k * P:(k + 1) * P],
                                            identf[0:T, 0:T])
                    last.then_inc(s["turned"], 1)

                def group(g, more):
                    pe.wait_ge(s["t_lo_ready"], g * G + (G + CREDIT["t_lo_ready"]))
                    for q in range(NQ):
                        up(g, q)
                        if more and q == NQ - 1:
                            turn_batch(g + 1, 0)
                            turn_batch(g + 1, 1)
                        if q:
                            down(g, q - 1)
                    if more:
                        turn_batch(g + 1, 2)
                        turn_batch(g + 1, 3)
                    down(g, NQ - 1)

                for t in range(G):
                    turn_batch(0, t)
                with pe.Fori(0, GROUPS - 1) as i:
                    group(i, True)
                group(GROUPS - 1, False)


def kernel(**inputs):
    import numpy as np
    import concourse.bacc as bacc
    from concourse.bass_utils import run_bass_kernel_spmd

    x = {n.replace("L0_xattn_", "").replace("L0_ffn_", ""): np.asarray(v) for n, v in inputs.items()}
    kv = np.concatenate([x["Wk"], x["Wv"]], axis=1).reshape(CK, H, 2, HD)
    kv_b = np.concatenate([x["bk"], x["bv"]]).reshape(H, 2, HD)
    laid = {"x": x["x"], "ctxT": x["ctx_1024"].transpose(0, 2, 1), "g_xattn": x["g_xattn"], "g_ffn": x["g_ffn"],
            "Wq": x["Wq"], "bq": x["bq"], "Wk_heads": kv[:, :, 0].reshape(CK, C), "Wv_heads": kv[:, :, 1].reshape(CK, C),
            "bk_heads": kv_b[:, 0].reshape(C), "bv_heads": kv_b[:, 1].reshape(C), "Wg": x["Wg"]}
    for n in ("Wkv_dca", "bkv_dca", "qn_w", "qn_b", "kn_w", "kn_b", "kn_dca_w", "kn_dca_b", "Wo", "bo",
              "b0b", "b1b"):
        laid[n] = x[n]
    for n in ("b0a", "b1a"):
        laid[n] = x[n].reshape(KF, P).T
    for n in ("W0a", "W0b", "W1a", "W1b"):
        laid[n + "T"] = x[n].T

    nc = bacc.Bacc("TRN2", target_bir_lowering=False, num_devices=1)
    arrays, aps = {}, {}
    for n, v in laid.items():
        arrays[f"in_{n}"] = np.ascontiguousarray(v)
        aps[n] = nc.dram_tensor(f"in_{n}", v.shape, mybir.dt.from_np(v.dtype), kind="ExternalInput").ap()
    out = nc.dram_tensor("out", (B, T, C), F32, kind="ExternalOutput").ap()
    build(nc, aps, out)
    got = run_bass_kernel_spmd(nc, [arrays], core_ids=[0])
    return got.results[0]["out"]
```
